# Optimizing a Trainium2 kernel written in Bass

```python
import numpy as np
import jax
import jax.numpy as jnp

def _softmax(x, axis=-1):
    return jax.nn.softmax(x, axis=axis)

def _gelu(x):
    return jax.nn.gelu(x, approximate=True)

def _silu(x):
    return jax.nn.silu(x)

def _sigmoid(x):
    return jax.nn.sigmoid(x)

def _layernorm(x, axis=-1, eps=1e-05):
    m = jnp.mean(x, axis=axis, keepdims=True)
    v = jnp.var(x, axis=axis, keepdims=True)
    return (x - m) / jnp.sqrt(v + eps)

def _scatter_add(tgt, idx, src, axis=0):
    return tgt.at[idx].add(src)

def _segment_sum(src, seg, n):
    return jax.ops.segment_sum(src, seg, n)
kernel_name = 'mk_adaln_d2_jaxref_r8_57b593'

def setup_inputs(seed: int=0):
    np.random.seed(seed)
    _w = jnp.asarray

    def _L0_attn_setup():
        import jax, jax.numpy as jnp
        import numpy as np
        B, T, HID = (2, 256, 256)
        NKH, NVH = (16, 32)
        DK, DV = (128, 128)
        R = NVH // NKH
        KDIM, VDIM = (NKH * DK, NVH * DV)
        CONV_K = 4
        EPS = 1e-06

        def _silu(x):
            return x * jax.nn.sigmoid(x)

        def _l2norm(x, eps=1e-06):
            return x * jax.lax.rsqrt(jnp.sum(x * x, axis=-1, keepdims=True) + eps)
        key = jax.random.key(seed)
        ks = jax.random.split(key, 8)
        w = lambda k, shape, sc=0.02: jax.random.normal(k, shape, jnp.float32) * sc
        return {'hidden_states': jax.random.normal(ks[0], (B, T, HID), jnp.float32), 'W_qkvz': w(ks[1], (HID, 2 * KDIM + 2 * VDIM)), 'W_ba': w(ks[2], (HID, 2 * NVH)), 'conv_w': w(ks[3], (2 * KDIM + VDIM, CONV_K), 0.1), 'dt_bias': jnp.ones((NVH,), jnp.float32), 'A_log': jax.random.normal(ks[4], (NVH,), jnp.float32), 'norm_weight': jnp.ones((DV,), jnp.float32), 'W_out': w(ks[5], (VDIM, HID))}
    _L0_attn_in = _L0_attn_setup()

    def _L0_ffn_setup():
        import jax, jax.numpy as jnp
        import numpy as np
        DIM = 256
        HID = 704
        ZERO_POINT = 128.0

        def _qlinear(x, wq, scale):
            W = (wq.astype(jnp.float32) - ZERO_POINT) * scale[:, None]
            return jnp.einsum('bsd,hd->bsh', x, W)
        key = jax.random.key(seed)
        ks = jax.random.split(key, 7)
        B, S = (4, 256)
        sg = jax.random.uniform(ks[1], (HID,)) * (0.02 / np.sqrt(DIM)) + 0.0001
        su = jax.random.uniform(ks[3], (HID,)) * (0.02 / np.sqrt(DIM)) + 0.0001
        sd = jax.random.uniform(ks[5], (DIM,)) * (0.02 / np.sqrt(HID)) + 0.0001
        return {'x': jax.random.normal(ks[0], (B, S, DIM), dtype=jnp.float32), 'wq_gate': jax.random.randint(ks[2], (HID, DIM), 0, 32, dtype=jnp.int32), 's_gate': sg, 'wq_up': jax.random.randint(ks[4], (HID, DIM), 0, 32, dtype=jnp.int32), 's_up': su, 'wq_down': jax.random.randint(ks[6], (DIM, HID), 0, 32, dtype=jnp.int32), 's_down': sd}
    _L0_ffn_in = _L0_ffn_setup()
    _L0_c = _w((lambda *s: np.random.randn(*s).astype(np.float32) * 0.05)(4, 256))
    _L0_wmod = _w((lambda *s: np.random.randn(*s).astype(np.float32) * 0.05)(256, 6 * 256) * 256 ** (-0.5))

    def _L1_attn_setup():
        import jax, jax.numpy as jnp
        import numpy as np
        HIDDEN = 256
        NUM_HEADS = 16
        HEAD_DIM = HIDDEN // NUM_HEADS
        key = jax.random.key(seed)
        ks = jax.random.split(key, 5)
        scale = 1.0 / np.sqrt(HIDDEN)
        x = jax.random.normal(ks[0], (2, 256, HIDDEN), dtype=jnp.float32)
        wq = jax.random.normal(ks[1], (HIDDEN, HIDDEN), dtype=jnp.float32) * scale
        wk = jax.random.normal(ks[2], (HIDDEN, HIDDEN), dtype=jnp.float32) * scale
        wv = jax.random.normal(ks[3], (HIDDEN, HIDDEN), dtype=jnp.float32) * scale
        wo = jax.random.normal(ks[4], (HIDDEN, HIDDEN), dtype=jnp.float32) * scale
        return {'x': x, 'wq': wq, 'wk': wk, 'wv': wv, 'wo': wo}
    _L1_attn_in = _L1_attn_setup()

    def _L1_ffn_setup():
        import math
        import jax, jax.numpy as jnp
        import numpy as np
        DIM = 256
        RANK = 8
        B, T = (4, 512)

        def _orthogonal(key, n):
            a = jax.random.normal(key, (n, n), dtype=jnp.float32)
            q, r = jnp.linalg.qr(a)
            q = q * jnp.sign(jnp.diagonal(r))[None, :]
            return q
        key = jax.random.key(seed)
        kx, kf = jax.random.split(key)
        x = jax.random.normal(kx, (B, T, DIM), dtype=jnp.float32)
        fkeys = jax.random.split(kf, RANK)
        factors = jnp.stack([_orthogonal(fkeys[r], DIM) * (r + 1) ** (-0.5) for r in range(RANK)])
        bias = jnp.zeros((DIM,), dtype=jnp.float32)
        return {'x': x, 'factors': factors, 'bias': bias}
    _L1_ffn_in = _L1_ffn_setup()
    _L1_c = _w((lambda *s: np.random.randn(*s).astype(np.float32) * 0.05)(4, 256))
    _L1_wmod = _w((lambda *s: np.random.randn(*s).astype(np.float32) * 0.05)(256, 6 * 256) * 256 ** (-0.5))
    _d = {'L0_attn_hidden_states': _L0_attn_in['hidden_states'], 'L0_attn_W_qkvz': _L0_attn_in['W_qkvz'], 'L0_attn_W_ba': _L0_attn_in['W_ba'], 'L0_attn_conv_w': _L0_attn_in['conv_w'], 'L0_attn_dt_bias': _L0_attn_in['dt_bias'], 'L0_attn_A_log': _L0_attn_in['A_log'], 'L0_attn_norm_weight': _L0_attn_in['norm_weight'], 'L0_attn_W_out': _L0_attn_in['W_out'], 'L0_ffn_wq_gate': _L0_ffn_in['wq_gate'], 'L0_ffn_s_gate': _L0_ffn_in['s_gate'], 'L0_ffn_wq_up': _L0_ffn_in['wq_up'], 'L0_ffn_s_up': _L0_ffn_in['s_up'], 'L0_ffn_wq_down': _L0_ffn_in['wq_down'], 'L0_ffn_s_down': _L0_ffn_in['s_down'], 'L0_c': _L0_c, 'L0_wmod': _L0_wmod, 'L1_attn_wq': _L1_attn_in['wq'], 'L1_attn_wk': _L1_attn_in['wk'], 'L1_attn_wv': _L1_attn_in['wv'], 'L1_attn_wo': _L1_attn_in['wo'], 'L1_ffn_factors': _L1_ffn_in['factors'], 'L1_ffn_bias': _L1_ffn_in['bias'], 'L1_c': _L1_c, 'L1_wmod': _L1_wmod}
    _x0 = _d['L0_attn_hidden_states']
    _d['L0_attn_hidden_states'] = jax.random.normal(jax.random.fold_in(jax.random.key(seed), 1), (4, 256, 256), dtype=_x0.dtype)
    del _x0
    return _d

def reference(L0_attn_hidden_states, L0_attn_W_qkvz, L0_attn_W_ba, L0_attn_conv_w, L0_attn_dt_bias, L0_attn_A_log, L0_attn_norm_weight, L0_attn_W_out, L0_ffn_wq_gate, L0_ffn_s_gate, L0_ffn_wq_up, L0_ffn_s_up, L0_ffn_wq_down, L0_ffn_s_down, L0_c, L0_wmod, L1_attn_wq, L1_attn_wk, L1_attn_wv, L1_attn_wo, L1_ffn_factors, L1_ffn_bias, L1_c, L1_wmod):

    def _L0_attn_ref(hidden_states, W_qkvz, W_ba, conv_w, dt_bias, A_log, norm_weight, W_out):
        import jax, jax.numpy as jnp
        import numpy as np
        B, T, HID = (2, 256, 256)
        NKH, NVH = (16, 32)
        DK, DV = (128, 128)
        R = NVH // NKH
        KDIM, VDIM = (NKH * DK, NVH * DV)
        CONV_K = 4
        EPS = 1e-06

        def _silu(x):
            return x * jax.nn.sigmoid(x)

        def _l2norm(x, eps=1e-06):
            return x * jax.lax.rsqrt(jnp.sum(x * x, axis=-1, keepdims=True) + eps)
        Bv, Tv = hidden_states.shape[:2]
        qkvz = hidden_states @ W_qkvz
        ba = hidden_states @ W_ba
        qkvz = qkvz.reshape(Bv, Tv, NKH, 2 * DK + 2 * R * DV)
        q, k, v, z = jnp.split(qkvz, [DK, 2 * DK, 2 * DK + R * DV], axis=3)
        v = v.reshape(Bv, Tv, NVH, DV)
        z = z.reshape(Bv, Tv, NVH, DV)
        ba = ba.reshape(Bv, Tv, NKH, 2 * R)
        b, a = jnp.split(ba, 2, axis=3)
        b = b.reshape(Bv, Tv, NVH)
        a = a.reshape(Bv, Tv, NVH)
        mixed = jnp.concatenate([q.reshape(Bv, Tv, KDIM), k.reshape(Bv, Tv, KDIM), v.reshape(Bv, Tv, VDIM)], axis=-1)
        xp = jnp.pad(mixed, ((0, 0), (CONV_K - 1, 0), (0, 0)))
        conv = sum((xp[:, j:j + Tv, :] * conv_w[:, j] for j in range(CONV_K)))
        conv = _silu(conv)
        q, k, v = jnp.split(conv, [KDIM, 2 * KDIM], axis=-1)
        q = q.reshape(Bv, Tv, NKH, DK)
        k = k.reshape(Bv, Tv, NKH, DK)
        v = v.reshape(Bv, Tv, NVH, DV)
        beta = jax.nn.sigmoid(b)
        g = -jnp.exp(A_log) * jax.nn.softplus(a + dt_bias)
        alpha = jnp.exp(g)
        q = jnp.repeat(q, R, axis=2)
        k = jnp.repeat(k, R, axis=2)
        q = _l2norm(q) * DK ** (-0.5)
        k = _l2norm(k)

        def step(S, inp):
            q_t, k_t, v_t, a_t, b_t = inp
            S = S * a_t[..., None, None]
            err = jnp.einsum('bhkv,bhk->bhv', S, k_t)
            v_new = (v_t - err) * b_t[..., None]
            S = S + k_t[..., None] * v_new[..., None, :]
            o = jnp.einsum('bhkv,bhk->bhv', S, q_t)
            return (S, o)
        tm = lambda x: jnp.swapaxes(x, 0, 1)
        S0 = jnp.zeros((Bv, NVH, DK, DV), hidden_states.dtype)
        _, o = jax.lax.scan(step, S0, (tm(q), tm(k), tm(v), tm(alpha), tm(beta)))
        o = jnp.swapaxes(o, 0, 1)
        og = o * _silu(z)
        og = og * jax.lax.rsqrt(jnp.mean(og * og, axis=-1, keepdims=True) + EPS) * norm_weight
        return og.reshape(Bv, Tv, VDIM) @ W_out

    def _L0_ffn_ref(x, wq_gate, s_gate, wq_up, s_up, wq_down, s_down):
        import jax, jax.numpy as jnp
        import numpy as np
        DIM = 256
        HID = 704
        ZERO_POINT = 128.0

        def _qlinear(x, wq, scale):
            W = (wq.astype(jnp.float32) - ZERO_POINT) * scale[:, None]
            return jnp.einsum('bsd,hd->bsh', x, W)
        gate = _qlinear(x, wq_gate, s_gate)
        gate = jax.nn.silu(gate)
        up = _qlinear(x, wq_up, s_up)
        return _qlinear(gate * up, wq_down, s_down)

    def _L1_attn_ref(x, wq, wk, wv, wo):
        import jax, jax.numpy as jnp
        import numpy as np
        HIDDEN = 256
        NUM_HEADS = 16
        HEAD_DIM = HIDDEN // NUM_HEADS
        B, S, _ = x.shape
        q = (x @ wq.T).reshape(B, S, NUM_HEADS, HEAD_DIM)
        k = (x @ wk.T).reshape(B, S, NUM_HEADS, HEAD_DIM)
        v = (x @ wv.T).reshape(B, S, NUM_HEADS, HEAD_DIM)
        scores = jnp.einsum('bqhd,bkhd->bhqk', q, k) / np.sqrt(HEAD_DIM).astype(np.float32)
        causal = jnp.tril(jnp.ones((S, S), dtype=bool))
        scores = jnp.where(causal, scores, -jnp.inf)
        att = jax.nn.softmax(scores, axis=-1)
        out = jnp.einsum('bhqk,bkhd->bqhd', att, v).reshape(B, S, HIDDEN)
        return out @ wo.T

    def _L1_ffn_ref(x, factors, bias):
        import math
        import jax, jax.numpy as jnp
        import numpy as np
        DIM = 256
        RANK = 8
        B, T = (4, 512)

        def _orthogonal(key, n):
            a = jax.random.normal(key, (n, n), dtype=jnp.float32)
            q, r = jnp.linalg.qr(a)
            q = q * jnp.sign(jnp.diagonal(r))[None, :]
            return q
        rank = factors.shape[0]
        mixed = jnp.einsum('btd,rde->bte', x, factors)
        mixed = mixed / math.sqrt(rank) + bias
        return mixed
    x = L0_attn_hidden_states
    mod = (_silu(L0_c) @ L0_wmod).reshape(L0_c.shape[0], 6, 1, -1)
    sa, ca, ga, sb, cb, gb = (mod[:, 0], mod[:, 1], mod[:, 2], mod[:, 3], mod[:, 4], mod[:, 5])
    ga = (2 * (ga >= 0) - 1) * jnp.maximum(jnp.abs(ga), 0.25)
    gb = (2 * (gb >= 0) - 1) * jnp.maximum(jnp.abs(gb), 0.25)
    h = _layernorm(x, axis=-1) * (1 + ca) + sa
    x = x + ga * _L0_attn_ref(h, L0_attn_W_qkvz, L0_attn_W_ba, L0_attn_conv_w, L0_attn_dt_bias, L0_attn_A_log, L0_attn_norm_weight, L0_attn_W_out)
    h = _layernorm(x, axis=-1) * (1 + cb) + sb
    x = x + gb * _L0_ffn_ref(h, L0_ffn_wq_gate, L0_ffn_s_gate, L0_ffn_wq_up, L0_ffn_s_up, L0_ffn_wq_down, L0_ffn_s_down)
    mod = (_silu(L1_c) @ L1_wmod).reshape(L1_c.shape[0], 6, 1, -1)
    sa, ca, ga, sb, cb, gb = (mod[:, 0], mod[:, 1], mod[:, 2], mod[:, 3], mod[:, 4], mod[:, 5])
    ga = (2 * (ga >= 0) - 1) * jnp.maximum(jnp.abs(ga), 0.25)
    gb = (2 * (gb >= 0) - 1) * jnp.maximum(jnp.abs(gb), 0.25)
    h = _layernorm(x, axis=-1) * (1 + ca) + sa
    x = x + ga * _L1_attn_ref(h, L1_attn_wq, L1_attn_wk, L1_attn_wv, L1_attn_wo)
    h = _layernorm(x, axis=-1) * (1 + cb) + sb
    x = x + gb * _L1_ffn_ref(h, L1_ffn_factors, L1_ffn_bias)
    return x

_drawn_inputs = setup_inputs


def setup_inputs(seed=0):
    import zlib

    import numpy as np

    out = dict(_drawn_inputs(seed))
    spreads = {'L0_attn_dt_bias': (1.0, 0.6),
     'L0_attn_norm_weight': (1.0, 0.6),
     'L1_ffn_bias': (0.0, 2.0)}
    factors = {'L0_attn_W_qkvz': 7.321,
     'L0_attn_W_ba': 8.0,
     'L0_attn_conv_w': 7.173,
     'L0_attn_A_log': 8.0,
     'L0_attn_W_out': 7.296,
     'L0_ffn_s_gate': 8.0,
     'L0_ffn_s_up': 26.086,
     'L0_ffn_s_down': 8.0,
     'L0_c': 6.902,
     'L0_wmod': 6.865,
     'L1_attn_wq': 8.0,
     'L1_attn_wk': 8.0,
     'L1_attn_wv': 8.0,
     'L1_attn_wo': 8.0,
     'L1_ffn_factors': 64.0,
     'L1_c': 8.0,
     'L1_wmod': 8.0}
    for name, (base, spread) in spreads.items():
        noise = np.random.default_rng([zlib.crc32(name.encode()), seed]).standard_normal(out[name].shape)
        drawn = base * np.exp(spread * noise) if base else spread * noise
        out[name] = jnp.asarray(drawn.astype(out[name].dtype))
    for name, factor in factors.items():
        out[name] = (out[name] * factor).astype(out[name].dtype)
    return out
```

```python
import concourse.bass as bass
from concourse import mybir
from contextlib import ExitStack
import numpy as np


F32 = mybir.dt.float32
BF16 = mybir.dt.bfloat16
I32 = mybir.dt.int32
ALU = mybir.AluOpType
ACT = mybir.ActivationFunctionType
AX = mybir.AxisListType

B, T, D = 4, 256, 256
P = 128
NC = T // P
NT = B * NC
KC = D // P
NKH, R = 16, 2
NVH = NKH * R
DK = 128
CW = 2 * DK + 2 * R * DK
TAPS = 4
BLK = 32
NBLK = P // BLK
SLOTS = NC * NBLK * B * R
HID = 704
HT = (HID + P - 1) // P
HREM = HID - (HT - 1) * P
NH1, HD = 16, 16
QT = NH1 // 4
RANK = 8
MODS = 6


def build(nc, x_d, wqkvz_d, wba_d, convw_d, dtb_d, alog_d, nw_d, wout_d, wg_d, sg_d, wu_d, su_d, wd_d, sd_d,
          c0_d, wmod0_d, wq1_d, wk1_d, wv1_d, wo1_d, fac_d, bias_d, c1_d, wmod1_d, out_d):
    outer = ExitStack()
    sems = {}

    def sem(name):
        if name not in sems:
            sems[name] = outer.enter_context(nc.semaphore(name))
        return sems[name]

    def wait(eng, name, value):
        if isinstance(value, int) and value <= 0:
            return
        eng.wait_ge(sem(name), value)

    class Chain:

        def __init__(self, eng, name):
            self.eng, self.name, self.n = eng, name, 0

        def after(self, ins):
            ins.then_inc(sem(self.name), 1)
            self.n += 1
            self.eng.wait_ge(sem(self.name), self.n)

    with outer:
        def sb(name, shape, dt=F32, ctx=outer):
            return ctx.enter_context(nc.sbuf_tensor(name, shape, dt))

        bank = [outer.enter_context(nc.psum_tensor(f"bank{i}", [P, 512], F32)) for i in range(8)]

        alpha_dr = nc.dram_tensor("alpha_scratch", [NVH, B * T], F32, kind="Internal").ap()
        blkin_dr = nc.dram_tensor("blk_in_scratch", [NC, NBLK, B * R, BLK, BLK], F32, kind="Internal").ap()
        tinv_dr = nc.dram_tensor("tinv_scratch", [NC, NBLK, B * R, BLK, BLK], F32, kind="Internal").ap()
        winv_dr = nc.dram_tensor("winv_scratch", [NC, NBLK, B * R, BLK, BLK], F32, kind="Internal").ap()

        x = sb("x", [P, NT, D])
        xn = sb("xn", [P, NT, D])
        hT = sb("hT", [P, KC, B * T])
        eye = sb("eye", [P, T])
        eyeb = sb("eyeb", [P, P], BF16)
        cmask = sb("cmask", [P, P], BF16)
        modT = sb("modT", [P, 2, MODS * KC, B])
        gates = sb("gates", [P, 2, 2, B, D])
        stats = sb("stats", [P, NT, 6])
        mv = sb("mv", [P, NT, 2])
        rstd = sb("rstd", [P, NT])
        vare = sb("vare", [P, NT])
        mhalf = sb("mhalf", [P, NT])
        ident = eye[:, 0:P]

        def ln_vector(dve, pre, ready):
            for t in range(NT):
                ready(t)
                nc.vector.bn_stats(stats[:, t, :], x[:, t, :]).then_inc(sem(pre + "_stats"), 1)
            for t in range(NT):
                dve.wait_ge(sem(pre + "_stats"), t + 1)
                nc.vector.bn_aggr(mv[:, t, :], stats[:, t, :]).then_inc(sem(pre + "_mv"), 1)
            for t in range(NT):
                if t == 0:
                    dve.wait_ge(sem(pre + "_rstd"), 2)
                nc.vector.tensor_scalar(xn[:, t, :], x[:, t, :], mv[:, t, 0:1], rstd[:, t:t + 1],
                                        ALU.subtract, ALU.mult).then_inc(sem(pre + "_norm"), 1)

        def ln_pool(pool, pre):
            pool.wait_ge(sem(pre + "_mv"), NT)
            nc.gpsimd.tensor_scalar(vare[:], mv[:, :, 1], 1e-5, None, ALU.add).then_inc(sem(pre + "_rstd"), 1)
            pool.wait_ge(sem(pre + "_rstd"), 1)
            nc.gpsimd.tensor_tensor(rstd[:], vare[:], mhalf[:], ALU.pow).then_inc(sem(pre + "_rstd"), 1)

        def ln_tensor(pe, pre):
            for b in range(B):
                pe.wait_ge(sem(pre + "_norm"), NC * (b + 1))
                wait(pe, pre + "_hT", KC * (b - 1))
                for k in range(KC):
                    for c in range(NC):
                        last = nc.tensor.transpose(bank[b % 2][:, k * T + c * P:k * T + (c + 1) * P],
                                                   xn[:, NC * b + c, k * P:(k + 1) * P], ident)
                last.then_inc(sem(pre + "_tr"), 1)

        def ln_scalar(act, pre, layer, shift, scale):
            for b in range(B):
                act.wait_ge(sem(pre + "_tr"), b + 1)
                for k in range(KC):
                    nc.scalar.activation(hT[:, k, b * T:(b + 1) * T], bank[b % 2][:, k * T:(k + 1) * T],
                                         ACT.Identity, bias=modT[:, layer, shift * KC + k, b:b + 1],
                                         scale=modT[:, layer, scale * KC + k, b:b + 1]).then_inc(sem(pre + "_hT"), 1)

        beta = sb("beta", [P, NT, NVH])
        with ExitStack() as s0:
            wmod = [sb(f"wmod{l}", [P, KC, MODS * D], ctx=s0) for l in range(2)]
            cin = sb("cin", [P, 2, KC, B], ctx=s0)
            csil = sb("csil", [P, 2, KC, B], ctx=s0)
            cbc = sb("cbc", [P, 2, KC, B, P], ctx=s0)
            gsign = sb("gsign", [P, 512], ctx=s0)
            gabs = sb("gabs", [P, 512], ctx=s0)
            wba = sb("wba", [P, KC, NKH, 2 * R], ctx=s0)
            wb = sb("wb", [P, KC, NVH], ctx=s0)
            wa = sb("wa", [P, KC, NVH], ctx=s0)
            dtb = sb("dtb", [NVH, 1], ctx=s0)
            alog = sb("alog", [NVH, 1], ctx=s0)
            nega = sb("nega", [NVH, 1], ctx=s0)
            ea = sb("ea", [NVH, 1], ctx=s0)
            ga_ = [sb(f"gate_tmp{i}", [NVH, B * T], ctx=s0) for i in range(6)]
            gx, gab, gu, gw, gl, gd = ga_

            block = s0.enter_context(nc.Block())

            @block.sync
            def _(sp):
                for b in range(B):
                    sp.dma_start(x[:, NC * b:NC * (b + 1), :], x_d[b].rearrange("(c p) d -> p c d", p=P)).then_inc(sem("x_in"), 16)
                for l, (c_d, w_d) in enumerate(((c0_d, wmod0_d), (c1_d, wmod1_d))):
                    for k in range(KC):
                        sp.dma_start(cin[:, l, k, :], c_d[:, k * P:(k + 1) * P].rearrange("b p -> p b"), allow_slow_non_contiguous=True).then_inc(sem("c_in"), 16)
                    sp.dma_start(wmod[l][:], w_d.rearrange("(k p) n -> p k n", p=P)).then_inc(sem(f"wmod_in{l}"), 16)
                    if l == 0:
                        sp.dma_start(wba[:].rearrange("p k h r -> p k (h r)"), wba_d.rearrange("(k p) n -> p k n", p=P)).then_inc(sem("wba_in"), 16)
                        sp.dma_start(dtb[:], dtb_d.rearrange("(h o) -> h o", o=1)).then_inc(sem("wba_in"), 16)
                        sp.dma_start(alog[:], alog_d.rearrange("(h o) -> h o", o=1)).then_inc(sem("wba_in"), 16)
                sp.wait_ge(sem("alpha"), 1)
                sp.dma_start(alpha_dr, gx[:]).then_inc(sem("alpha_out"), 16)
                sp.wait_ge(sem("alpha_out"), 16)

            @block.gpsimd
            def _(pool):
                nc.gpsimd.memset(eye[:], 0.0).then_inc(sem("const"), 1)
                nc.gpsimd.memset(eyeb[:], 0.0).then_inc(sem("const"), 1)
                nc.gpsimd.memset(cmask[:], 0.0).then_inc(sem("const"), 1)
                nc.gpsimd.memset(mhalf[:], -0.5).then_inc(sem("const"), 1)
                pool.wait_ge(sem("const"), 4)
                nc.gpsimd.affine_select(out=eye[:, 0:P], in_=eye[:, 0:P], compare_op=ALU.not_equal, fill=1.0, base=0,
                                        pattern=[[-1, P]], channel_multiplier=1).then_inc(sem("const"), 1)
                nc.gpsimd.affine_select(out=eyeb[:], in_=eyeb[:], compare_op=ALU.not_equal, fill=1.0, base=0,
                                        pattern=[[-1, P]], channel_multiplier=1).then_inc(sem("const"), 1)
                nc.gpsimd.affine_select(out=cmask[:], in_=cmask[:], compare_op=ALU.is_ge, fill=-1e30, base=0,
                                        pattern=[[-1, P]], channel_multiplier=1).then_inc(sem("const"), 1)
                ln_pool(pool, "ln0")

            @block.scalar
            def _(act):
                act.wait_ge(sem("c_in"), 16 * 2 * KC)
                nc.scalar.activation(csil[:], cin[:], ACT.Silu).then_inc(sem("csil"), 1)
                act.wait_ge(sem("modT"), 4)
                ln_scalar(act, "ln0", 0, 0, 1)
                act.wait_ge(sem("b_proj"), 1)
                nc.scalar.activation(beta[:].rearrange("p t h -> p (t h)"), bank[2][:, 0:NT * NVH], ACT.Sigmoid).then_inc(sem("beta"), 1)
                act.wait_ge(sem("gx"), 1)
                nc.scalar.activation(gab[:], gx[:], ACT.Abs).then_inc(sem("g_act"), 1)
                act.wait_ge(sem("g_act"), 1)
                nc.scalar.activation(gu[:], gab[:], ACT.Exp, scale=-1.0).then_inc(sem("g_act"), 1)
                nc.scalar.activation(ea[:], alog[:], ACT.Exp).then_inc(sem("g_act"), 1)
                act.wait_ge(sem("gw"), 1)
                nc.scalar.activation(gl[:], gw[:], ACT.Ln).then_inc(sem("g_act"), 1)
                act.wait_ge(sem("gneg"), 1)
                nc.scalar.activation(gx[:], gu[:], ACT.Exp).then_inc(sem("alpha"), 1)

            @block.vector
            def _(dve):
                dve.wait_ge(sem("wba_in"), 48)
                nc.vector.tensor_copy(wb[:].rearrange("p k (h r) -> p k h r", r=R), wba[:, :, :, 0:R]).then_inc(sem("wba_cut"), 1)
                nc.vector.tensor_copy(wa[:].rearrange("p k (h r) -> p k h r", r=R), wba[:, :, :, R:2 * R]).then_inc(sem("wba_cut"), 1)
                dve.wait_ge(sem("csil"), 1)
                for l in range(2):
                    for k in range(KC):
                        nc.vector.tensor_copy(cbc[:, l, k], csil[:, l, k].unsqueeze(2).broadcast_to([P, B, P])).then_inc(sem("cbc"), 1)
                for l in range(2):
                    dve.wait_ge(sem("mod_mm"), l + 1)
                    nc.vector.tensor_copy(modT[:, l].rearrange("p m b -> p (m b)"), bank[2 + l][:, 0:MODS * KC * B]).then_inc(sem("modT"), 1)
                for l in range(2):
                    dve.wait_ge(sem("modT"), 2)
                for m in (1, 4):
                    v = modT[:, :, m * KC:(m + 1) * KC, :].rearrange("p l k b -> p l (k b)")
                    nc.vector.tensor_scalar(v, v, 1.0, None, ALU.add).then_inc(sem("modT"), 1)
                ln_vector(dve, "ln0", lambda t: dve.wait_ge(sem("x_in"), 16 * B))
                ch = Chain(dve, "gate_chain")
                for l in range(2):
                    for m in range(2):
                        for bb in range(B // 2):
                            n = (l * 2 + m) * 2 + bb
                            dve.wait_ge(sem("gate_mm"), n + 1)
                            src = bank[4 + n % 2][:]
                            ch.after(nc.vector.tensor_scalar(gsign[:], src, -1.0, None, ALU.mult))
                            ch.after(nc.vector.tensor_tensor(gabs[:], src, gsign[:], ALU.max))
                            ch.after(nc.vector.tensor_scalar(gabs[:], gabs[:], 0.25, None, ALU.max))
                            ch.after(nc.vector.tensor_scalar(gsign[:], src, 0.0, 2.0, ALU.is_ge, ALU.mult))
                            nc.vector.scalar_tensor_tensor(
                                gates[:, l, m, 2 * bb:2 * bb + 2, :].rearrange("p b d -> p (b d)"), gsign[:], -1.0, gabs[:],
                                ALU.add, ALU.mult).then_inc(sem("gates"), 1)
                            dve.wait_ge(sem("gates"), n + 1)
                gc = Chain(dve, "g_chain")
                for h in range(2):
                    dve.wait_ge(sem("a_proj"), h + 1)
                    i = nc.vector.tensor_scalar(gx[:, h * 512:(h + 1) * 512], bank[6 + h][0:NVH, :], dtb[:, 0:1], None, ALU.add)
                    if h == 0:
                        gc.after(i)
                i.then_inc(sem("gx"), 1)
                dve.wait_ge(sem("g_act"), 2)
                nc.vector.tensor_scalar(gw[:], gu[:], 1.0, None, ALU.add).then_inc(sem("gw"), 1)
                dve.wait_ge(sem("gw"), 1)
                gc.after(nc.vector.tensor_scalar(gd[:], gw[:], -1.0, 1e-30, ALU.add, ALU.add))
                gc.after(nc.vector.reciprocal(gd[:], gd[:]))
                dve.wait_ge(sem("g_act"), 4)
                gc.after(nc.vector.scalar_tensor_tensor(gl[:], gl[:], 1e-30, gd[:], ALU.add, ALU.mult))
                gc.after(nc.vector.tensor_tensor(gl[:], gl[:], gu[:], ALU.mult))
                gc.after(nc.vector.tensor_scalar(gx[:], gx[:], 0.0, None, ALU.max))
                gc.after(nc.vector.tensor_tensor(gl[:], gl[:], gx[:], ALU.add))
                gc.after(nc.vector.tensor_scalar(nega[:], ea[:], -1.0, None, ALU.mult))
                nc.vector.tensor_scalar(gu[:], gl[:], nega[:, 0:1], None, ALU.mult).then_inc(sem("gneg"), 1)

            @block.tensor
            def _(pe):
                pe.wait_ge(sem("const"), 7)
                for l in range(2):
                    pe.wait_ge(sem(f"wmod_in{l}"), 16)
                    pe.wait_ge(sem("csil"), 1)
                    for m in range(MODS * KC):
                        for k in range(KC):
                            last = nc.tensor.matmul(bank[2 + l][:, m * B:(m + 1) * B], wmod[l][:, k, m * P:(m + 1) * P],
                                                    csil[:, l, k, :], start=(k == 0), stop=(k == KC - 1))
                    last.then_inc(sem("mod_mm"), 1)
                pe.wait_ge(sem("cbc"), 2 * KC)
                for l in range(2):
                    for m, entry in enumerate((2, 5)):
                        for bb in range(B // 2):
                            n = (l * 2 + m) * 2 + bb
                            wait(pe, "gates", n - 1)
                            for b in range(2):
                                for k in range(KC):
                                    last = nc.tensor.matmul(bank[4 + n % 2][:, b * D:(b + 1) * D], cbc[:, l, k, 2 * bb + b, :],
                                                            wmod[l][:, k, entry * D:(entry + 1) * D],
                                                            start=(k == 0), stop=(k == KC - 1))
                            last.then_inc(sem("gate_mm"), 1)
                ln_tensor(pe, "ln0")
                pe.wait_ge(sem("ln0_hT"), KC * B)
                pe.wait_ge(sem("wba_cut"), 2)
                pe.wait_ge(sem("modT"), 4)
                for t in range(NT):
                    for k in range(KC):
                        last = nc.tensor.matmul(bank[2][:, t * NVH:(t + 1) * NVH], hT[:, k, t * P:(t + 1) * P], wb[:, k, :],
                                                start=(k == 0), stop=(k == KC - 1))
                last.then_inc(sem("b_proj"), 1)
                for h in range(2):
                    for k in range(KC):
                        last = nc.tensor.matmul(bank[6 + h][0:NVH, :], wa[:, k, :], hT[:, k, h * 512:(h + 1) * 512],
                                                start=(k == 0), stop=(k == KC - 1))
                    last.then_inc(sem("a_proj"), 1)

        acc = xn
        with ExitStack() as s1:
            wq = [sb(f"wq{p}", [P, KC, CW], ctx=s1) for p in range(2)]
            wo = [sb(f"wo{p}", [P, R, D], ctx=s1) for p in range(2)]
            alb = [sb(f"alb{p}", [P, R, B * T], ctx=s1) for p in range(2)]
            cw = [sb(f"cw{p}", [P, 4, TAPS], ctx=s1) for p in range(2)]
            bet = [sb(f"bet{p}", [P, NT, R], ctx=s1) for p in range(2)]
            nw = sb("nw", [P, 1], ctx=s1)
            negoff = sb("negoff", [P, P], ctx=s1)
            ones = sb("ones", [P, 1], ctx=s1)
            npow = sb("npow", [P, 4], ctx=s1)
            nscale = sb("nscale", [P, 4], ctx=s1)
            cqk = sb("cqk", [P, 2, T], ctx=s1)
            sqk = [sb(f"sqk{i}", [P, 2, T], ctx=s1) for i in range(2)]
            sqq = [sb(f"sqq{i}", [P, 2, T], ctx=s1) for i in range(2)]
            cv = sb("cv", [P, R, T], ctx=s1)
            sv = [sb(f"sv{i}", [P, R, T], ctx=s1) for i in range(2)]
            nrm = [sb(f"nrm{i}", [P, 4], ctx=s1) for i in range(2)]
            rcn = [sb(f"rcn{i}", [P, 2], ctx=s1) for i in range(2)]
            cj = [sb(f"cj{i}", [P, NC, R], ctx=s1) for i in range(2)]
            vsc = [sb(f"vsc{p}", [P, B, 4], ctx=s1) for p in range(2)]
            E1 = sb("E1", [P, R, T], ctx=s1)
            E2 = sb("E2", [P, R, P], ctx=s1)
            BP1 = [sb(f"BP1{p}", [P, B, R, 2, T], ctx=s1) for p in range(2)]
            BP2 = [sb(f"BP2{p}", [P, B, R, 2, P], ctx=s1) for p in range(2)]
            Dm = sb("Dm", [SLOTS, BLK, BLK], ctx=s1)
            Tn = sb("Tn", [SLOTS, BLK, BLK], ctx=s1)
            Wn = sb("Wn", [SLOTS, BLK, BLK], ctx=s1)
            tmp = sb("tmp", [SLOTS, 256], ctx=s1)
            T32 = sb("T32", [P, NC, B * R, P], ctx=s1)
            W32 = sb("W32", [P, NC, B * R, P], ctx=s1)
            zs = sb("zs", [P, B, NC, R * DK], ctx=s1)
            Vs = sb("Vs", [P, B, NC, R, DK], ctx=s1)
            MTs = sb("MTs", [P, NC, R, P], ctx=s1)
            xs = sb("xs", [P, 3, R, DK], ctx=s1)
            R2 = sb("R2", [P, R, DK], ctx=s1)
            Y = sb("Y", [P, NC, R, DK], ctx=s1)
            og = [sb(f"og{i}", [P, NC, R, DK], ctx=s1) for i in range(2)]
            ogn = sb("ogn", [P, NC, R, DK], ctx=s1)
            junk = sb("junk", [P, DK], ctx=s1)
            ss = sb("ss", [P, 4], ctx=s1)
            sse = sb("sse", [P, 4], ctx=s1)
            ro = sb("ro", [P, 4], ctx=s1)
            OTs = sb("OTs", [P, R, NC, P], ctx=s1)

            bQK, bG1, bG2, bV, bZ, bVT, bX, bF = bank
            bMT, bO, bOT = bV, bZ, bVT
            NTS = 3 + 2 * (BLK - 1)

            def at(kh, b, per, k=0):
                return kh * (B * per) + (b * per + k)

            def pe_qk(kh, p, b):
                if b == 0:
                    wait(nc.tensor, "w_in", (kh + 1) * 80)
                wait(nc.tensor, "conv_qk", at(kh, b, 6))
                for t in range(2):
                    for k in range(KC):
                        last = nc.tensor.matmul(bQK[:, t * T:(t + 1) * T], wq[p][:, k, t * DK:(t + 1) * DK],
                                                hT[:, k, b * T:(b + 1) * T], start=(k == 0), stop=(k == KC - 1))
                last.then_inc(sem("qk_mm"), 1)

            def pe_gram(kh, p, b):
                i = b % 2
                wait(nc.tensor, "silu_qk", at(kh, b, 1, 1))
                wait(nc.tensor, "square_qk", at(kh, b, 1, 1))
                wait(nc.tensor, "bp", at(kh, b, 4))
                nc.tensor.matmul(bG1[:], sqk[i][:, 1, 0:P], sqk[i][:].rearrange("p x t -> p (x t)"), start=True, stop=True)
                nc.tensor.matmul(bG2[:, 0:2 * P].rearrange("p (x t) -> p x t", x=2), sqk[i][:, 1, P:T], sqk[i][:, :, P:T],
                                 start=True, stop=True)
                for q in range(2):
                    for c in range(NC):
                        last = nc.tensor.matmul(bG2[:, 256 + 2 * q + c:257 + 2 * q + c], sqq[i][:, q, c * P:(c + 1) * P],
                                                ones[:, 0:1], start=True, stop=True)
                last.then_inc(sem("gram"), 1)

            def pe_v(kh, p, b):
                wait(nc.tensor, "conv_v", at(kh, b, 6))
                wait(nc.tensor, "mt_evac", at(kh, 0, 1))
                for t in range(R):
                    for k in range(KC):
                        last = nc.tensor.matmul(bV[:, t * T:(t + 1) * T], wq[p][:, k, (2 + t) * DK:(3 + t) * DK],
                                                hT[:, k, b * T:(b + 1) * T], start=(k == 0), stop=(k == KC - 1))
                last.then_inc(sem("v_mm"), 1)

            def pe_z(kh, p, b):
                wait(nc.tensor, "silu_z", at(kh, b, 1))
                wait(nc.tensor, "og", at(kh, 0, 2))
                for c in range(NC):
                    for k in range(KC):
                        last = nc.tensor.matmul(bZ[:, c * 256:(c + 1) * 256], hT[:, k, b * T + c * P:b * T + (c + 1) * P],
                                                wq[p][:, k, 4 * DK:6 * DK], start=(k == 0), stop=(k == KC - 1))
                last.then_inc(sem("z_mm"), 1)

            def pe_vt(kh, p, b):
                wait(nc.tensor, "silu_v", at(kh, b, 1, 1))
                wait(nc.tensor, "vs", at(kh, b, 2))
                wait(nc.tensor, "ots", at(kh, 0, 1))
                for c in range(NC):
                    for h in range(R):
                        n = c * R + h
                        last = nc.tensor.transpose(bVT[:, n * P:(n + 1) * P], sv[b % 2][:, h, c * P:(c + 1) * P], ident)
                last.then_inc(sem("vt"), 1)

            def pe_mt(kh, p, b):
                if b == 0:
                    wait(nc.tensor, "t_in", (kh + 1) * 16 * 2 * NC * NBLK)
                    wait(nc.tensor, "conv_v", at(kh, B - 1, 6, 6))
                wait(nc.tensor, "mt_evac", at(kh, b, 1))
                for c, bp in ((0, BP1[p][:, b, :, :, 0:P]), (1, BP2[p][:, b])):
                    for h in range(R):
                        last = nc.tensor.matmul(bMT[:, (c * R + h) * P:(c * R + h + 1) * P], T32[:, c, b * R + h, :],
                                                bp[:, h, 1, :], start=True, stop=True)
                last.then_inc(sem("mt"), 1)

            def pe_half(kh, b, n):
                if n == 0:
                    wait(nc.tensor, "y", at(kh, b, 2))
                return bX[:, (n + b) % 2 * 256:(n + b) % 2 * 256 + 256]

            def reader(kh, b, n):
                if n in (3, 8):
                    return "y", at(kh, b, 2, 1 if n == 3 else 2)
                return "x_add", at(kh, b, 7, n + 1 if n < 3 else n)

            def pe_product(kh, p, b, n):
                half = pe_half(kh, b, n)
                c = 0 if n < 4 else 1
                if n == 0:
                    wait(nc.tensor, "mt_evac", at(kh, b, 1, 1))
                    wait(nc.tensor, "vs", at(kh, b, 2, 2))
                else:
                    wait(nc.tensor, *reader(kh, b, n - 1))
                for h in range(R):
                    if n in (3, 8):
                        lhs, rhs = W32[:, c, b * R + h, :], xs[:, 2, h, :]
                    elif n == 4:
                        lhs, rhs = BP1[p][:, b, h, 1, P:T], Y[:, 0, h, :]
                    else:
                        r = n if c == 0 else n - 5
                        lhs = MTs[:, c, h, :]
                        rhs = xs[:, r - 1, h, :] if r else (Vs[:, b, 0, h, :] if c == 0 else R2[:, h, :])
                    last = nc.tensor.matmul(half[:, h * P:(h + 1) * P], lhs, rhs, start=True, stop=True)
                last.then_inc(sem("x_mm"), 1)

            def pe_o(kh, p, b, c):
                if c == 0:
                    wait(nc.tensor, "y", at(kh, b, 2, 1))
                    wait(nc.tensor, "og", at(kh, b, 2))
                    wait(nc.tensor, "silu_z", at(kh, B - 1, 1, 1))
                else:
                    wait(nc.tensor, "y", at(kh, b, 2, 2))
                for h in range(R):
                    o = bO[:, (c * R + h) * P:(c * R + h + 1) * P]
                    last = nc.tensor.matmul(o, BP1[p][:, b, h, 0, c * P:(c + 1) * P], Y[:, 0, h, :], start=True, stop=(c == 0))
                    if c == 1:
                        last = nc.tensor.matmul(o, BP2[p][:, b, h, 0, :], Y[:, 1, h, :], start=False, stop=True)
                last.then_inc(sem("o"), 1)

            def pe_ot(kh, p, b):
                wait(nc.tensor, "ogn", at(kh, b, 4, 4))
                wait(nc.tensor, "ots", at(kh, b, 1))
                wait(nc.tensor, "vs", at(kh, B - 1, 2, 2))
                for h in range(R):
                    for c in range(NC):
                        n = h * NC + c
                        last = nc.tensor.transpose(bOT[:, n * P:(n + 1) * P], ogn[:, c, h, :], ident)
                last.then_inc(sem("ot"), 1)

            def pe_f(kh, p, b):
                wait(nc.tensor, "ots", at(kh, b, 1, 1))
                wait(nc.tensor, "acc", at(kh, b, 1))
                if b == 0:
                    wait(nc.tensor, "wo_scaled", kh + 1)
                for c in range(NC):
                    for h in range(R):
                        last = nc.tensor.matmul(bF[:, c * D:(c + 1) * D], OTs[:, h, c, :], wo[p][:, h, :],
                                                start=(h == 0), stop=(h == R - 1))
                last.then_inc(sem("f"), 1)

            def pe_body(kh, p, ahead):
                for b in range(B):
                    pe_v(kh, p, b)
                    pe_z(kh, p, b)
                    if b:
                        pe_vt(kh, p, b - 1)
                pe_vt(kh, p, B - 1)
                for b in range(B):
                    pe_mt(kh, p, b)
                    if ahead:
                        pe_qk(kh + 1, 1 - p, b)
                    pe_product(kh, p, b, 0)
                    pe_product(kh, p, b, 1)
                    pe_product(kh, p, b, 2)
                    pe_product(kh, p, b, 3)
                    if b:
                        pe_ot(kh, p, b - 1)
                    pe_product(kh, p, b, 4)
                    pe_o(kh, p, b, 0)
                    pe_product(kh, p, b, 5)
                    if b:
                        pe_f(kh, p, b - 1)
                    pe_product(kh, p, b, 6)
                    if ahead:
                        pe_gram(kh + 1, 1 - p, b)
                    pe_product(kh, p, b, 7)
                    pe_product(kh, p, b, 8)
                    pe_o(kh, p, b, 1)
                pe_ot(kh, p, B - 1)
                pe_f(kh, p, B - 1)

            def act_tap0(kh, p, b, name, bk, dst, first):
                wait(nc.scalar, name + "_mm", at(kh, b, 1, 1))
                wait(nc.scalar, "silu_" + name, at(kh, b, 1))
                for t in range(2):
                    nc.scalar.activation(dst[:, t, :], bk[:, t * T:(t + 1) * T], ACT.Copy,
                                         scale=cw[p][:, first + t, TAPS - 1:TAPS]).then_inc(sem("tap0_" + name), 1)

            def act_silu_qk(kh, p, b):
                wait(nc.scalar, "conv_qk", at(kh, b, 6, 6))
                wait(nc.scalar, "gram", at(kh, b, 1, -1))
                wait(nc.scalar, "square_qk", at(kh, b, 1))
                nc.scalar.activation(sqk[b % 2][:], cqk[:], ACT.Silu).then_inc(sem("silu_qk"), 1)
                wait(nc.scalar, "silu_qk", at(kh, b, 1, 1))
                nc.scalar.activation(sqq[b % 2][:], sqk[b % 2][:], ACT.Square).then_inc(sem("square_qk"), 1)

            def act_silu_z(kh, p, b):
                wait(nc.scalar, "z_mm", at(kh, b, 1, 1))
                nc.scalar.activation(zs[:, b].rearrange("p c n -> p (c n)"), bZ[:], ACT.Silu).then_inc(sem("silu_z"), 1)

            def act_silu_v(kh, p, b):
                wait(nc.scalar, "conv_v", at(kh, b, 6, 6))
                wait(nc.scalar, "vt", at(kh, b, 1, -1))
                nc.scalar.activation(sv[b % 2][:], cv[:], ACT.Silu).then_inc(sem("silu_v"), 1)

            def act_vs(kh, p, b):
                wait(nc.scalar, "vt", at(kh, b, 1, 1))
                wait(nc.scalar, "vsc", at(kh, b, 1, 1))
                for c in range(NC):
                    nc.scalar.activation(Vs[:, b, c], bVT[:, c * 256:(c + 1) * 256].rearrange("p (h d) -> p h d", h=R), ACT.Copy,
                                         scale=vsc[p][:, b, 2 + c:3 + c]).then_inc(sem("vs"), 1)

            def act_y(kh, p, b, c):
                n = 3 if c == 0 else 8
                wait(nc.scalar, "x_mm", at(kh, b, 9, n + 1))
                if c == 0:
                    wait(nc.scalar, "o", at(kh, b, 2))
                nc.scalar.activation(Y[:, c], bX[:, (n + b) % 2 * 256:(n + b) % 2 * 256 + 256].rearrange("p (h d) -> p h d", h=R),
                                     ACT.Copy).then_inc(sem("y"), 1)

            def act_ss(kh, p, b):
                wait(nc.scalar, "ro", at(kh, b, 2, -1))
                for c in range(NC):
                    wait(nc.scalar, "og", at(kh, b, 2, c + 1))
                    for h in range(R):
                        n = c * R + h
                        wait(nc.scalar, "ss", at(kh, b, 4, n))
                        nc.scalar.activation(junk[:], og[b % 2][:, c, h, :], ACT.Square, accum_out=ss[:, n:n + 1]).then_inc(sem("ss"), 1)

            def act_ogn(kh, p, b):
                wait(nc.scalar, "ro", at(kh, b, 2, 2))
                wait(nc.scalar, "ot", at(kh, b, 1))
                for c in range(NC):
                    for h in range(R):
                        n = c * R + h
                        nc.scalar.activation(ogn[:, c, h, :], og[b % 2][:, c, h, :], ACT.Copy, scale=ro[:, n:n + 1]).then_inc(sem("ogn"), 1)

            def act_ots(kh, p, b):
                wait(nc.scalar, "ot", at(kh, b, 1, 1))
                wait(nc.scalar, "f", at(kh, b, 1))
                nc.scalar.activation(OTs[:].rearrange("p h c t -> p (h c t)"), bOT[:], ACT.Copy).then_inc(sem("ots"), 1)

            def act_body(kh, p, ahead):
                for b in range(B):
                    act_tap0(kh, p, b, "v", bV, cv, 2)
                    act_silu_z(kh, p, b)
                    if b:
                        act_vs(kh, p, b - 1)
                    act_silu_v(kh, p, b)
                act_vs(kh, p, B - 1)
                for b in range(B):
                    if ahead:
                        act_tap0(kh + 1, 1 - p, b, "qk", bQK, cqk, 0)
                    if b:
                        act_ss(kh, p, b - 1)
                        act_ogn(kh, p, b - 1)
                    act_y(kh, p, b, 0)
                    if b:
                        act_ots(kh, p, b - 1)
                    if ahead:
                        act_silu_qk(kh + 1, 1 - p, b)
                    act_y(kh, p, b, 1)
                act_ss(kh, p, B - 1)
                act_ogn(kh, p, B - 1)
                act_ots(kh, p, B - 1)

            def dve_tap(kh, p, b, name, bk, dst, first, s):
                for t in range(2):
                    if s == 1:
                        wait(nc.vector, "tap0_" + name, at(kh, b, 2, 2))
                    else:
                        wait(nc.vector, "conv_" + name, at(kh, b, 6, 2 * (s - 2) + t + 1))
                    nc.vector.scalar_tensor_tensor(dst[:, t, s:T], bk[:, t * T:(t + 1) * T - s],
                                                   cw[p][:, first + t, TAPS - 1 - s:TAPS - s], dst[:, t, s:T],
                                                   ALU.mult, ALU.add).then_inc(sem("conv_" + name), 1)

            def dve_scan(kh, p, b, n):
                if b == 0 and n == 0:
                    wait(nc.vector, "w_in", (kh + 1) * 80)
                h = n % R
                wait(nc.vector, "bp", at(kh, b, 4))
                if n < R:
                    nc.vector.tensor_tensor_scan(E1[:, h, :], alb[p][:, h, b * T:(b + 1) * T], eye[:], 0.0,
                                                 ALU.mult, ALU.add).then_inc(sem("scan"), 1)
                else:
                    nc.vector.tensor_tensor_scan(E2[:, h, :], alb[p][:, h, b * T + P:(b + 1) * T], ident, 0.0,
                                                 ALU.mult, ALU.add).then_inc(sem("scan"), 1)

            def dve_bet(kh, p):
                src = beta[:, :, kh * R:kh * R + R] if isinstance(kh, int) else beta[:, :, bass.ds(kh * R, R)]
                nc.vector.tensor_copy(bet[p][:], src).then_inc(sem("bet"), 1)
                wait(nc.vector, "w_in", (kh + 1) * 80)
                nc.vector.tensor_scalar(wo[p][:], wo[p][:], nw[:, 0:1], None, ALU.mult).then_inc(sem("wo_scaled"), 1)

            def dve_bp(kh, p, b):
                i = b % 2
                wait(nc.vector, "gram", at(kh, b, 1, 1))
                wait(nc.vector, "vsc", at(kh, b, 1, -1))
                nc.vector.scalar_tensor_tensor(nrm[i][:], bG2[:, 256:260], 1e-6, nscale[:], ALU.add, ALU.mult).then_inc(sem("nrm"), 1)
                wait(nc.vector, "nrm", at(kh, b, 1, 1))
                nc.vector.reciprocal(rcn[i][:], nrm[i][:, 2:4]).then_inc(sem("rcn"), 1)
                wait(nc.vector, "rcn", at(kh, b, 1, 1))
                wait(nc.vector, "bet", kh + 1)
                nc.vector.tensor_tensor(cj[i][:], bet[p][:, NC * b:NC * (b + 1), :], rcn[i][:].unsqueeze(2).broadcast_to([P, NC, R]),
                                        ALU.mult).then_inc(sem("cj"), 1)
                wait(nc.vector, "cj", at(kh, b, 1, 1))
                wait(nc.vector, "scan", at(kh, b, 4, 4))
                for h in range(R):
                    nc.vector.scalar_tensor_tensor(BP1[p][:, b, h], bG1[:].rearrange("p (x t) -> p x t", x=2), cj[i][:, 0, h:h + 1],
                                                   E1[:, h, :].unsqueeze(1).broadcast_to([P, 2, T]), ALU.mult, ALU.mult).then_inc(sem("bp"), 1)
                    nc.vector.scalar_tensor_tensor(BP2[p][:, b, h], bG2[:, 0:2 * P].rearrange("p (x t) -> p x t", x=2), cj[i][:, 1, h:h + 1],
                                                   E2[:, h, :].unsqueeze(1).broadcast_to([P, 2, P]), ALU.mult, ALU.mult).then_inc(sem("bp"), 1)

            def dve_mt(kh, p, b):
                wait(nc.vector, "mt", at(kh, b, 1, 1))
                nc.vector.tensor_tensor(MTs[:].rearrange("p c h t -> p (c h) t"), bMT[:].rearrange("p (n t) -> p n t", t=P),
                                        negoff[:].unsqueeze(1).broadcast_to([P, NC * R, P]), ALU.mult).then_inc(sem("mt_evac"), 1)

            def dve_x(kh, p, b, n):
                wait(nc.vector, "x_mm", at(kh, b, 9, n + 1))
                half = bX[:, (n + b) % 2 * 256:(n + b) % 2 * 256 + 256].rearrange("p (h d) -> p h d", h=R)
                if n == 4:
                    wait(nc.vector, "x_add", at(kh, b, 7, 3))
                    nc.vector.tensor_tensor(R2[:], Vs[:, b, 1], half, ALU.subtract).then_inc(sem("x_add"), 1)
                else:
                    rhs = Vs[:, b, 0] if n < 4 else R2[:]
                    if n == 5:
                        wait(nc.vector, "x_add", at(kh, b, 7, 4))
                    nc.vector.tensor_tensor(xs[:, n if n < 4 else n - 5], rhs, half, ALU.add).then_inc(sem("x_add"), 1)

            def dve_og(kh, p, b):
                for c in range(NC):
                    wait(nc.vector, "o", at(kh, b, 2, 2))
                    wait(nc.vector, "silu_z", at(kh, b, 1, 1))
                    if c == 0:
                        wait(nc.vector, "ogn", at(kh, b, 4, -4))
                    nc.vector.scalar_tensor_tensor(og[b % 2][:, c].rearrange("p h d -> p (h d)"), bO[:, c * 256:(c + 1) * 256],
                                                   vsc[p][:, b, c:c + 1], zs[:, b, c, :], ALU.mult, ALU.mult).then_inc(sem("og"), 1)

            def dve_acc(kh, p, b):
                wait(nc.vector, "f", at(kh, b, 1, 1))
                a = acc[:, NC * b:NC * (b + 1), :].rearrange("p c d -> p (c d)")
                wait(nc.vector, "acc", at(kh, b, 1, 1 - B))
                nc.vector.tensor_tensor(a, a, bF[:], ALU.add).then_inc(sem("acc"), 1)

            def dve_body(kh, p, ahead):
                for b in range(B):
                    for s in range(1, TAPS):
                        dve_tap(kh, p, b, "v", bV, cv, 2, s)
                k2, p2 = kh + 1, 1 - p
                if ahead:
                    dve_bet(k2, p2)
                for b in range(B):
                    dve_mt(kh, p, b)
                    dve_x(kh, p, b, 0)
                    if ahead:
                        dve_scan(k2, p2, b, 0)
                    dve_x(kh, p, b, 1)
                    if ahead:
                        dve_tap(k2, p2, b, "qk", bQK, cqk, 0, 1)
                    dve_x(kh, p, b, 2)
                    if ahead:
                        dve_tap(k2, p2, b, "qk", bQK, cqk, 0, 2)
                        dve_tap(k2, p2, b, "qk", bQK, cqk, 0, 3)
                    dve_x(kh, p, b, 4)
                    if ahead:
                        dve_scan(k2, p2, b, 1)
                    dve_x(kh, p, b, 5)
                    if ahead:
                        dve_scan(k2, p2, b, 2)
                    dve_x(kh, p, b, 6)
                    if ahead:
                        dve_scan(k2, p2, b, 3)
                    if b:
                        dve_acc(kh, p, b - 1)
                    dve_x(kh, p, b, 7)
                    if ahead:
                        dve_bp(k2, p2, b)
                    dve_og(kh, p, b)
                dve_acc(kh, p, B - 1)

            def pool_vsc(kh, p, b):
                wait(nc.gpsimd, "nrm", at(kh, b, 1, 1))
                if b == 0:
                    wait(nc.gpsimd, "og", at(kh - 2, B - 1, 2, 2))
                nc.gpsimd.tensor_tensor(vsc[p][:, b, :], nrm[b % 2][:], npow[:], ALU.pow).then_inc(sem("vsc"), 1)

            def pool_ro(kh, p, b):
                wait(nc.gpsimd, "ss", at(kh, b, 4, 4))
                wait(nc.gpsimd, "ro", at(kh, b, 2))
                nc.gpsimd.tensor_scalar(sse[:], ss[:], 1.0 / DK, 1e-6, ALU.mult, ALU.add).then_inc(sem("ro"), 1)
                wait(nc.gpsimd, "ro", at(kh, b, 2, 1))
                wait(nc.gpsimd, "ogn", at(kh, b, 4))
                nc.gpsimd.tensor_tensor(ro[:], sse[:], mhalf[:, 0:4], ALU.pow).then_inc(sem("ro"), 1)

            def pool_inverse(kh):
                n = 0

                def step(ins):
                    nonlocal n
                    ins.then_inc(sem("t_step"), 1)
                    n += 1
                    wait(nc.gpsimd, "t_step", kh * NTS + n)

                wait(nc.gpsimd, "blk_in", (kh + 1) * 16)
                wait(nc.gpsimd, "t_out", kh * 32)
                step(nc.gpsimd.memset(Tn[:], 0.0))
                step(nc.gpsimd.affine_select(out=Tn[:], in_=Tn[:], compare_op=ALU.not_equal, fill=1.0, base=0,
                                             pattern=[[1, BLK], [-1, BLK]], channel_multiplier=0))
                for j in range(BLK - 1):
                    r, c = BLK - 1 - j, j + 1
                    t = tmp[:, 0:r * c].rearrange("p (i c) -> p i c", c=c)
                    step(nc.gpsimd.tensor_tensor(t, Dm[:, j, j + 1:BLK].unsqueeze(2).broadcast_to([SLOTS, r, c]),
                                                 Tn[:, j, 0:c].unsqueeze(1).broadcast_to([SLOTS, r, c]), ALU.mult))
                    step(nc.gpsimd.tensor_tensor(Tn[:, j + 1:BLK, 0:c], Tn[:, j + 1:BLK, 0:c], t, ALU.subtract))
                step(nc.gpsimd.tensor_copy(Wn[:], Tn[:].rearrange("p i c -> p c i")))

            def pool_body(kh, p, ahead):
                for b in range(B):
                    if b:
                        pool_ro(kh, p, b - 1)
                    if ahead:
                        pool_vsc(kh + 1, 1 - p, b)
                pool_ro(kh, p, B - 1)
                if ahead:
                    pool_inverse(kh + 1)

            def sp_load(kh, p):
                def one(a, n):
                    return slice(a, a + n)

                wait(nc.sync, "z_mm", at(kh - 1, 0, 1))
                wait(nc.sync, "f", at(kh - 1, 0, 1))
                wait(nc.sync, "conv_v", at(kh - 1, 0, 6))
                wait(nc.sync, "scan", at(kh - 1, 0, 4))
                nc.sync.dma_start(wq[p][:], wqkvz_d[:, one(kh * CW, CW)].rearrange("(k p) n -> p k n", p=P)).then_inc(sem("w_in"), 16)
                nc.sync.dma_start(alb[p][:].rearrange("p r t -> p (r t)"),
                                  alpha_dr[one(kh * R, R), :].rearrange("(o r) t -> o (r t)", o=1).broadcast_to([P, R * B * T])).then_inc(sem("w_in"), 16)
                cwr = convw_d.rearrange("(g p) s -> p g s", p=P)
                nc.sync.dma_start(cw[p][:, 0:2, :], convw_d[0:2 * NKH * P].rearrange("(x g p) s -> p x g s", x=2, p=P)[:, :, one(kh, 1), :]
                                  .rearrange("p x g s -> p (x g) s")).then_inc(sem("w_in"), 16)
                nc.sync.dma_start(cw[p][:, 2:4, :], cwr[:, one(kh * R + 2 * NKH, R), :]).then_inc(sem("w_in"), 16)
                nc.sync.dma_start(wo[p][:], wout_d[one(kh * R * DK, R * DK), :].rearrange("(h p) n -> p h n", p=DK)).then_inc(sem("w_in"), 16)

            def sp_blocks_in(kh, p):
                wait(nc.sync, "bp", at(kh, B - 1, 4, 4))
                for n in range(NBLK):
                    r = slice(n * BLK, (n + 1) * BLK)
                    for c, src in ((0, BP1[p]), (1, BP2[p])):
                        nc.sync.dma_start(blkin_dr[c, n].rearrange("u j i -> j u i"),
                                          src[r, :, :, 1, r].rearrange("j b h i -> j (b h) i")).then_inc(sem("blk_dr"), 16)
                wait(nc.sync, "blk_dr", (kh + 1) * 16 * NC * NBLK)
                wait(nc.sync, "t_step", kh * NTS)
                nc.sync.dma_start(Dm[:].rearrange("s j i -> s (j i)"), blkin_dr.rearrange("c n u j i -> (c n u) (j i)")).then_inc(sem("blk_in"), 16)

            def sp_blocks_out(kh):
                wait(nc.sync, "t_step", (kh + 1) * NTS)
                wait(nc.sync, "t_in", kh * 32 * NC * NBLK)
                nc.sync.dma_start(tinv_dr.rearrange("c n u j i -> (c n u) (j i)"), Tn[:].rearrange("s j i -> s (j i)")).then_inc(sem("t_out"), 16)
                nc.sync.dma_start(winv_dr.rearrange("c n u j i -> (c n u) (j i)"), Wn[:].rearrange("s j i -> s (j i)")).then_inc(sem("t_out"), 16)
                wait(nc.sync, "t_out", (kh + 1) * 32)
                wait(nc.sync, "o", at(kh, 0, 2))
                for n in range(NBLK):
                    r = slice(n * BLK, (n + 1) * BLK)
                    for c in range(NC):
                        nc.sync.dma_start(T32[r, c, :, r], tinv_dr[c, n].rearrange("u j i -> j u i")).then_inc(sem("t_in"), 16)
                        nc.sync.dma_start(W32[r, c, :, r], winv_dr[c, n].rearrange("u j i -> j u i")).then_inc(sem("t_in"), 16)

            block = s1.enter_context(nc.Block())

            @block.sync
            def _(sp):
                sp.dma_start(nw[:], nw_d.rearrange("(p o) -> p o", o=1)).then_inc(sem("nw_in"), 16)
                sp_load(0, 0)
                sp.wait_ge(sem("zero"), 2)
                sp_blocks_in(0, 0)
                sp_load(1, 1)
                sp_blocks_out(0)
                for kh in range(1, NKH):
                    sp_blocks_in(kh, kh % 2)
                    if kh + 1 < NKH:
                        sp_load(kh + 1, (kh + 1) % 2)
                    sp_blocks_out(kh)

            @block.tensor
            def _(pe):
                pe.wait_ge(sem("const1"), 1)
                for b in range(B):
                    pe_qk(0, 0, b)
                    pe_gram(0, 0, b)
                pe_body(0, 0, True)
                with pe.Fori(1, NKH - 2, 2) as kh:
                    pe_body(kh, 1, True)
                    pe_body(kh + 1, 0, True)
                pe_body(NKH - 1, 1, False)

            @block.scalar
            def _(act):
                act.wait_ge(sem("w_in"), 80)
                for b in range(B):
                    act_tap0(0, 0, b, "qk", bQK, cqk, 0)
                    act_silu_qk(0, 0, b)
                act_body(0, 0, True)
                with act.Fori(1, NKH - 2, 2) as kh:
                    act_body(kh, 1, True)
                    act_body(kh + 1, 0, True)
                act_body(NKH - 1, 1, False)

            @block.vector
            def _(dve):
                nc.vector.memset(T32[:].rearrange("p c u t -> p (c u t)"), 0.0).then_inc(sem("zero"), 1)
                nc.vector.memset(W32[:].rearrange("p c u t -> p (c u t)"), 0.0).then_inc(sem("zero"), 1)
                for b in range(B):
                    nc.vector.memset(acc[:, NC * b:NC * (b + 1), :].rearrange("p c d -> p (c d)"), 0.0).then_inc(sem("acc0"), 1)
                dve.wait_ge(sem("acc0"), B)
                dve.wait_ge(sem("const1"), 1)
                dve.wait_ge(sem("nw_in"), 16)
                dve_bet(0, 0)
                for b in range(B):
                    for n in range(4):
                        dve_scan(0, 0, b, n)
                    for s in range(1, TAPS):
                        dve_tap(0, 0, b, "qk", bQK, cqk, 0, s)
                    dve_bp(0, 0, b)
                dve_body(0, 0, True)
                with dve.Fori(1, NKH - 2, 2) as kh:
                    dve_body(kh, 1, True)
                    dve_body(kh + 1, 0, True)
                dve_body(NKH - 1, 1, False)

            @block.gpsimd
            def _(pool):
                n = 0
                for t, v in ((negoff[:], -1.0), (ones[:], 1.0), (npow[:, 0:2], -0.5), (npow[:, 2:4], 0.5),
                             (nscale[:, 0:2], float(DK)), (nscale[:, 2:4], 1.0)):
                    nc.gpsimd.memset(t, v).then_inc(sem("const1a"), 1)
                    n += 1
                pool.wait_ge(sem("const1a"), n)
                for m in range(NBLK):
                    r = slice(m * BLK, (m + 1) * BLK)
                    nc.gpsimd.memset(negoff[r, r], 0.0).then_inc(sem("const1a"), 1)
                    n += 1
                pool.wait_ge(sem("const1a"), n)
                nc.gpsimd.memset(tmp[:], 0.0).then_inc(sem("const1"), 1)
                pool.wait_ge(sem("const1"), 1)
                for b in range(B):
                    pool_vsc(0, 0, b)
                pool_inverse(0)
                pool_body(0, 0, True)
                for kh in range(1, NKH):
                    pool_body(kh, kh % 2, kh < NKH - 1)

        def residual(ch, t_out, b, branch, layer, m, mark):
            g = gates[:, layer, m, b, :].unsqueeze(1).broadcast_to([P, NC, D])
            wait(nc.vector, mark, b)
            ch.after(nc.vector.tensor_tensor(t_out, branch, g, ALU.mult))
            xv = x[:, NC * b:NC * (b + 1), :]
            nc.vector.tensor_tensor(xv, xv, t_out, ALU.add).then_inc(sem(mark), 1)

        with ExitStack() as s2:
            wraw = [sb(f"wraw{i}", [P, HT, D], I32, ctx=s2) for i in range(2)]
            draw = sb("draw", [P, KC, HID], I32, ctx=s2)
            wsc = sb("wsc", [P, 3, HT], ctx=s2)
            wnat = [sb(f"wnat{i}", [P, HT, D], ctx=s2) for i in range(2)]
            dnat = sb("dnat", [P, KC, HID], ctx=s2)
            wT = [sb(f"wT{i}", [P, KC, HT * P], ctx=s2) for i in range(2)]
            dT = sb("dT", [P, HT, D], ctx=s2)
            gsil = sb("gsil", [P, 2, 512], ctx=s2)
            hact = sb("hact", [P, HT, B * T], ctx=s2)
            rt = sb("rt2", [P, NC, D], ctx=s2)
            block = s2.enter_context(nc.Block())

            def rows(m):
                return P if m < HT - 1 else HREM

            @block.sync
            def _(sp):
                for i, (w_d, s_d) in enumerate(((wg_d, sg_d), (wu_d, su_d))):
                    sp.dma_start(wraw[i][:, 0:HT - 1, :], w_d[0:(HT - 1) * P, :].rearrange("(m p) d -> p m d", p=P)).then_inc(sem("ffn_w_in"), 16)
                    sp.dma_start(wraw[i][0:HREM, HT - 1, :], w_d[(HT - 1) * P:HID, :]).then_inc(sem("ffn_w_in"), 16)
                    sp.dma_start(wsc[:, i, 0:HT - 1], s_d[0:(HT - 1) * P].rearrange("(m p) -> p m", p=P), allow_slow_non_contiguous=True).then_inc(sem("ffn_w_in"), 16)
                    sp.dma_start(wsc[0:HREM, i, HT - 1:HT], s_d[(HT - 1) * P:HID].rearrange("(p o) -> p o", o=1)).then_inc(sem("ffn_w_in"), 16)
                sp.dma_start(draw[:], wd_d.rearrange("(m p) d -> p m d", p=P)).then_inc(sem("ffn_w_in"), 16)
                sp.dma_start(wsc[:, 2, 0:KC], sd_d.rearrange("(m p) -> p m", p=P), allow_slow_non_contiguous=True).then_inc(sem("ffn_w_in"), 16)

            @block.gpsimd
            def _(pool):
                ln_pool(pool, "ln1")

            @block.vector
            def _(dve):
                ch = Chain(dve, "ffn_chain")
                for b in range(B):
                    residual(ch, rt[:], b, acc[:, NC * b:NC * (b + 1), :], 0, 0, "res0a")
                ln_vector(dve, "ln1", lambda t: dve.wait_ge(sem("res0a"), t // NC + 1))
                dve.wait_ge(sem("ffn_w_in"), 160)
                for i in range(2):
                    for m in range(HT):
                        r = rows(m)
                        nc.vector.tensor_scalar(wnat[i][0:r, m, :], wraw[i][0:r, m, :], -128.0, wsc[0:r, i, m:m + 1],
                                                ALU.add, ALU.mult).then_inc(sem("deq"), 1)
                for m in range(KC):
                    nc.vector.tensor_scalar(dnat[:, m, :], draw[:, m, :], -128.0, wsc[:, 2, m:m + 1],
                                            ALU.add, ALU.mult).then_inc(sem("deq"), 1)
                for n in range(2 * HT):
                    th, m = divmod(n, HT)
                    r = rows(m)
                    dve.wait_ge(sem("up_mm"), n + 1)
                    dve.wait_ge(sem("gsil"), n + 1)
                    nc.vector.tensor_tensor(hact[0:r, m, th * 512:(th + 1) * 512], gsil[0:r, n % 2, :], bank[4 + n % 2][0:r, :],
                                            ALU.mult).then_inc(sem("hact"), 1)
                for b in range(B):
                    dve.wait_ge(sem("down_mm"), b + 1)
                    residual(ch, rt[:], b, bank[6 + b % 2][:].rearrange("p (c d) -> p c d", c=NC), 0, 1, "res0b")

            @block.scalar
            def _(act):
                ln_scalar(act, "ln1", 0, 3, 4)
                for n in range(3 * HT):
                    i, m = divmod(n, HT)
                    r = rows(m)
                    act.wait_ge(sem("wtr"), n + 1)
                    bk = bank[2 + n % 2]
                    if i < 2:
                        nc.scalar.activation(wT[i][:, :, m * P:m * P + r], bk[:, 0:2 * P].rearrange("p (k r) -> p k r", k=2)[:, :, 0:r],
                                             ACT.Copy).then_inc(sem("wT"), 1)
                    else:
                        nc.scalar.activation(dT[0:r, m, :], bk[0:r, 0:D], ACT.Copy).then_inc(sem("wT"), 1)
                for n in range(2 * HT):
                    th, m = divmod(n, HT)
                    r = rows(m)
                    act.wait_ge(sem("gate_mm2"), n + 1)
                    wait(act, "hact", n - 1)
                    nc.scalar.activation(gsil[0:r, n % 2, :], bank[2 + n % 2][0:r, :], ACT.Silu).then_inc(sem("gsil"), 1)

            @block.tensor
            def _(pe):
                ln_tensor(pe, "ln1")
                for n in range(3 * HT):
                    i, m = divmod(n, HT)
                    r = rows(m)
                    pe.wait_ge(sem("deq"), 2 * HT + KC if i == 2 else n + 1)
                    wait(pe, "wT", n - 1)
                    bk = bank[2 + n % 2]
                    for k in range(KC):
                        if i < 2:
                            last = nc.tensor.transpose(bk[:, k * P:k * P + r], wnat[i][0:r, m, k * P:(k + 1) * P], ident[0:r, 0:r])
                        else:
                            last = nc.tensor.transpose(bk[0:r, k * P:(k + 1) * P], dnat[:, k, m * P:m * P + r], ident)
                    last.then_inc(sem("wtr"), 1)
                pe.wait_ge(sem("ln1_hT"), KC * B)
                pe.wait_ge(sem("wT"), 3 * HT)
                for n in range(2 * HT):
                    th, m = divmod(n, HT)
                    r = rows(m)
                    wait(pe, "gsil", n - 1)
                    for k in range(KC):
                        last = nc.tensor.matmul(bank[2 + n % 2][0:r, :], wT[0][:, k, m * P:m * P + r], hT[:, k, th * 512:(th + 1) * 512],
                                                start=(k == 0), stop=(k == KC - 1))
                    last.then_inc(sem("gate_mm2"), 1)
                    wait(pe, "hact", n - 1)
                    for k in range(KC):
                        last = nc.tensor.matmul(bank[4 + n % 2][0:r, :], wT[1][:, k, m * P:m * P + r], hT[:, k, th * 512:(th + 1) * 512],
                                                start=(k == 0), stop=(k == KC - 1))
                    last.then_inc(sem("up_mm"), 1)
                for b in range(B):
                    pe.wait_ge(sem("hact"), HT * (b // 2 + 1))
                    wait(pe, "res0b", b - 1)
                    for c in range(NC):
                        t = NC * b + c
                        for m in range(HT):
                            r = rows(m)
                            last = nc.tensor.matmul(bank[6 + b % 2][:, c * D:(c + 1) * D], hact[0:r, m, t * P:(t + 1) * P], dT[0:r, m, :],
                                                    start=(m == 0), stop=(m == HT - 1))
                    last.then_inc(sem("down_mm"), 1)

        with ExitStack() as s3:
            wn1 = sb("wn1", [P, 4, KC, D], ctx=s3)
            wpad = sb("wpad", [P, 2, KC, NH1, 32], ctx=s3)
            wvo = sb("wvo", [P, 2, KC, D], ctx=s3)
            qkT = sb("qkT", [P, 2, QT, B * T], ctx=s3)
            v1 = sb("v1", [P, NT, D], ctx=s3)
            NBUF = 4
            prob = sb("prob", [P, NBUF, 384], ctx=s3)
            probT = sb("probT", [P, NBUF, 384], ctx=s3)
            mx = sb("mx", [P, B, NH1, NC], ctx=s3)
            nmx = sb("nmx", [P, B, NH1, NC], ctx=s3)
            sums = sb("sums", [P, B, NC, NH1], ctx=s3)
            rsum = sb("rsum", [P, B, NC, NH1], ctx=s3)
            at1 = sb("at1", [P, NC, D], ctx=s3)
            atT = sb("atT", [P, KC, NC, P], ctx=s3)
            rt = sb("rt3", [P, NC, D], ctx=s3)
            block = s3.enter_context(nc.Block())
            NBH = B * NH1
            HS = float(HD) ** -0.5

            @block.sync
            def _(sp):
                for i, w_d in enumerate((wq1_d, wk1_d, wv1_d, wo1_d)):
                    sp.dma_start(wn1[:, i], w_d.rearrange("(m p) d -> p m d", p=P)).then_inc(sem("w1_in"), 16)

            @block.gpsimd
            def _(pool):
                nc.gpsimd.memset(wpad[:].rearrange("p a k h e -> p (a k h e)"), 0.0).then_inc(sem("wpad0"), 1)
                ln_pool(pool, "ln2")

            @block.vector
            def _(dve):
                ln_vector(dve, "ln2", lambda t: None)
                for n in range(2 * QT * 2):
                    i, rest = divmod(n, QT * 2)
                    q, th = divmod(rest, 2)
                    dve.wait_ge(sem("qk1_mm"), n + 1)
                    nc.vector.tensor_copy(qkT[:, i, q, th * 512:(th + 1) * 512], bank[2 + n % 2][:]).then_inc(sem("qk1"), 1)
                ch = Chain(dve, "att_chain")
                for n in range(NBH + 2):
                    if n < NBH:
                        b, h = divmod(n, NH1)
                        dve.wait_ge(sem("s_mm"), n + 1)
                        s = bank[n % 3]
                        nc.vector.reduce_max(mx[:, b, h, 0:1], s[:, 0:P], AX.X).then_inc(sem("mx"), 1)
                        nc.vector.reduce_max(mx[:, b, h, 1:2], s[:, P:3 * P], AX.X).then_inc(sem("mx"), 1)
                        dve.wait_ge(sem("mx"), 2 * (n + 1))
                        nc.vector.tensor_scalar(nmx[:, b, h, :], mx[:, b, h, :], -HS, None, ALU.mult).then_inc(sem("nmx"), 1)
                    if n >= 2:
                        m = n - 2
                        b, h = divmod(m, NH1)
                        dve.wait_ge(sem("pt_mm"), m + 1)
                        wait(dve, "pv", m - NBUF + 1)
                        nc.vector.tensor_copy(probT[:, m % NBUF, :], bank[3 + m % 2][:, 0:384]).then_inc(sem("pt"), 1)
                    if n >= 4 and (n - 4) % NH1 == NH1 - 1 or n == NBH + 1:
                        b = (n - 4) // NH1 if n < NBH + 1 else B - 1
                        dve.wait_ge(sem("expo"), 2 * NH1 * (b + 1))
                        ch.after(nc.vector.reciprocal(rsum[:, b], sums[:, b]))
                        dve.wait_ge(sem("pv"), NH1 * (b + 1))
                        wait(dve, "at_tr", b)
                        nc.vector.tensor_tensor(at1[:].rearrange("p c (h e) -> p (c h) e", e=HD),
                                                bank[5][:].rearrange("p (n e) -> p n e", e=HD),
                                                rsum[:, b].rearrange("p c h -> p (c h)").unsqueeze(2).broadcast_to([P, NC * NH1, HD]),
                                                ALU.mult).then_inc(sem("at1"), 1)
                        if b:
                            dve.wait_ge(sem("o1_mm"), b)
                            residual(ch, rt[:], b - 1, bank[7][:].rearrange("p (c d) -> p c d", c=NC), 1, 0, "res1a")
                dve.wait_ge(sem("o1_mm"), B)
                residual(ch, rt[:], B - 1, bank[7][:].rearrange("p (c d) -> p c d", c=NC), 1, 0, "res1a")

            @block.scalar
            def _(act):
                ln_scalar(act, "ln2", 1, 0, 1)
                act.wait_ge(sem("wpad0"), 1)
                for n in range(8):
                    i, k = divmod(n, 2)
                    act.wait_ge(sem("w1tr"), n + 1)
                    src = bank[2 + n % 2][:, 0:D]
                    if i < 2:
                        nc.scalar.activation(wpad[:, i, k, :, 0:HD], src.rearrange("p (h e) -> p h e", e=HD), ACT.Copy).then_inc(sem("w1T"), 1)
                    else:
                        nc.scalar.activation(wvo[:, i - 2, k, :], src, ACT.Copy).then_inc(sem("w1T"), 1)
                for b in range(B):
                    act.wait_ge(sem("v1_mm"), b + 1)
                    nc.scalar.activation(v1[:, NC * b:NC * (b + 1), :].rearrange("p c d -> p (c d)"), bank[4 + b % 2][:], ACT.Copy).then_inc(sem("v1"), 1)
                for n in range(NBH + 5):
                    if n < NBH:
                        b, h = divmod(n, NH1)
                        act.wait_ge(sem("nmx"), n + 1)
                        wait(act, "pt_mm", n - NBUF + 1)
                        s = bank[n % 3]
                        for c in range(NC):
                            lo, hi = (0, P) if c == 0 else (P, 3 * P)
                            nc.scalar.activation(prob[:, n % NBUF, lo:hi], s[:, lo:hi], ACT.Exp, bias=nmx[:, b, h, c:c + 1],
                                                 scale=HS, accum_out=sums[:, b, c, h:h + 1]).then_inc(sem("expo"), 1)
                    if n >= 5 and (n - 5) % NH1 == NH1 - 1:
                        b = (n - 5) // NH1
                        act.wait_ge(sem("at_tr"), b + 1)
                        wait(act, "o1_mm", b)
                        nc.scalar.activation(atT[:].rearrange("p k c t -> p (k c t)"), bank[6][:], ACT.Copy).then_inc(sem("atT"), 1)

            @block.tensor
            def _(pe):
                ln_tensor(pe, "ln2")
                pe.wait_ge(sem("w1_in"), 64)
                for n in range(8):
                    i, k = divmod(n, 2)
                    wait(pe, "w1T", n - 1)
                    for m in range(KC):
                        last = nc.tensor.transpose(bank[2 + n % 2][:, m * P:(m + 1) * P], wn1[:, i, m, k * P:(k + 1) * P], ident)
                    last.then_inc(sem("w1tr"), 1)
                pe.wait_ge(sem("w1T"), 8)
                pe.wait_ge(sem("ln2_hT"), KC * B)
                for n in range(2 * QT * 2):
                    i, rest = divmod(n, QT * 2)
                    q, th = divmod(rest, 2)
                    wait(pe, "qk1", n - 1)
                    for k in range(KC):
                        last = nc.tensor.matmul(bank[2 + n % 2][:], wpad[:, i, k, 4 * q:4 * q + 4, :].rearrange("p h e -> p (h e)"),
                                                hT[:, k, th * 512:(th + 1) * 512], start=(k == 0), stop=(k == KC - 1))
                    last.then_inc(sem("qk1_mm"), 1)
                for b in range(B):
                    wait(pe, "v1", b - 1)
                    for c in range(NC):
                        t = NC * b + c
                        for k in range(KC):
                            last = nc.tensor.matmul(bank[4 + b % 2][:, c * D:(c + 1) * D], hT[:, k, t * P:(t + 1) * P], wvo[:, 0, k, :],
                                                    start=(k == 0), stop=(k == KC - 1))
                    last.then_inc(sem("v1_mm"), 1)
                pe.wait_ge(sem("qk1"), 2 * QT * 2)
                pe.wait_ge(sem("v1"), B)
                for n in range(NBH + 5):
                    if n < NBH:
                        b, h = divmod(n, NH1)
                        wait(pe, "expo", 2 * (n - 2))
                        s = bank[n % 3]
                        pr = slice(32 * (h % 4), 32 * (h % 4) + 32)
                        for c in range(NC):
                            lo, w = (0, P) if c == 0 else (P, 2 * P)
                            nc.tensor.matmul(s[:, lo:lo + w], qkT[pr, 0, h // 4, b * T + c * P:b * T + (c + 1) * P],
                                             qkT[pr, 1, h // 4, b * T:b * T + w], start=True, stop=False)
                            last = nc.tensor.matmul(s[:, lo + w - P:lo + w], eyeb[:], cmask[:], start=False, stop=True)
                        last.then_inc(sem("s_mm"), 1)
                    if 2 <= n < NBH + 2:
                        m = n - 2
                        pe.wait_ge(sem("expo"), 2 * (m + 1))
                        wait(pe, "pt", m - 1)
                        for j in range(3):
                            last = nc.tensor.transpose(bank[3 + m % 2][:, j * P:(j + 1) * P], prob[:, m % NBUF, j * P:(j + 1) * P], ident)
                        last.then_inc(sem("pt_mm"), 1)
                    if 3 <= n < NBH + 3:
                        m = n - 3
                        b, h = divmod(m, NH1)
                        pe.wait_ge(sem("pt"), m + 1)
                        if h == 0:
                            wait(pe, "at1", b)
                        e = slice(h * HD, (h + 1) * HD)
                        o = [bank[5][:, c * D + h * HD:c * D + (h + 1) * HD] for c in range(NC)]
                        nc.tensor.matmul(o[0], probT[:, m % NBUF, 0:P], v1[:, NC * b, e], start=True, stop=True)
                        nc.tensor.matmul(o[1], probT[:, m % NBUF, P:2 * P], v1[:, NC * b, e], start=True, stop=False)
                        nc.tensor.matmul(o[1], probT[:, m % NBUF, 2 * P:3 * P], v1[:, NC * b + 1, e], start=False, stop=True).then_inc(sem("pv"), 1)
                    if n >= 5 and (n - 5) % NH1 == NH1 - 1:
                        b = (n - 5) // NH1
                        pe.wait_ge(sem("at1"), b + 1)
                        wait(pe, "atT", b)
                        for k in range(KC):
                            for c in range(NC):
                                last = nc.tensor.transpose(bank[6][:, (k * NC + c) * P:(k * NC + c + 1) * P], at1[:, c, k * P:(k + 1) * P], ident)
                        last.then_inc(sem("at_tr"), 1)
                        pe.wait_ge(sem("atT"), b + 1)
                        wait(pe, "res1a", b)
                        for c in range(NC):
                            for k in range(KC):
                                last = nc.tensor.matmul(bank[7][:, c * D:(c + 1) * D], atT[:, k, c, :], wvo[:, 1, k, :],
                                                        start=(k == 0), stop=(k == KC - 1))
                        last.then_inc(sem("o1_mm"), 1)

        with ExitStack() as s4:
            fac = sb("fac", [P, RANK, KC, D], ctx=s4)
            fsum = sb("fsum", [P, KC, D], ctx=s4)
            biasb = sb("biasb", [P, D], ctx=s4)
            rt = sb("rt4", [P, NC, D], ctx=s4)
            block = s4.enter_context(nc.Block())

            @block.sync
            def _(sp):
                sp.dma_start(fac[:], fac_d.rearrange("r (k p) e -> p r k e", p=P)).then_inc(sem("fac_in"), 16)
                sp.dma_start(biasb[:], bias_d.rearrange("(o e) -> o e", o=1).broadcast_to([P, D])).then_inc(sem("fac_in"), 16)
                for b in range(B):
                    sp.wait_ge(sem("res1b"), b + 1)
                    sp.dma_start(out_d[b].rearrange("(c p) d -> p c d", p=P), x[:, NC * b:NC * (b + 1), :]).then_inc(sem("out"), 16)
                sp.wait_ge(sem("out"), 16 * B)

            @block.gpsimd
            def _(pool):
                ln_pool(pool, "ln3")

            @block.scalar
            def _(act):
                ln_scalar(act, "ln3", 1, 3, 4)

            @block.vector
            def _(dve):
                ln_vector(dve, "ln3", lambda t: None)
                ch = Chain(dve, "fac_chain")
                dve.wait_ge(sem("fac_in"), 32)
                ch.after(nc.vector.tensor_tensor(fsum[:], fac[:, 0], fac[:, 1], ALU.add))
                for r in range(2, RANK):
                    i = nc.vector.tensor_tensor(fsum[:], fsum[:], fac[:, r], ALU.add)
                    if r < RANK - 1:
                        ch.after(i)
                i.then_inc(sem("fsum"), 1)
                for b in range(B):
                    dve.wait_ge(sem("fac_mm"), b + 1)
                    wait(dve, "res1b", b)
                    ch.after(nc.vector.scalar_tensor_tensor(rt[:], bank[2 + b % 2][:].rearrange("p (c d) -> p c d", c=NC), float(RANK) ** -0.5,
                                                            biasb[:].unsqueeze(1).broadcast_to([P, NC, D]), ALU.mult, ALU.add))
                    residual(ch, rt[:], b, rt[:], 1, 1, "res1b")

            @block.tensor
            def _(pe):
                ln_tensor(pe, "ln3")
                pe.wait_ge(sem("ln3_hT"), KC * B)
                pe.wait_ge(sem("fsum"), 1)
                for b in range(B):
                    wait(pe, "res1b", b - 1)
                    for c in range(NC):
                        t = NC * b + c
                        for k in range(KC):
                            last = nc.tensor.matmul(bank[2 + b % 2][:, c * D:(c + 1) * D], hT[:, k, t * P:(t + 1) * P], fsum[:, k, :],
                                                    start=(k == 0), stop=(k == KC - 1))
                    last.then_inc(sem("fac_mm"), 1)


_INS = ['L0_attn_hidden_states', 'L0_attn_W_qkvz', 'L0_attn_W_ba', 'L0_attn_conv_w', 'L0_attn_dt_bias', 'L0_attn_A_log',
        'L0_attn_norm_weight', 'L0_attn_W_out', 'L0_ffn_wq_gate', 'L0_ffn_s_gate', 'L0_ffn_wq_up', 'L0_ffn_s_up',
        'L0_ffn_wq_down', 'L0_ffn_s_down', 'L0_c', 'L0_wmod', 'L1_attn_wq', 'L1_attn_wk', 'L1_attn_wv', 'L1_attn_wo',
        'L1_ffn_factors', 'L1_ffn_bias', 'L1_c', 'L1_wmod']


def kernel(**inputs):
    import concourse.bacc as _bacc
    from concourse.bass_utils import run_bass_kernel_spmd as _run

    nc = _bacc.Bacc("TRN2", target_bir_lowering=False, num_devices=1)
    arrays, args = {}, []
    for name in _INS:
        a = np.ascontiguousarray(inputs[name])
        arrays[f"in_{name}"] = a
        args.append(nc.dram_tensor(f"in_{name}", a.shape, mybir.dt.from_np(a.dtype), kind="ExternalInput").ap())
    args.append(nc.dram_tensor("out_x", (B, T, D), F32, kind="ExternalOutput").ap())
    build(nc, *args)
    r = _run(nc, [arrays], core_ids=[0])
    return r.results[0]["out_x"]
```

```python
import concourse.bass as bass
from concourse import mybir
from contextlib import ExitStack
import numpy as np


F32 = mybir.dt.float32
BF16 = mybir.dt.bfloat16
I32 = mybir.dt.int32
ALU = mybir.AluOpType
ACT = mybir.ActivationFunctionType
AX = mybir.AxisListType

B, T, D = 4, 256, 256
P = 128
NC = T // P
NT = B * NC
KC = D // P
NKH, R = 16, 2
NVH = NKH * R
DK = 128
CW = 2 * DK + 2 * R * DK
TAPS = 4
BLK = 32
NBLK = P // BLK
SLOTS = NC * NBLK * B * R
HID = 704
HT = (HID + P - 1) // P
HREM = HID - (HT - 1) * P
NH1, HD = 16, 16
QT = NH1 // 4
RANK = 8
MODS = 6


def build(nc, x_d, wqkvz_d, wba_d, convw_d, dtb_d, alog_d, nw_d, wout_d, wg_d, sg_d, wu_d, su_d, wd_d, sd_d,
          c0_d, wmod0_d, wq1_d, wk1_d, wv1_d, wo1_d, fac_d, bias_d, c1_d, wmod1_d, out_d):
    outer = ExitStack()
    sems = {}

    def sem(name):
        if name not in sems:
            sems[name] = outer.enter_context(nc.semaphore(name))
        return sems[name]

    def wait(eng, name, value):
        if isinstance(value, int) and value <= 0:
            return
        eng.wait_ge(sem(name), value)

    class Chain:

        def __init__(self, eng, name):
            self.eng, self.name, self.n = eng, name, 0

        def after(self, ins):
            ins.then_inc(sem(self.name), 1)
            self.n += 1
            self.eng.wait_ge(sem(self.name), self.n)

    with outer:
        def sb(name, shape, dt=F32, ctx=outer):
            return ctx.enter_context(nc.sbuf_tensor(name, shape, dt))

        bank = [outer.enter_context(nc.psum_tensor(f"bank{i}", [P, 512], F32)) for i in range(8)]

        alpha_dr = nc.dram_tensor("alpha_scratch", [NVH, B * T], F32, kind="Internal").ap()
        blkin_dr = nc.dram_tensor("blk_in_scratch", [NC, NBLK, B * R, BLK, BLK], F32, kind="Internal").ap()
        tinv_dr = nc.dram_tensor("tinv_scratch", [NBLK, B, NC, R, BLK, BLK], F32, kind="Internal").ap()

        x = sb("x", [P, NT, D])
        xn = sb("xn", [P, NT, D])
        hT = sb("hT", [P, KC, B * T])
        eye = sb("eye", [P, T])
        eyeb = sb("eyeb", [P, P], BF16)
        cmask = sb("cmask", [P, P], BF16)
        modT = sb("modT", [P, 2, MODS * KC, B])
        gates = sb("gates", [P, 2, 2, B, D])
        stats = sb("stats", [P, NT, 6])
        mv = sb("mv", [P, NT, 2])
        rstd = sb("rstd", [P, NT])
        vare = sb("vare", [P, NT])
        mhalf = sb("mhalf", [P, NT])
        ident = eye[:, 0:P]

        def ln_vector(dve, pre, ready):
            for t in range(NT):
                ready(t)
                nc.vector.bn_stats(stats[:, t, :], x[:, t, :]).then_inc(sem(pre + "_stats"), 1)
            for t in range(NT):
                dve.wait_ge(sem(pre + "_stats"), t + 1)
                nc.vector.bn_aggr(mv[:, t, :], stats[:, t, :]).then_inc(sem(pre + "_mv"), 1)
            for t in range(NT):
                if t == 0:
                    dve.wait_ge(sem(pre + "_rstd"), 2)
                nc.vector.tensor_scalar(xn[:, t, :], x[:, t, :], mv[:, t, 0:1], rstd[:, t:t + 1],
                                        ALU.subtract, ALU.mult).then_inc(sem(pre + "_norm"), 1)

        def ln_pool(pool, pre):
            pool.wait_ge(sem(pre + "_mv"), NT)
            nc.gpsimd.tensor_scalar(vare[:], mv[:, :, 1], 1e-5, None, ALU.add).then_inc(sem(pre + "_rstd"), 1)
            pool.wait_ge(sem(pre + "_rstd"), 1)
            nc.gpsimd.tensor_tensor(rstd[:], vare[:], mhalf[:], ALU.pow).then_inc(sem(pre + "_rstd"), 1)

        def ln_tensor(pe, pre):
            for b in range(B):
                pe.wait_ge(sem(pre + "_norm"), NC * (b + 1))
                wait(pe, pre + "_hT", KC * (b - 1))
                for k in range(KC):
                    for c in range(NC):
                        last = nc.tensor.transpose(bank[b % 2][:, k * T + c * P:k * T + (c + 1) * P],
                                                   xn[:, NC * b + c, k * P:(k + 1) * P], ident)
                last.then_inc(sem(pre + "_tr"), 1)

        def ln_scalar(act, pre, layer, shift, scale):
            for b in range(B):
                act.wait_ge(sem(pre + "_tr"), b + 1)
                for k in range(KC):
                    nc.scalar.activation(hT[:, k, b * T:(b + 1) * T], bank[b % 2][:, k * T:(k + 1) * T],
                                         ACT.Identity, bias=modT[:, layer, shift * KC + k, b:b + 1],
                                         scale=modT[:, layer, scale * KC + k, b:b + 1]).then_inc(sem(pre + "_hT"), 1)

        beta = sb("beta", [P, NT, NVH])
        with ExitStack() as s0:
            wmod = [sb(f"wmod{l}", [P, KC, MODS * D], ctx=s0) for l in range(2)]
            cin = sb("cin", [P, 2, KC, B], ctx=s0)
            csil = sb("csil", [P, 2, KC, B], ctx=s0)
            cbc = sb("cbc", [P, 2, KC, B, P], ctx=s0)
            gsign = sb("gsign", [P, 512], ctx=s0)
            gabs = sb("gabs", [P, 512], ctx=s0)
            wba = sb("wba", [P, KC, NKH, 2 * R], ctx=s0)
            wb = sb("wb", [P, KC, NVH], ctx=s0)
            wa = sb("wa", [P, KC, NVH], ctx=s0)
            dtb = sb("dtb", [NVH, 1], ctx=s0)
            alog = sb("alog", [NVH, 1], ctx=s0)
            nega = sb("nega", [NVH, 1], ctx=s0)
            ea = sb("ea", [NVH, 1], ctx=s0)
            ga_ = [sb(f"gate_tmp{i}", [NVH, B * T], ctx=s0) for i in range(6)]
            gx, gab, gu, gw, gl, gd = ga_

            block = s0.enter_context(nc.Block())

            @block.sync
            def _(sp):
                for b in range(B):
                    sp.dma_start(x[:, NC * b:NC * (b + 1), :], x_d[b].rearrange("(c p) d -> p c d", p=P)).then_inc(sem("x_in"), 16)
                for l, (c_d, w_d) in enumerate(((c0_d, wmod0_d), (c1_d, wmod1_d))):
                    for k in range(KC):
                        sp.dma_start(cin[:, l, k, :], c_d[:, k * P:(k + 1) * P].rearrange("b p -> p b"), allow_slow_non_contiguous=True).then_inc(sem("c_in"), 16)
                    sp.dma_start(wmod[l][:], w_d.rearrange("(k p) n -> p k n", p=P)).then_inc(sem(f"wmod_in{l}"), 16)
                    if l == 0:
                        sp.dma_start(wba[:].rearrange("p k h r -> p k (h r)"), wba_d.rearrange("(k p) n -> p k n", p=P)).then_inc(sem("wba_in"), 16)
                        sp.dma_start(dtb[:], dtb_d.rearrange("(h o) -> h o", o=1)).then_inc(sem("wba_in"), 16)
                        sp.dma_start(alog[:], alog_d.rearrange("(h o) -> h o", o=1)).then_inc(sem("wba_in"), 16)
                sp.wait_ge(sem("alpha"), 1)
                sp.dma_start(alpha_dr, gx[:]).then_inc(sem("alpha_out"), 16)
                sp.wait_ge(sem("alpha_out"), 16)

            @block.gpsimd
            def _(pool):
                nc.gpsimd.memset(eye[:], 0.0).then_inc(sem("const"), 1)
                nc.gpsimd.memset(eyeb[:], 0.0).then_inc(sem("const"), 1)
                nc.gpsimd.memset(cmask[:], 0.0).then_inc(sem("const"), 1)
                nc.gpsimd.memset(mhalf[:], -0.5).then_inc(sem("const"), 1)
                pool.wait_ge(sem("const"), 4)
                nc.gpsimd.affine_select(out=eye[:, 0:P], in_=eye[:, 0:P], compare_op=ALU.not_equal, fill=1.0, base=0,
                                        pattern=[[-1, P]], channel_multiplier=1).then_inc(sem("const"), 1)
                nc.gpsimd.affine_select(out=eyeb[:], in_=eyeb[:], compare_op=ALU.not_equal, fill=1.0, base=0,
                                        pattern=[[-1, P]], channel_multiplier=1).then_inc(sem("const"), 1)
                nc.gpsimd.affine_select(out=cmask[:], in_=cmask[:], compare_op=ALU.is_ge, fill=-1e30, base=0,
                                        pattern=[[-1, P]], channel_multiplier=1).then_inc(sem("const"), 1)
                ln_pool(pool, "ln0")

            @block.scalar
            def _(act):
                act.wait_ge(sem("c_in"), 16 * 2 * KC)
                nc.scalar.activation(csil[:], cin[:], ACT.Silu).then_inc(sem("csil"), 1)
                act.wait_ge(sem("modT"), 4)
                ln_scalar(act, "ln0", 0, 0, 1)
                act.wait_ge(sem("b_proj"), 1)
                nc.scalar.activation(beta[:].rearrange("p t h -> p (t h)"), bank[2][:, 0:NT * NVH], ACT.Sigmoid).then_inc(sem("beta"), 1)
                act.wait_ge(sem("gx"), 1)
                nc.scalar.activation(gab[:], gx[:], ACT.Abs).then_inc(sem("g_act"), 1)
                act.wait_ge(sem("g_act"), 1)
                nc.scalar.activation(gu[:], gab[:], ACT.Exp, scale=-1.0).then_inc(sem("g_act"), 1)
                nc.scalar.activation(ea[:], alog[:], ACT.Exp).then_inc(sem("g_act"), 1)
                act.wait_ge(sem("gw"), 1)
                nc.scalar.activation(gl[:], gw[:], ACT.Ln).then_inc(sem("g_act"), 1)
                act.wait_ge(sem("gneg"), 1)
                nc.scalar.activation(gx[:], gu[:], ACT.Exp).then_inc(sem("alpha"), 1)

            @block.vector
            def _(dve):
                dve.wait_ge(sem("wba_in"), 48)
                nc.vector.tensor_copy(wb[:].rearrange("p k (h r) -> p k h r", r=R), wba[:, :, :, 0:R]).then_inc(sem("wba_cut"), 1)
                nc.vector.tensor_copy(wa[:].rearrange("p k (h r) -> p k h r", r=R), wba[:, :, :, R:2 * R]).then_inc(sem("wba_cut"), 1)
                dve.wait_ge(sem("csil"), 1)
                for l in range(2):
                    for k in range(KC):
                        nc.vector.tensor_copy(cbc[:, l, k], csil[:, l, k].unsqueeze(2).broadcast_to([P, B, P])).then_inc(sem("cbc"), 1)
                for l in range(2):
                    dve.wait_ge(sem("mod_mm"), l + 1)
                    nc.vector.tensor_copy(modT[:, l].rearrange("p m b -> p (m b)"), bank[2 + l][:, 0:MODS * KC * B]).then_inc(sem("modT"), 1)
                for l in range(2):
                    dve.wait_ge(sem("modT"), 2)
                for m in (1, 4):
                    v = modT[:, :, m * KC:(m + 1) * KC, :].rearrange("p l k b -> p l (k b)")
                    nc.vector.tensor_scalar(v, v, 1.0, None, ALU.add).then_inc(sem("modT"), 1)
                ln_vector(dve, "ln0", lambda t: dve.wait_ge(sem("x_in"), 16 * B))
                ch = Chain(dve, "gate_chain")
                for l in range(2):
                    for m in range(2):
                        for bb in range(B // 2):
                            n = (l * 2 + m) * 2 + bb
                            dve.wait_ge(sem("gate_mm"), n + 1)
                            src = bank[4 + n % 2][:]
                            ch.after(nc.vector.tensor_scalar(gsign[:], src, -1.0, None, ALU.mult))
                            ch.after(nc.vector.tensor_tensor(gabs[:], src, gsign[:], ALU.max))
                            ch.after(nc.vector.tensor_scalar(gabs[:], gabs[:], 0.25, None, ALU.max))
                            ch.after(nc.vector.tensor_scalar(gsign[:], src, 0.0, 2.0, ALU.is_ge, ALU.mult))
                            nc.vector.scalar_tensor_tensor(
                                gates[:, l, m, 2 * bb:2 * bb + 2, :].rearrange("p b d -> p (b d)"), gsign[:], -1.0, gabs[:],
                                ALU.add, ALU.mult).then_inc(sem("gates"), 1)
                            dve.wait_ge(sem("gates"), n + 1)
                gc = Chain(dve, "g_chain")
                for h in range(2):
                    dve.wait_ge(sem("a_proj"), h + 1)
                    i = nc.vector.tensor_scalar(gx[:, h * 512:(h + 1) * 512], bank[6 + h][0:NVH, :], dtb[:, 0:1], None, ALU.add)
                    if h == 0:
                        gc.after(i)
                i.then_inc(sem("gx"), 1)
                dve.wait_ge(sem("g_act"), 2)
                nc.vector.tensor_scalar(gw[:], gu[:], 1.0, None, ALU.add).then_inc(sem("gw"), 1)
                dve.wait_ge(sem("gw"), 1)
                gc.after(nc.vector.tensor_scalar(gd[:], gw[:], -1.0, 1e-30, ALU.add, ALU.add))
                gc.after(nc.vector.reciprocal(gd[:], gd[:]))
                dve.wait_ge(sem("g_act"), 4)
                gc.after(nc.vector.scalar_tensor_tensor(gl[:], gl[:], 1e-30, gd[:], ALU.add, ALU.mult))
                gc.after(nc.vector.tensor_tensor(gl[:], gl[:], gu[:], ALU.mult))
                gc.after(nc.vector.tensor_scalar(gx[:], gx[:], 0.0, None, ALU.max))
                gc.after(nc.vector.tensor_tensor(gl[:], gl[:], gx[:], ALU.add))
                gc.after(nc.vector.tensor_scalar(nega[:], ea[:], -1.0, None, ALU.mult))
                nc.vector.tensor_scalar(gu[:], gl[:], nega[:, 0:1], None, ALU.mult).then_inc(sem("gneg"), 1)

            @block.tensor
            def _(pe):
                pe.wait_ge(sem("const"), 7)
                for l in range(2):
                    pe.wait_ge(sem(f"wmod_in{l}"), 16)
                    pe.wait_ge(sem("csil"), 1)
                    for m in range(MODS * KC):
                        for k in range(KC):
                            last = nc.tensor.matmul(bank[2 + l][:, m * B:(m + 1) * B], wmod[l][:, k, m * P:(m + 1) * P],
                                                    csil[:, l, k, :], start=(k == 0), stop=(k == KC - 1))
                    last.then_inc(sem("mod_mm"), 1)
                pe.wait_ge(sem("cbc"), 2 * KC)
                for l in range(2):
                    for m, entry in enumerate((2, 5)):
                        for bb in range(B // 2):
                            n = (l * 2 + m) * 2 + bb
                            wait(pe, "gates", n - 1)
                            for b in range(2):
                                for k in range(KC):
                                    last = nc.tensor.matmul(bank[4 + n % 2][:, b * D:(b + 1) * D], cbc[:, l, k, 2 * bb + b, :],
                                                            wmod[l][:, k, entry * D:(entry + 1) * D],
                                                            start=(k == 0), stop=(k == KC - 1))
                            last.then_inc(sem("gate_mm"), 1)
                ln_tensor(pe, "ln0")
                pe.wait_ge(sem("ln0_hT"), KC * B)
                pe.wait_ge(sem("wba_cut"), 2)
                pe.wait_ge(sem("modT"), 4)
                for t in range(NT):
                    for k in range(KC):
                        last = nc.tensor.matmul(bank[2][:, t * NVH:(t + 1) * NVH], hT[:, k, t * P:(t + 1) * P], wb[:, k, :],
                                                start=(k == 0), stop=(k == KC - 1))
                last.then_inc(sem("b_proj"), 1)
                for h in range(2):
                    for k in range(KC):
                        last = nc.tensor.matmul(bank[6 + h][0:NVH, :], wa[:, k, :], hT[:, k, h * 512:(h + 1) * 512],
                                                start=(k == 0), stop=(k == KC - 1))
                    last.then_inc(sem("a_proj"), 1)

        acc = xn
        with ExitStack() as s1:
            wqk = [sb(f"wqk{p}", [P, KC, 2 * DK], ctx=s1) for p in range(2)]
            wvz = [sb(f"wvz{p}", [P, KC, 2 * R * DK], ctx=s1) for p in range(2)]
            wo = [sb(f"wo{p}", [P, R, D], ctx=s1) for p in range(2)]
            alb = [sb(f"alb{p}", [P, R, B * T], ctx=s1) for p in range(2)]
            cw = [sb(f"cw{p}", [P, 4, TAPS], ctx=s1) for p in range(2)]
            bet = [sb(f"bet{p}", [P, NT, R], ctx=s1) for p in range(2)]
            nw = sb("nw", [P, 1], ctx=s1)
            negoff = sb("negoff", [P, P], ctx=s1)
            ones = sb("ones", [P, 1], ctx=s1)
            npow = sb("npow", [P, 4], ctx=s1)
            nscale = sb("nscale", [P, 4], ctx=s1)
            cqk = sb("cqk", [P, 2, T], ctx=s1)
            sqk = [sb(f"sqk{i}", [P, 2, T], ctx=s1) for i in range(2)]
            sqq = [sb(f"sqq{i}", [P, 2, T], ctx=s1) for i in range(2)]
            cv = sb("cv", [P, R, T], ctx=s1)
            sv = [sb(f"sv{i}", [P, R, T], ctx=s1) for i in range(2)]
            nrm = [sb(f"nrm{i}", [P, 4], ctx=s1) for i in range(2)]
            rcn = [sb(f"rcn{i}", [P, 2], ctx=s1) for i in range(2)]
            cj = [sb(f"cj{i}", [P, NC, R], ctx=s1) for i in range(2)]
            vsc = [sb(f"vsc{p}", [P, B, 4], ctx=s1) for p in range(2)]
            E1 = sb("E1", [P, R, T], ctx=s1)
            E2 = sb("E2", [P, R, P], ctx=s1)
            BP = [sb(f"BP{p}", [P, B, R, 2, T + P], ctx=s1) for p in range(2)]
            Dm = sb("Dm", [SLOTS, BLK, BLK], ctx=s1)
            Tn = sb("Tn", [SLOTS, BLK, BLK], ctx=s1)
            tmp = sb("tmp", [SLOTS, 256], ctx=s1)
            T32 = sb("T32", [P, B, NC * R, P], ctx=s1)
            W32 = sb("W32", [P, NC * R, P], ctx=s1)
            zs = sb("zs", [P, B, NC, R * DK], ctx=s1)
            Vs = sb("Vs", [P, B, NC, R, DK], ctx=s1)
            MTs = sb("MTs", [P, NC, R, P], ctx=s1)
            xs = sb("xs", [P, 3, R, DK], ctx=s1)
            R2 = sb("R2", [P, R, DK], ctx=s1)
            Y = sb("Y", [P, NC, R, DK], ctx=s1)
            og = [sb(f"og{i}", [P, NC, R, DK], ctx=s1) for i in range(2)]
            ogn = sb("ogn", [P, NC, R, DK], ctx=s1)
            junk = sb("junk", [P, DK], ctx=s1)
            ss = sb("ss", [P, 4], ctx=s1)
            sse = sb("sse", [P, 4], ctx=s1)
            ro = sb("ro", [P, 4], ctx=s1)
            OTs = sb("OTs", [P, R, NC, P], ctx=s1)

            bQK, bG2, bV, bZ, bVT, bMT, bX, bO = bank
            bG1, bOT, bF = bQK, bVT, bMT
            NTS = 2 + 2 * (BLK - 1)

            def at(kh, b, per, k=0):
                return kh * (B * per) + (b * per + k)

            LEAD_QK, LEAD_GRAM, LEAD_VZ = 2 * B, 2 * B - 1, 3
            NG = NKH * B

            def shift(kh, b, n):
                dk, bb = divmod(b + n, B)
                return kh + dk, bb

            def exists(kh, b, n):
                return not isinstance(kh, int) or 0 <= B * kh + b + n < NG

            def pe_qk(kh, p, b, t):
                if t == 0:
                    if b == 0:
                        wait(nc.tensor, f"qk_in{p}", (kh - p) * 24 + 48)
                    wait(nc.tensor, "bp", at(kh, b, 4))
                for k in range(KC):
                    last = nc.tensor.matmul(bQK[:, t * T:(t + 1) * T], wqk[p][:, k, t * DK:(t + 1) * DK],
                                            hT[:, k, b * T:(b + 1) * T], start=(k == 0), stop=(k == KC - 1))
                if t == 1:
                    last.then_inc(sem("qk_mm"), 1)

            def pe_gram0(kh, p, b):
                i = b % 2
                wait(nc.tensor, "silu_qk", at(kh, b, 1, 1))
                wait(nc.tensor, "square_qk", at(kh, b, 1, 1))
                wait(nc.tensor, "bp", at(kh, b, 4))
                nc.tensor.matmul(bG1[:], sqk[i][:, 1, 0:P], sqk[i][:].rearrange("p x t -> p (x t)"), start=True, stop=True)

            def pe_gram1(kh, p, b):
                i = b % 2
                nc.tensor.matmul(bG2[:, 0:2 * P].rearrange("p (x t) -> p x t", x=2), sqk[i][:, 1, P:T], sqk[i][:, :, P:T],
                                 start=True, stop=True)
                for q in range(2):
                    for c in range(NC):
                        last = nc.tensor.matmul(bG2[:, 256 + 2 * q + c:257 + 2 * q + c], sqq[i][:, q, c * P:(c + 1) * P],
                                                ones[:, 0:1], start=True, stop=True)
                last.then_inc(sem("gram"), 1)

            def pe_v(kh, p, b, t):
                if t == 0:
                    if b == 0:
                        wait(nc.tensor, f"vz_in{p}", (kh - p) * 16 + 32)
                    wait(nc.tensor, "conv_v", at(kh, b, 6))
                for k in range(KC):
                    last = nc.tensor.matmul(bV[:, t * T:(t + 1) * T], wvz[p][:, k, t * DK:(t + 1) * DK],
                                            hT[:, k, b * T:(b + 1) * T], start=(k == 0), stop=(k == KC - 1))
                if t == 1:
                    last.then_inc(sem("v_mm"), 1)

            def pe_z(kh, p, b, c):
                if c == 0:
                    wait(nc.tensor, "silu_z", at(kh, b, 1))
                for k in range(KC):
                    last = nc.tensor.matmul(bZ[:, c * 256:(c + 1) * 256], hT[:, k, b * T + c * P:b * T + (c + 1) * P],
                                            wvz[p][:, k, R * DK:2 * R * DK], start=(k == 0), stop=(k == KC - 1))
                if c == 1:
                    last.then_inc(sem("z_mm"), 1)

            def pe_vt(kh, p, b):
                wait(nc.tensor, "silu_v", at(kh, b, 1, 1))
                wait(nc.tensor, "vs", at(kh, b, 2))
                wait(nc.tensor, "ots", at(kh, b, 1, -3))
                for c in range(NC):
                    for h in range(R):
                        n = c * R + h
                        last = nc.tensor.transpose(bVT[:, n * P:(n + 1) * P], sv[b % 2][:, h, c * P:(c + 1) * P], ident)
                last.then_inc(sem("vt"), 1)

            def block_of(p, b, h, x, c, i):
                o = i * P if c == 0 else T
                return BP[p][:, b, h, x, o:o + P]

            def pe_mt(kh, p, b):
                wait(nc.tensor, f"t_in{b}", (kh + 1) * 64)
                wait(nc.tensor, "acc", at(kh, b, 1, -1))
                for c in range(NC):
                    for h in range(R):
                        last = nc.tensor.matmul(bMT[:, (c * R + h) * P:(c * R + h + 1) * P], T32[:, b, c * R + h, :],
                                                block_of(p, b, h, 1, c, c), start=True, stop=True)
                last.then_inc(sem("mt"), 1)

            def pe_wt(kh, p, b):
                v = at(kh, b, 2, 6)
                wait(nc.tensor, "vs", min(v, 2 * NG) if isinstance(v, int) else v)
                for n in range(NC * R):
                    last = nc.tensor.transpose(bVT[:, n * P:(n + 1) * P], T32[:, b, n, :], ident)
                last.then_inc(sem("wt"), 1)

            def pe_half(kh, b, n):
                if n == 0:
                    wait(nc.tensor, "y", at(kh, b, 2))
                return bX[:, (n + b) % 2 * 256:(n + b) % 2 * 256 + 256]

            def reader(kh, b, n):
                if n in (3, 8):
                    return "y", at(kh, b, 2, 1 if n == 3 else 2)
                return "x_add", at(kh, b, 7, n + 1 if n < 3 else n)

            def pe_product(kh, p, b, n):
                half = pe_half(kh, b, n)
                c = 0 if n < 4 else 1
                if n == 3:
                    wait(nc.tensor, "w32", at(kh, b, 1, 1))
                if n == 0:
                    wait(nc.tensor, "mt_evac", at(kh, b, 1, 1))
                    wait(nc.tensor, "vs", at(kh, b, 2, 2))
                else:
                    wait(nc.tensor, *reader(kh, b, n - 1))
                for h in range(R):
                    if n in (3, 8):
                        lhs, rhs = W32[:, c * R + h, :], xs[:, 2, h, :]
                    elif n == 4:
                        lhs, rhs = block_of(p, b, h, 1, 0, 1), Y[:, 0, h, :]
                    else:
                        r = n if c == 0 else n - 5
                        lhs = MTs[:, c, h, :]
                        rhs = xs[:, r - 1, h, :] if r else (Vs[:, b, 0, h, :] if c == 0 else R2[:, h, :])
                    last = nc.tensor.matmul(half[:, h * P:(h + 1) * P], lhs, rhs, start=True, stop=True)
                last.then_inc(sem("x_mm"), 1)

            def pe_o(kh, p, b, c):
                if c == 0:
                    wait(nc.tensor, "y", at(kh, b, 2, 1))
                    wait(nc.tensor, "og", at(kh, b, 2))
                else:
                    wait(nc.tensor, "y", at(kh, b, 2, 2))
                for h in range(R):
                    o = bO[:, (c * R + h) * P:(c * R + h + 1) * P]
                    last = nc.tensor.matmul(o, block_of(p, b, h, 0, 0, c), Y[:, 0, h, :], start=True, stop=(c == 0))
                    if c == 1:
                        last = nc.tensor.matmul(o, block_of(p, b, h, 0, 1, 1), Y[:, 1, h, :], start=False, stop=True)
                last.then_inc(sem("o"), 1)

            def pe_ot(kh, p, b):
                wait(nc.tensor, "ogn", at(kh, b, 4, 4))
                v = at(kh, b, 1, 2)
                wait(nc.tensor, "w32", min(v, NG) if isinstance(v, int) else v)
                for h in range(R):
                    for c in range(NC):
                        n = h * NC + c
                        last = nc.tensor.transpose(bOT[:, n * P:(n + 1) * P], ogn[:, c, h, :], ident)
                last.then_inc(sem("ot"), 1)

            def pe_f(kh, p, b, c):
                if c == 0:
                    wait(nc.tensor, "ots", at(kh, b, 1, 1))
                    v = at(kh, b, 1, 2)
                    wait(nc.tensor, "mt_evac", min(v, NG) if isinstance(v, int) else v)
                    if b == 0:
                        wait(nc.tensor, "wo_scaled", kh + 1)
                for h in range(R):
                    last = nc.tensor.matmul(bF[:, c * D:(c + 1) * D], OTs[:, h, c, :], wo[p][:, h, :],
                                            start=(h == 0), stop=(h == R - 1))
                if c == 1:
                    last.then_inc(sem("f"), 1)

            def beside(kh, p, b, n):
                k2, b2 = shift(kh, b, n)
                return (k2, (p + (b + n) // B) % 2, b2) if exists(kh, b, n) else None

            def pe_step(kh, p, b):
                qk, gram, vz, vt, last = (beside(kh, p, b, n) for n in (LEAD_QK, LEAD_GRAM, LEAD_VZ, LEAD_VZ - 1, -1))
                pe_mt(kh, p, b)
                if gram:
                    pe_gram0(*gram)
                    pe_gram1(*gram)
                pe_product(kh, p, b, 0)
                if vt:
                    pe_vt(*vt)
                pe_product(kh, p, b, 1)
                if vz:
                    pe_v(*vz, 0)
                pe_wt(kh, p, b)
                pe_product(kh, p, b, 2)
                if vz:
                    pe_v(*vz, 1)
                pe_product(kh, p, b, 3)
                if qk:
                    pe_qk(*qk, 0)
                pe_product(kh, p, b, 4)
                if qk:
                    pe_qk(*qk, 1)
                pe_o(kh, p, b, 0)
                if last:
                    pe_ot(*last)
                pe_product(kh, p, b, 5)
                if last:
                    pe_f(*last, 0)
                pe_product(kh, p, b, 6)
                if last:
                    pe_f(*last, 1)
                pe_product(kh, p, b, 7)
                if vz:
                    pe_z(*vz, 0)
                pe_product(kh, p, b, 8)
                if vz:
                    pe_z(*vz, 1)
                pe_o(kh, p, b, 1)

            def act_tap0(kh, p, b, name, bk, dst, first):
                wait(nc.scalar, name + "_mm", at(kh, b, 1, 1))
                wait(nc.scalar, "silu_" + name, at(kh, b, 1))
                for t in range(2):
                    nc.scalar.activation(dst[:, t, :], bk[:, t * T:(t + 1) * T], ACT.Copy,
                                         scale=cw[p][:, first + t, TAPS - 1:TAPS]).then_inc(sem("tap0_" + name), 1)

            def act_silu_qk(kh, p, b):
                wait(nc.scalar, "conv_qk", at(kh, b, 6, 6))
                wait(nc.scalar, "gram", at(kh, b, 1, -1))
                wait(nc.scalar, "square_qk", at(kh, b, 1))
                nc.scalar.activation(sqk[b % 2][:], cqk[:], ACT.Silu).then_inc(sem("silu_qk"), 1)
                wait(nc.scalar, "silu_qk", at(kh, b, 1, 1))
                nc.scalar.activation(sqq[b % 2][:], sqk[b % 2][:], ACT.Square).then_inc(sem("square_qk"), 1)

            def act_silu_z(kh, p, b):
                wait(nc.scalar, "z_mm", at(kh, b, 1, 1))
                nc.scalar.activation(zs[:, b].rearrange("p c n -> p (c n)"), bZ[:], ACT.Silu).then_inc(sem("silu_z"), 1)

            def act_silu_v(kh, p, b):
                wait(nc.scalar, "conv_v", at(kh, b, 6, 6))
                wait(nc.scalar, "vt", at(kh, b, 1, -1))
                nc.scalar.activation(sv[b % 2][:], cv[:], ACT.Silu).then_inc(sem("silu_v"), 1)

            def act_vs(kh, p, b):
                wait(nc.scalar, "vt", at(kh, b, 1, 1))
                wait(nc.scalar, "vsc", at(kh, b, 1, 1))
                for c in range(NC):
                    nc.scalar.activation(Vs[:, b, c], bVT[:, c * 256:(c + 1) * 256].rearrange("p (h d) -> p h d", h=R), ACT.Copy,
                                         scale=vsc[p][:, b, 2 + c:3 + c]).then_inc(sem("vs"), 1)

            def act_w32(kh, p, b):
                wait(nc.scalar, "wt", at(kh, b, 1, 1))
                nc.scalar.activation(W32[:].rearrange("p u t -> p (u t)"), bVT[:], ACT.Copy).then_inc(sem("w32"), 1)

            def act_y(kh, p, b, c):
                n = 3 if c == 0 else 8
                wait(nc.scalar, "x_mm", at(kh, b, 9, n + 1))
                if c == 0:
                    wait(nc.scalar, "o", at(kh, b, 2))
                nc.scalar.activation(Y[:, c], bX[:, (n + b) % 2 * 256:(n + b) % 2 * 256 + 256].rearrange("p (h d) -> p h d", h=R),
                                     ACT.Copy).then_inc(sem("y"), 1)

            def act_ss(kh, p, b):
                wait(nc.scalar, "ro", at(kh, b, 2, -1))
                for c in range(NC):
                    wait(nc.scalar, "og", at(kh, b, 2, c + 1))
                    for h in range(R):
                        n = c * R + h
                        wait(nc.scalar, "ss", at(kh, b, 4, n))
                        nc.scalar.activation(junk[:], og[b % 2][:, c, h, :], ACT.Square, accum_out=ss[:, n:n + 1]).then_inc(sem("ss"), 1)

            def act_ogn(kh, p, b):
                wait(nc.scalar, "ro", at(kh, b, 2, 2))
                wait(nc.scalar, "ot", at(kh, b, 1))
                for c in range(NC):
                    for h in range(R):
                        n = c * R + h
                        nc.scalar.activation(ogn[:, c, h, :], og[b % 2][:, c, h, :], ACT.Copy, scale=ro[:, n:n + 1]).then_inc(sem("ogn"), 1)

            def act_ots(kh, p, b):
                wait(nc.scalar, "ot", at(kh, b, 1, 1))
                wait(nc.scalar, "f", at(kh, b, 1))
                nc.scalar.activation(OTs[:].rearrange("p h c t -> p (h c t)"), bOT[:], ACT.Copy).then_inc(sem("ots"), 1)

            def act_step(kh, p, b):
                qk, vz, vt, last = (beside(kh, p, b, n) for n in (LEAD_QK, LEAD_VZ, LEAD_VZ - 1, -1))
                if last:
                    act_ss(*last)
                if vt:
                    act_silu_z(*vt)
                    act_vs(*vt)
                act_w32(kh, p, b)
                if vz:
                    act_tap0(*vz, "v", bV, cv, 2)
                act_y(kh, p, b, 0)
                if last:
                    act_ogn(*last)
                if qk:
                    act_tap0(*qk, "qk", bQK, cqk, 0)
                if last:
                    act_ots(*last)
                if vz:
                    act_silu_v(*vz)
                act_y(kh, p, b, 1)
                if qk:
                    act_silu_qk(*qk)

            def dve_tap(kh, p, b, name, bk, dst, first, s):
                for t in range(2):
                    if s == 1:
                        wait(nc.vector, "tap0_" + name, at(kh, b, 2, 2))
                    else:
                        wait(nc.vector, "conv_" + name, at(kh, b, 6, 2 * (s - 2) + t + 1))
                    nc.vector.scalar_tensor_tensor(dst[:, t, s:T], bk[:, t * T:(t + 1) * T - s],
                                                   cw[p][:, first + t, TAPS - 1 - s:TAPS - s], dst[:, t, s:T],
                                                   ALU.mult, ALU.add).then_inc(sem("conv_" + name), 1)

            def dve_scan(kh, p, b, n):
                if b == 0 and n == 0:
                    wait(nc.vector, f"qk_in{p}", (kh - p) * 24 + 48)
                h = n % R
                wait(nc.vector, "bp", at(kh, b, 4))
                if n < R:
                    nc.vector.tensor_tensor_scan(E1[:, h, :], alb[p][:, h, b * T:(b + 1) * T], eye[:], 0.0,
                                                 ALU.mult, ALU.add).then_inc(sem("scan"), 1)
                else:
                    nc.vector.tensor_tensor_scan(E2[:, h, :], alb[p][:, h, b * T + P:(b + 1) * T], ident, 0.0,
                                                 ALU.mult, ALU.add).then_inc(sem("scan"), 1)

            def dve_bet(kh, p):
                src = beta[:, :, kh * R:kh * R + R] if isinstance(kh, int) else beta[:, :, bass.ds(kh * R, R)]
                nc.vector.tensor_copy(bet[p][:], src).then_inc(sem("bet"), 1)

            def dve_wo(kh, p):
                wait(nc.vector, "wo_in", (kh + 1) * 16)
                nc.vector.tensor_scalar(wo[p][:], wo[p][:], nw[:, 0:1], None, ALU.mult).then_inc(sem("wo_scaled"), 1)

            def dve_scales(kh, p, b):
                i = b % 2
                wait(nc.vector, "gram", at(kh, b, 1, 1))
                wait(nc.vector, "vsc", at(kh, b, 1, -1))
                nc.vector.scalar_tensor_tensor(nrm[i][:], bG2[:, 256:260], 1e-6, nscale[:], ALU.add, ALU.mult).then_inc(sem("nrm"), 1)
                wait(nc.vector, "nrm", at(kh, b, 1, 1))
                nc.vector.reciprocal(rcn[i][:], nrm[i][:, 2:4]).then_inc(sem("rcn"), 1)
                wait(nc.vector, "rcn", at(kh, b, 1, 1))
                wait(nc.vector, "bet", kh + 1)
                nc.vector.tensor_tensor(cj[i][:], bet[p][:, NC * b:NC * (b + 1), :], rcn[i][:].unsqueeze(2).broadcast_to([P, NC, R]),
                                        ALU.mult).then_inc(sem("cj"), 1)

            def dve_bp(kh, p, b, h):
                i = b % 2
                if h == 0:
                    wait(nc.vector, "cj", at(kh, b, 1, 1))
                    wait(nc.vector, "scan", at(kh, b, 4, 4))
                nc.vector.scalar_tensor_tensor(BP[p][:, b, h, :, 0:T], bG1[:].rearrange("p (x t) -> p x t", x=2), cj[i][:, 0, h:h + 1],
                                               E1[:, h, :].unsqueeze(1).broadcast_to([P, 2, T]), ALU.mult, ALU.mult).then_inc(sem("bp"), 1)
                nc.vector.scalar_tensor_tensor(BP[p][:, b, h, :, T:T + P], bG2[:, 0:2 * P].rearrange("p (x t) -> p x t", x=2), cj[i][:, 1, h:h + 1],
                                               E2[:, h, :].unsqueeze(1).broadcast_to([P, 2, P]), ALU.mult, ALU.mult).then_inc(sem("bp"), 1)

            def dve_mt(kh, p, b):
                wait(nc.vector, "mt", at(kh, b, 1, 1))
                nc.vector.tensor_tensor(MTs[:].rearrange("p c h t -> p (c h) t"), bMT[:].rearrange("p (n t) -> p n t", t=P),
                                        negoff[:].unsqueeze(1).broadcast_to([P, NC * R, P]), ALU.mult).then_inc(sem("mt_evac"), 1)

            def dve_x(kh, p, b, n):
                wait(nc.vector, "x_mm", at(kh, b, 9, n + 1))
                half = bX[:, (n + b) % 2 * 256:(n + b) % 2 * 256 + 256].rearrange("p (h d) -> p h d", h=R)
                if n == 4:
                    wait(nc.vector, "x_add", at(kh, b, 7, 3))
                    nc.vector.tensor_tensor(R2[:], Vs[:, b, 1], half, ALU.subtract).then_inc(sem("x_add"), 1)
                else:
                    rhs = Vs[:, b, 0] if n < 4 else R2[:]
                    if n == 5:
                        wait(nc.vector, "x_add", at(kh, b, 7, 4))
                    nc.vector.tensor_tensor(xs[:, n if n < 4 else n - 5], rhs, half, ALU.add).then_inc(sem("x_add"), 1)

            def dve_og(kh, p, b):
                for c in range(NC):
                    wait(nc.vector, "o", at(kh, b, 2, 2))
                    wait(nc.vector, "silu_z", at(kh, b, 1, 1))
                    if c == 0:
                        wait(nc.vector, "ogn", at(kh, b, 4, -4))
                    nc.vector.scalar_tensor_tensor(og[b % 2][:, c].rearrange("p h d -> p (h d)"), bO[:, c * 256:(c + 1) * 256],
                                                   vsc[p][:, b, c:c + 1], zs[:, b, c, :], ALU.mult, ALU.mult).then_inc(sem("og"), 1)

            def dve_acc(kh, p, b):
                wait(nc.vector, "f", at(kh, b, 1, 1))
                a = acc[:, NC * b:NC * (b + 1), :].rearrange("p c d -> p (c d)")
                wait(nc.vector, "acc", at(kh, b, 1, 1 - B))
                nc.vector.tensor_tensor(a, a, bF[:], ALU.add).then_inc(sem("acc"), 1)

            def dve_step(kh, p, b):
                qk, gram, vz, last = (beside(kh, p, b, n) for n in (LEAD_QK, LEAD_GRAM, LEAD_VZ, -1))

                def taps_qk(n):
                    if qk:
                        dve_tap(*qk, "qk", bQK, cqk, 0, n)

                def taps_v(n):
                    if vz:
                        dve_tap(*vz, "v", bV, cv, 2, n)

                if last:
                    dve_og(*last)
                dve_mt(kh, p, b)
                if b == 0:
                    dve_wo(kh, p)
                if gram and gram[2] == 0:
                    dve_bet(gram[0], gram[1])
                dve_x(kh, p, b, 0)
                if gram:
                    dve_scales(*gram)
                dve_x(kh, p, b, 1)
                if gram:
                    dve_bp(*gram, 0)
                dve_x(kh, p, b, 2)
                if gram:
                    dve_bp(*gram, 1)
                taps_v(1)
                dve_x(kh, p, b, 4)
                taps_v(2)
                taps_qk(1)
                dve_x(kh, p, b, 5)
                taps_v(3)
                dve_x(kh, p, b, 6)
                taps_qk(2)
                dve_x(kh, p, b, 7)
                taps_qk(3)
                if last:
                    dve_acc(*last)
                if qk:
                    for n in range(2 * R):
                        dve_scan(*qk, n)

            def pool_vsc(kh, p, b):
                wait(nc.gpsimd, "nrm", at(kh, b, 1, 1))
                wait(nc.gpsimd, "og", at(kh - 2, b, 2, 2))
                nc.gpsimd.tensor_tensor(vsc[p][:, b, :], nrm[b % 2][:], npow[:], ALU.pow).then_inc(sem("vsc"), 1)

            def pool_ro(kh, p, b):
                wait(nc.gpsimd, "ss", at(kh, b, 4, 4))
                wait(nc.gpsimd, "ro", at(kh, b, 2))
                nc.gpsimd.tensor_scalar(sse[:], ss[:], 1.0 / DK, 1e-6, ALU.mult, ALU.add).then_inc(sem("ro"), 1)
                wait(nc.gpsimd, "ro", at(kh, b, 2, 1))
                wait(nc.gpsimd, "ogn", at(kh, b, 4))
                nc.gpsimd.tensor_tensor(ro[:], sse[:], mhalf[:, 0:4], ALU.pow).then_inc(sem("ro"), 1)

            SPLIT = {0: (0, 2), 1: (2, 15), 2: (15, 30), 3: (30, BLK - 1)}

            def pool_step_done(ins, value):
                ins.then_inc(sem("t_step"), 1)
                wait(nc.gpsimd, "t_step", value)

            def pool_inverse_start(kh):
                wait(nc.gpsimd, "t_out", kh * 32)
                pool_step_done(nc.gpsimd.memset(Tn[:], 0.0), kh * NTS + 1)
                pool_step_done(nc.gpsimd.affine_select(out=Tn[:], in_=Tn[:], compare_op=ALU.not_equal, fill=1.0, base=0,
                                                       pattern=[[1, BLK], [-1, BLK]], channel_multiplier=0), kh * NTS + 2)

            def pool_inverse(kh, lo, hi):
                if lo == 0:
                    wait(nc.gpsimd, "blk_in", (kh + 1) * 16)
                for j in range(lo, hi):
                    r, c = BLK - 1 - j, j + 1
                    t = tmp[:, 0:r * c].rearrange("p (i c) -> p i c", c=c)
                    pool_step_done(nc.gpsimd.tensor_tensor(t, Dm[:, j, j + 1:BLK].unsqueeze(2).broadcast_to([SLOTS, r, c]),
                                                           Tn[:, j, 0:c].unsqueeze(1).broadcast_to([SLOTS, r, c]), ALU.mult),
                                   kh * NTS + 2 * j + 3)
                    pool_step_done(nc.gpsimd.tensor_tensor(Tn[:, j + 1:BLK, 0:c], Tn[:, j + 1:BLK, 0:c], t, ALU.subtract),
                                   kh * NTS + 2 * j + 4)

            def pool_step(kh, p, b):
                last, gram = beside(kh, p, b, -1), beside(kh, p, b, LEAD_GRAM)
                if last:
                    pool_ro(*last)
                if gram:
                    pool_vsc(*gram)
                if kh + 1 < NKH:
                    if b == 0:
                        pool_inverse_start(kh + 1)
                    pool_inverse(kh + 1, *SPLIT[b])

            def sp_load_qk(kh):
                p = kh % 2
                wait(nc.sync, "qk_mm", at(kh - 1, 0, 1))
                wait(nc.sync, "conv_qk", at(kh - 1, 0, 6))
                wait(nc.sync, "scan", at(kh - 1, 0, 4))
                nc.sync.dma_start(wqk[p][:], wqkvz_d[:, kh * CW:kh * CW + 2 * DK].rearrange("(k p) n -> p k n", p=P)).then_inc(sem(f"qk_in{p}"), 16)
                nc.sync.dma_start(cw[p][:, 0:2, :], convw_d[0:2 * NKH * P].rearrange("(x g p) s -> p x g s", x=2, p=P)[:, :, kh, :])\
                    .then_inc(sem(f"qk_in{p}"), 16)
                nc.sync.dma_start(alb[p][:].rearrange("p r t -> p (r t)"),
                                  alpha_dr[kh * R:(kh + 1) * R, :].rearrange("(o r) t -> o (r t)", o=1).broadcast_to([P, R * B * T]))\
                    .then_inc(sem(f"qk_in{p}"), 16)

            def sp_load_vz(kh):
                p = kh % 2
                wait(nc.sync, "z_mm", at(kh - 1, 0, 1))
                wait(nc.sync, "conv_v", at(kh - 1, 0, 6))
                nc.sync.dma_start(wvz[p][:], wqkvz_d[:, kh * CW + 2 * DK:(kh + 1) * CW].rearrange("(k p) n -> p k n", p=P)).then_inc(sem(f"vz_in{p}"), 16)
                nc.sync.dma_start(cw[p][:, 2:4, :], convw_d.rearrange("(g p) s -> p g s", p=P)[:, 2 * NKH + kh * R:2 * NKH + (kh + 1) * R, :])\
                    .then_inc(sem(f"vz_in{p}"), 16)

            def sp_load_wo(kh):
                wait(nc.sync, "f", at(kh - 1, 0, 1))
                nc.sync.dma_start(wo[kh % 2][:], wout_d[kh * R * DK:(kh + 1) * R * DK, :].rearrange("(h p) n -> p h n", p=DK)).then_inc(sem("wo_in"), 16)

            def sp_blocks_in(kh):
                wait(nc.sync, "bp", at(kh, B - 1, 4, 4))
                for n in range(NBLK):
                    r = slice(n * BLK, (n + 1) * BLK)
                    for c in range(NC):
                        i = (T if c else 0) + n * BLK
                        nc.sync.dma_start(blkin_dr[c, n].rearrange("u j i -> j u i"),
                                          BP[kh % 2][r, :, :, 1, i:i + BLK].rearrange("j b h i -> j (b h) i")).then_inc(sem("blk_dr"), 16)
                wait(nc.sync, "blk_dr", (kh + 1) * 16 * NC * NBLK)
                nc.sync.dma_start(Dm[:].rearrange("s j i -> s (j i)"), blkin_dr.rearrange("c n u j i -> (c n u) (j i)")).then_inc(sem("blk_in"), 16)

            def sp_blocks_out(kh):
                wait(nc.sync, "t_step", (kh + 1) * NTS)
                for b in range(B):
                    wait(nc.sync, f"t_in{b}", kh * 64)
                for c in range(NC):
                    half = slice(c * SLOTS // NC, (c + 1) * SLOTS // NC)
                    nc.sync.dma_start(tinv_dr[:, :, c].rearrange("n b h j i -> (n b) h (j i)"), Tn[half].rearrange("s j i -> s (j i)"))\
                        .then_inc(sem("t_out"), 16)
                wait(nc.sync, "t_out", (kh + 1) * 32)
                for b in range(B):
                    wait(nc.sync, "y", at(kh - 1, b, 2, 2))
                    for n in range(NBLK):
                        r = slice(n * BLK, (n + 1) * BLK)
                        nc.sync.dma_start(T32[r, b, :, r], tinv_dr[n, b].rearrange("c h j i -> j (c h) i")).then_inc(sem(f"t_in{b}"), 16)

            block = s1.enter_context(nc.Block())

            @block.sync
            def _(sp):
                sp.dma_start(nw[:], nw_d.rearrange("(p o) -> p o", o=1)).then_inc(sem("nw_in"), 16)
                sp_load_qk(0)
                sp_load_vz(0)
                sp_load_qk(1)
                sp_load_vz(1)
                sp_load_wo(0)
                sp.wait_ge(sem("zero"), 1)
                for kh in range(-1, NKH - 1):
                    sp_blocks_in(kh + 1)
                    if kh + 3 < NKH:
                        sp_load_qk(kh + 3)
                    if 0 <= kh and kh + 2 < NKH:
                        sp_load_vz(kh + 2)
                    if 0 <= kh:
                        sp_load_wo(kh + 1)
                    sp_blocks_out(kh + 1)

            LOOP = (1, NKH - 4)

            def steps(one, kh, p):
                for b in range(B):
                    one(kh, p, b)

            @block.tensor
            def _(pe):
                pe.wait_ge(sem("const1"), 1)
                for g in range(LEAD_QK):
                    kh, b = divmod(g, B)
                    for t in range(2):
                        pe_qk(kh, kh, b, t)
                    if g < LEAD_VZ:
                        for t in range(2):
                            pe_v(0, 0, b, t)
                        for c in range(NC):
                            pe_z(0, 0, b, c)
                        if g:
                            pe_vt(0, 0, b - 1)
                    if g < LEAD_GRAM:
                        pe_gram0(kh, kh, b)
                        pe_gram1(kh, kh, b)
                steps(pe_step, 0, 0)
                with pe.Fori(*LOOP, 2) as kh:
                    steps(pe_step, kh, 1)
                    steps(pe_step, kh + 1, 0)
                for kh in range(NKH - 3, NKH):
                    steps(pe_step, kh, kh % 2)
                pe_ot(NKH - 1, 1, B - 1)
                for c in range(NC):
                    pe_f(NKH - 1, 1, B - 1, c)

            @block.scalar
            def _(act):
                act.wait_ge(sem("qk_in0"), 48)
                act.wait_ge(sem("vz_in0"), 32)
                for g in range(LEAD_QK):
                    kh, b = divmod(g, B)
                    act_tap0(kh, kh, b, "qk", bQK, cqk, 0)
                    if g < LEAD_VZ:
                        act_tap0(0, 0, b, "v", bV, cv, 2)
                    act_silu_qk(kh, kh, b)
                    if g < LEAD_VZ:
                        if g:
                            act_silu_z(0, 0, b - 1)
                            act_vs(0, 0, b - 1)
                        act_silu_v(0, 0, b)
                steps(act_step, 0, 0)
                with act.Fori(*LOOP, 2) as kh:
                    steps(act_step, kh, 1)
                    steps(act_step, kh + 1, 0)
                for kh in range(NKH - 3, NKH):
                    steps(act_step, kh, kh % 2)
                act_ss(NKH - 1, 1, B - 1)
                act_ogn(NKH - 1, 1, B - 1)
                act_ots(NKH - 1, 1, B - 1)

            @block.vector
            def _(dve):
                nc.vector.memset(T32[:].rearrange("p b u t -> p (b u t)"), 0.0).then_inc(sem("zero"), 1)
                for b in range(B):
                    nc.vector.memset(acc[:, NC * b:NC * (b + 1), :].rearrange("p c d -> p (c d)"), 0.0).then_inc(sem("acc0"), 1)
                dve.wait_ge(sem("acc0"), B)
                dve.wait_ge(sem("const1"), 1)
                dve.wait_ge(sem("nw_in"), 16)
                for g in range(LEAD_QK):
                    kh, b = divmod(g, B)
                    if b == 0:
                        dve_bet(kh, kh)
                    for n in range(2 * R):
                        dve_scan(kh, kh, b, n)
                    for n in range(1, TAPS):
                        dve_tap(kh, kh, b, "qk", bQK, cqk, 0, n)
                    if g < LEAD_VZ:
                        for n in range(1, TAPS):
                            dve_tap(0, 0, b, "v", bV, cv, 2, n)
                    if g < LEAD_GRAM:
                        dve_scales(kh, kh, b)
                        for h in range(R):
                            dve_bp(kh, kh, b, h)
                steps(dve_step, 0, 0)
                with dve.Fori(*LOOP, 2) as kh:
                    steps(dve_step, kh, 1)
                    steps(dve_step, kh + 1, 0)
                for kh in range(NKH - 3, NKH):
                    steps(dve_step, kh, kh % 2)
                dve_og(NKH - 1, 1, B - 1)
                dve_acc(NKH - 1, 1, B - 1)

            @block.gpsimd
            def _(pool):
                n = 0
                for t, v in ((negoff[:], -1.0), (ones[:], 1.0), (npow[:, 0:2], -0.5), (npow[:, 2:4], 0.5),
                             (nscale[:, 0:2], float(DK)), (nscale[:, 2:4], 1.0)):
                    nc.gpsimd.memset(t, v).then_inc(sem("const1a"), 1)
                    n += 1
                pool.wait_ge(sem("const1a"), n)
                for m in range(NBLK):
                    r = slice(m * BLK, (m + 1) * BLK)
                    nc.gpsimd.memset(negoff[r, r], 0.0).then_inc(sem("const1a"), 1)
                    n += 1
                pool.wait_ge(sem("const1a"), n)
                nc.gpsimd.memset(tmp[:], 0.0).then_inc(sem("const1"), 1)
                pool.wait_ge(sem("const1"), 1)
                for b in range(B):
                    pool_vsc(0, 0, b)
                pool_inverse_start(0)
                pool_inverse(0, 0, BLK - 1)
                for b in range(LEAD_GRAM - B):
                    pool_vsc(1, 1, b)
                for kh in range(NKH):
                    for b in range(B):
                        pool_step(kh, kh % 2, b)
                pool_ro(NKH - 1, 1, B - 1)

        def residual(ch, t_out, b, branch, layer, m, mark):
            g = gates[:, layer, m, b, :].unsqueeze(1).broadcast_to([P, NC, D])
            wait(nc.vector, mark, b)
            ch.after(nc.vector.tensor_tensor(t_out, branch, g, ALU.mult))
            xv = x[:, NC * b:NC * (b + 1), :]
            nc.vector.tensor_tensor(xv, xv, t_out, ALU.add).then_inc(sem(mark), 1)

        with ExitStack() as s2:
            wraw = [sb(f"wraw{i}", [P, HT, D], I32, ctx=s2) for i in range(2)]
            draw = sb("draw", [P, KC, HID], I32, ctx=s2)
            wsc = sb("wsc", [P, 3, HT], ctx=s2)
            wnat = [sb(f"wnat{i}", [P, HT, D], ctx=s2) for i in range(2)]
            dnat = sb("dnat", [P, KC, HID], ctx=s2)
            wT = [sb(f"wT{i}", [P, KC, HT * P], ctx=s2) for i in range(2)]
            dT = sb("dT", [P, HT, D], ctx=s2)
            gsil = sb("gsil", [P, 2, 512], ctx=s2)
            hact = sb("hact", [P, HT, B * T], ctx=s2)
            rt = sb("rt2", [P, NC, D], ctx=s2)
            block = s2.enter_context(nc.Block())

            def rows(m):
                return P if m < HT - 1 else HREM

            @block.sync
            def _(sp):
                for i, (w_d, s_d) in enumerate(((wg_d, sg_d), (wu_d, su_d))):
                    sp.dma_start(wraw[i][:, 0:HT - 1, :], w_d[0:(HT - 1) * P, :].rearrange("(m p) d -> p m d", p=P)).then_inc(sem("ffn_w_in"), 16)
                    sp.dma_start(wraw[i][0:HREM, HT - 1, :], w_d[(HT - 1) * P:HID, :]).then_inc(sem("ffn_w_in"), 16)
                    sp.dma_start(wsc[:, i, 0:HT - 1], s_d[0:(HT - 1) * P].rearrange("(m p) -> p m", p=P), allow_slow_non_contiguous=True).then_inc(sem("ffn_w_in"), 16)
                    sp.dma_start(wsc[0:HREM, i, HT - 1:HT], s_d[(HT - 1) * P:HID].rearrange("(p o) -> p o", o=1)).then_inc(sem("ffn_w_in"), 16)
                sp.dma_start(draw[:], wd_d.rearrange("(m p) d -> p m d", p=P)).then_inc(sem("ffn_w_in"), 16)
                sp.dma_start(wsc[:, 2, 0:KC], sd_d.rearrange("(m p) -> p m", p=P), allow_slow_non_contiguous=True).then_inc(sem("ffn_w_in"), 16)

            @block.gpsimd
            def _(pool):
                ln_pool(pool, "ln1")

            @block.vector
            def _(dve):
                ch = Chain(dve, "ffn_chain")
                for b in range(B):
                    residual(ch, rt[:], b, acc[:, NC * b:NC * (b + 1), :], 0, 0, "res0a")
                ln_vector(dve, "ln1", lambda t: dve.wait_ge(sem("res0a"), t // NC + 1))
                dve.wait_ge(sem("ffn_w_in"), 160)
                for i in range(2):
                    for m in range(HT):
                        r = rows(m)
                        nc.vector.tensor_scalar(wnat[i][0:r, m, :], wraw[i][0:r, m, :], -128.0, wsc[0:r, i, m:m + 1],
                                                ALU.add, ALU.mult).then_inc(sem("deq"), 1)
                for m in range(KC):
                    nc.vector.tensor_scalar(dnat[:, m, :], draw[:, m, :], -128.0, wsc[:, 2, m:m + 1],
                                            ALU.add, ALU.mult).then_inc(sem("deq"), 1)
                for n in range(2 * HT):
                    th, m = divmod(n, HT)
                    r = rows(m)
                    dve.wait_ge(sem("up_mm"), n + 1)
                    dve.wait_ge(sem("gsil"), n + 1)
                    nc.vector.tensor_tensor(hact[0:r, m, th * 512:(th + 1) * 512], gsil[0:r, n % 2, :], bank[4 + n % 2][0:r, :],
                                            ALU.mult).then_inc(sem("hact"), 1)
                for b in range(B):
                    dve.wait_ge(sem("down_mm"), b + 1)
                    residual(ch, rt[:], b, bank[6 + b % 2][:].rearrange("p (c d) -> p c d", c=NC), 0, 1, "res0b")

            @block.scalar
            def _(act):
                ln_scalar(act, "ln1", 0, 3, 4)
                for n in range(3 * HT):
                    i, m = divmod(n, HT)
                    r = rows(m)
                    act.wait_ge(sem("wtr"), n + 1)
                    bk = bank[2 + n % 2]
                    if i < 2:
                        nc.scalar.activation(wT[i][:, :, m * P:m * P + r], bk[:, 0:2 * P].rearrange("p (k r) -> p k r", k=2)[:, :, 0:r],
                                             ACT.Copy).then_inc(sem("wT"), 1)
                    else:
                        nc.scalar.activation(dT[0:r, m, :], bk[0:r, 0:D], ACT.Copy).then_inc(sem("wT"), 1)
                for n in range(2 * HT):
                    th, m = divmod(n, HT)
                    r = rows(m)
                    act.wait_ge(sem("gate_mm2"), n + 1)
                    wait(act, "hact", n - 1)
                    nc.scalar.activation(gsil[0:r, n % 2, :], bank[2 + n % 2][0:r, :], ACT.Silu).then_inc(sem("gsil"), 1)

            @block.tensor
            def _(pe):
                ln_tensor(pe, "ln1")
                for n in range(3 * HT):
                    i, m = divmod(n, HT)
                    r = rows(m)
                    pe.wait_ge(sem("deq"), 2 * HT + KC if i == 2 else n + 1)
                    wait(pe, "wT", n - 1)
                    bk = bank[2 + n % 2]
                    for k in range(KC):
                        if i < 2:
                            last = nc.tensor.transpose(bk[:, k * P:k * P + r], wnat[i][0:r, m, k * P:(k + 1) * P], ident[0:r, 0:r])
                        else:
                            last = nc.tensor.transpose(bk[0:r, k * P:(k + 1) * P], dnat[:, k, m * P:m * P + r], ident)
                    last.then_inc(sem("wtr"), 1)
                pe.wait_ge(sem("ln1_hT"), KC * B)
                pe.wait_ge(sem("wT"), 3 * HT)
                for n in range(2 * HT):
                    th, m = divmod(n, HT)
                    r = rows(m)
                    wait(pe, "gsil", n - 1)
                    for k in range(KC):
                        last = nc.tensor.matmul(bank[2 + n % 2][0:r, :], wT[0][:, k, m * P:m * P + r], hT[:, k, th * 512:(th + 1) * 512],
                                                start=(k == 0), stop=(k == KC - 1))
                    last.then_inc(sem("gate_mm2"), 1)
                    wait(pe, "hact", n - 1)
                    for k in range(KC):
                        last = nc.tensor.matmul(bank[4 + n % 2][0:r, :], wT[1][:, k, m * P:m * P + r], hT[:, k, th * 512:(th + 1) * 512],
                                                start=(k == 0), stop=(k == KC - 1))
                    last.then_inc(sem("up_mm"), 1)
                for b in range(B):
                    pe.wait_ge(sem("hact"), HT * (b // 2 + 1))
                    wait(pe, "res0b", b - 1)
                    for c in range(NC):
                        t = NC * b + c
                        for m in range(HT):
                            r = rows(m)
                            last = nc.tensor.matmul(bank[6 + b % 2][:, c * D:(c + 1) * D], hact[0:r, m, t * P:(t + 1) * P], dT[0:r, m, :],
                                                    start=(m == 0), stop=(m == HT - 1))
                    last.then_inc(sem("down_mm"), 1)

        with ExitStack() as s3:
            wn1 = sb("wn1", [P, 4, KC, D], ctx=s3)
            wpad = sb("wpad", [P, 2, KC, NH1, 32], ctx=s3)
            wvo = sb("wvo", [P, 2, KC, D], ctx=s3)
            qkT = sb("qkT", [P, 2, QT, B * T], ctx=s3)
            v1 = sb("v1", [P, NT, D], ctx=s3)
            NBUF = 4
            prob = sb("prob", [P, NBUF, 384], ctx=s3)
            probT = sb("probT", [P, NBUF, 384], ctx=s3)
            mx = sb("mx", [P, B, NH1, NC], ctx=s3)
            nmx = sb("nmx", [P, B, NH1, NC], ctx=s3)
            sums = sb("sums", [P, B, NC, NH1], ctx=s3)
            rsum = sb("rsum", [P, B, NC, NH1], ctx=s3)
            at1 = sb("at1", [P, NC, D], ctx=s3)
            atT = sb("atT", [P, KC, NC, P], ctx=s3)
            rt = sb("rt3", [P, NC, D], ctx=s3)
            block = s3.enter_context(nc.Block())
            NBH = B * NH1
            HS = float(HD) ** -0.5

            @block.sync
            def _(sp):
                for i, w_d in enumerate((wq1_d, wk1_d, wv1_d, wo1_d)):
                    sp.dma_start(wn1[:, i], w_d.rearrange("(m p) d -> p m d", p=P)).then_inc(sem("w1_in"), 16)

            @block.gpsimd
            def _(pool):
                nc.gpsimd.memset(wpad[:].rearrange("p a k h e -> p (a k h e)"), 0.0).then_inc(sem("wpad0"), 1)
                ln_pool(pool, "ln2")

            @block.vector
            def _(dve):
                ln_vector(dve, "ln2", lambda t: None)
                for n in range(2 * QT * 2):
                    i, rest = divmod(n, QT * 2)
                    q, th = divmod(rest, 2)
                    dve.wait_ge(sem("qk1_mm"), n + 1)
                    nc.vector.tensor_copy(qkT[:, i, q, th * 512:(th + 1) * 512], bank[2 + n % 2][:]).then_inc(sem("qk1"), 1)
                ch = Chain(dve, "att_chain")
                for n in range(NBH + 2):
                    if n < NBH:
                        b, h = divmod(n, NH1)
                        dve.wait_ge(sem("s_mm"), n + 1)
                        s = bank[n % 3]
                        nc.vector.reduce_max(mx[:, b, h, 0:1], s[:, 0:P], AX.X).then_inc(sem("mx"), 1)
                        nc.vector.reduce_max(mx[:, b, h, 1:2], s[:, P:3 * P], AX.X).then_inc(sem("mx"), 1)
                        dve.wait_ge(sem("mx"), 2 * (n + 1))
                        nc.vector.tensor_scalar(nmx[:, b, h, :], mx[:, b, h, :], -HS, None, ALU.mult).then_inc(sem("nmx"), 1)
                    if n >= 2:
                        m = n - 2
                        b, h = divmod(m, NH1)
                        dve.wait_ge(sem("pt_mm"), m + 1)
                        wait(dve, "pv", m - NBUF + 1)
                        nc.vector.tensor_copy(probT[:, m % NBUF, :], bank[3 + m % 2][:, 0:384]).then_inc(sem("pt"), 1)
                    if n >= 4 and (n - 4) % NH1 == NH1 - 1 or n == NBH + 1:
                        b = (n - 4) // NH1 if n < NBH + 1 else B - 1
                        dve.wait_ge(sem("expo"), 2 * NH1 * (b + 1))
                        ch.after(nc.vector.reciprocal(rsum[:, b], sums[:, b]))
                        dve.wait_ge(sem("pv"), NH1 * (b + 1))
                        wait(dve, "at_tr", b)
                        nc.vector.tensor_tensor(at1[:].rearrange("p c (h e) -> p (c h) e", e=HD),
                                                bank[5][:].rearrange("p (n e) -> p n e", e=HD),
                                                rsum[:, b].rearrange("p c h -> p (c h)").unsqueeze(2).broadcast_to([P, NC * NH1, HD]),
                                                ALU.mult).then_inc(sem("at1"), 1)
                        if b:
                            dve.wait_ge(sem("o1_mm"), b)
                            residual(ch, rt[:], b - 1, bank[7][:].rearrange("p (c d) -> p c d", c=NC), 1, 0, "res1a")
                dve.wait_ge(sem("o1_mm"), B)
                residual(ch, rt[:], B - 1, bank[7][:].rearrange("p (c d) -> p c d", c=NC), 1, 0, "res1a")

            @block.scalar
            def _(act):
                ln_scalar(act, "ln2", 1, 0, 1)
                act.wait_ge(sem("wpad0"), 1)
                for n in range(8):
                    i, k = divmod(n, 2)
                    act.wait_ge(sem("w1tr"), n + 1)
                    src = bank[2 + n % 2][:, 0:D]
                    if i < 2:
                        nc.scalar.activation(wpad[:, i, k, :, 0:HD], src.rearrange("p (h e) -> p h e", e=HD), ACT.Copy).then_inc(sem("w1T"), 1)
                    else:
                        nc.scalar.activation(wvo[:, i - 2, k, :], src, ACT.Copy).then_inc(sem("w1T"), 1)
                for b in range(B):
                    act.wait_ge(sem("v1_mm"), b + 1)
                    nc.scalar.activation(v1[:, NC * b:NC * (b + 1), :].rearrange("p c d -> p (c d)"), bank[4 + b % 2][:], ACT.Copy).then_inc(sem("v1"), 1)
                for n in range(NBH + 5):
                    if n < NBH:
                        b, h = divmod(n, NH1)
                        act.wait_ge(sem("nmx"), n + 1)
                        wait(act, "pt_mm", n - NBUF + 1)
                        s = bank[n % 3]
                        for c in range(NC):
                            lo, hi = (0, P) if c == 0 else (P, 3 * P)
                            nc.scalar.activation(prob[:, n % NBUF, lo:hi], s[:, lo:hi], ACT.Exp, bias=nmx[:, b, h, c:c + 1],
                                                 scale=HS, accum_out=sums[:, b, c, h:h + 1]).then_inc(sem("expo"), 1)
                    if n >= 5 and (n - 5) % NH1 == NH1 - 1:
                        b = (n - 5) // NH1
                        act.wait_ge(sem("at_tr"), b + 1)
                        wait(act, "o1_mm", b)
                        nc.scalar.activation(atT[:].rearrange("p k c t -> p (k c t)"), bank[6][:], ACT.Copy).then_inc(sem("atT"), 1)

            @block.tensor
            def _(pe):
                ln_tensor(pe, "ln2")
                pe.wait_ge(sem("w1_in"), 64)
                for n in range(8):
                    i, k = divmod(n, 2)
                    wait(pe, "w1T", n - 1)
                    for m in range(KC):
                        last = nc.tensor.transpose(bank[2 + n % 2][:, m * P:(m + 1) * P], wn1[:, i, m, k * P:(k + 1) * P], ident)
                    last.then_inc(sem("w1tr"), 1)
                pe.wait_ge(sem("w1T"), 8)
                pe.wait_ge(sem("ln2_hT"), KC * B)
                for n in range(2 * QT * 2):
                    i, rest = divmod(n, QT * 2)
                    q, th = divmod(rest, 2)
                    wait(pe, "qk1", n - 1)
                    for k in range(KC):
                        last = nc.tensor.matmul(bank[2 + n % 2][:], wpad[:, i, k, 4 * q:4 * q + 4, :].rearrange("p h e -> p (h e)"),
                                                hT[:, k, th * 512:(th + 1) * 512], start=(k == 0), stop=(k == KC - 1))
                    last.then_inc(sem("qk1_mm"), 1)
                for b in range(B):
                    wait(pe, "v1", b - 1)
                    for c in range(NC):
                        t = NC * b + c
                        for k in range(KC):
                            last = nc.tensor.matmul(bank[4 + b % 2][:, c * D:(c + 1) * D], hT[:, k, t * P:(t + 1) * P], wvo[:, 0, k, :],
                                                    start=(k == 0), stop=(k == KC - 1))
                    last.then_inc(sem("v1_mm"), 1)
                pe.wait_ge(sem("qk1"), 2 * QT * 2)
                pe.wait_ge(sem("v1"), B)
                for n in range(NBH + 5):
                    if n < NBH:
                        b, h = divmod(n, NH1)
                        wait(pe, "expo", 2 * (n - 2))
                        s = bank[n % 3]
                        pr = slice(32 * (h % 4), 32 * (h % 4) + 32)
                        for c in range(NC):
                            lo, w = (0, P) if c == 0 else (P, 2 * P)
                            nc.tensor.matmul(s[:, lo:lo + w], qkT[pr, 0, h // 4, b * T + c * P:b * T + (c + 1) * P],
                                             qkT[pr, 1, h // 4, b * T:b * T + w], start=True, stop=False)
                            last = nc.tensor.matmul(s[:, lo + w - P:lo + w], eyeb[:], cmask[:], start=False, stop=True)
                        last.then_inc(sem("s_mm"), 1)
                    if 2 <= n < NBH + 2:
                        m = n - 2
                        pe.wait_ge(sem("expo"), 2 * (m + 1))
                        wait(pe, "pt", m - 1)
                        for j in range(3):
                            last = nc.tensor.transpose(bank[3 + m % 2][:, j * P:(j + 1) * P], prob[:, m % NBUF, j * P:(j + 1) * P], ident)
                        last.then_inc(sem("pt_mm"), 1)
                    if 3 <= n < NBH + 3:
                        m = n - 3
                        b, h = divmod(m, NH1)
                        pe.wait_ge(sem("pt"), m + 1)
                        if h == 0:
                            wait(pe, "at1", b)
                        e = slice(h * HD, (h + 1) * HD)
                        o = [bank[5][:, c * D + h * HD:c * D + (h + 1) * HD] for c in range(NC)]
                        nc.tensor.matmul(o[0], probT[:, m % NBUF, 0:P], v1[:, NC * b, e], start=True, stop=True)
                        nc.tensor.matmul(o[1], probT[:, m % NBUF, P:2 * P], v1[:, NC * b, e], start=True, stop=False)
                        nc.tensor.matmul(o[1], probT[:, m % NBUF, 2 * P:3 * P], v1[:, NC * b + 1, e], start=False, stop=True).then_inc(sem("pv"), 1)
                    if n >= 5 and (n - 5) % NH1 == NH1 - 1:
                        b = (n - 5) // NH1
                        pe.wait_ge(sem("at1"), b + 1)
                        wait(pe, "atT", b)
                        for k in range(KC):
                            for c in range(NC):
                                last = nc.tensor.transpose(bank[6][:, (k * NC + c) * P:(k * NC + c + 1) * P], at1[:, c, k * P:(k + 1) * P], ident)
                        last.then_inc(sem("at_tr"), 1)
                        pe.wait_ge(sem("atT"), b + 1)
                        wait(pe, "res1a", b)
                        for c in range(NC):
                            for k in range(KC):
                                last = nc.tensor.matmul(bank[7][:, c * D:(c + 1) * D], atT[:, k, c, :], wvo[:, 1, k, :],
                                                        start=(k == 0), stop=(k == KC - 1))
                        last.then_inc(sem("o1_mm"), 1)

        with ExitStack() as s4:
            fac = sb("fac", [P, RANK, KC, D], ctx=s4)
            fsum = sb("fsum", [P, KC, D], ctx=s4)
            biasb = sb("biasb", [P, D], ctx=s4)
            rt = sb("rt4", [P, NC, D], ctx=s4)
            block = s4.enter_context(nc.Block())

            @block.sync
            def _(sp):
                sp.dma_start(fac[:], fac_d.rearrange("r (k p) e -> p r k e", p=P)).then_inc(sem("fac_in"), 16)
                sp.dma_start(biasb[:], bias_d.rearrange("(o e) -> o e", o=1).broadcast_to([P, D])).then_inc(sem("fac_in"), 16)
                for b in range(B):
                    sp.wait_ge(sem("res1b"), b + 1)
                    sp.dma_start(out_d[b].rearrange("(c p) d -> p c d", p=P), x[:, NC * b:NC * (b + 1), :]).then_inc(sem("out"), 16)
                sp.wait_ge(sem("out"), 16 * B)

            @block.gpsimd
            def _(pool):
                ln_pool(pool, "ln3")

            @block.scalar
            def _(act):
                ln_scalar(act, "ln3", 1, 3, 4)

            @block.vector
            def _(dve):
                ln_vector(dve, "ln3", lambda t: None)
                ch = Chain(dve, "fac_chain")
                dve.wait_ge(sem("fac_in"), 32)
                ch.after(nc.vector.tensor_tensor(fsum[:], fac[:, 0], fac[:, 1], ALU.add))
                for r in range(2, RANK):
                    i = nc.vector.tensor_tensor(fsum[:], fsum[:], fac[:, r], ALU.add)
                    if r < RANK - 1:
                        ch.after(i)
                i.then_inc(sem("fsum"), 1)
                for b in range(B):
                    dve.wait_ge(sem("fac_mm"), b + 1)
                    wait(dve, "res1b", b)
                    ch.after(nc.vector.scalar_tensor_tensor(rt[:], bank[2 + b % 2][:].rearrange("p (c d) -> p c d", c=NC), float(RANK) ** -0.5,
                                                            biasb[:].unsqueeze(1).broadcast_to([P, NC, D]), ALU.mult, ALU.add))
                    residual(ch, rt[:], b, rt[:], 1, 1, "res1b")

            @block.tensor
            def _(pe):
                ln_tensor(pe, "ln3")
                pe.wait_ge(sem("ln3_hT"), KC * B)
                pe.wait_ge(sem("fsum"), 1)
                for b in range(B):
                    wait(pe, "res1b", b - 1)
                    for c in range(NC):
                        t = NC * b + c
                        for k in range(KC):
                            last = nc.tensor.matmul(bank[2 + b % 2][:, c * D:(c + 1) * D], hT[:, k, t * P:(t + 1) * P], fsum[:, k, :],
                                                    start=(k == 0), stop=(k == KC - 1))
                    last.then_inc(sem("fac_mm"), 1)


_INS = ['L0_attn_hidden_states', 'L0_attn_W_qkvz', 'L0_attn_W_ba', 'L0_attn_conv_w', 'L0_attn_dt_bias', 'L0_attn_A_log',
        'L0_attn_norm_weight', 'L0_attn_W_out', 'L0_ffn_wq_gate', 'L0_ffn_s_gate', 'L0_ffn_wq_up', 'L0_ffn_s_up',
        'L0_ffn_wq_down', 'L0_ffn_s_down', 'L0_c', 'L0_wmod', 'L1_attn_wq', 'L1_attn_wk', 'L1_attn_wv', 'L1_attn_wo',
        'L1_ffn_factors', 'L1_ffn_bias', 'L1_c', 'L1_wmod']


def kernel(**inputs):
    import concourse.bacc as _bacc
    from concourse.bass_utils import run_bass_kernel_spmd as _run

    nc = _bacc.Bacc("TRN2", target_bir_lowering=False, num_devices=1)
    arrays, args = {}, []
    for name in _INS:
        a = np.ascontiguousarray(inputs[name])
        arrays[f"in_{name}"] = a
        args.append(nc.dram_tensor(f"in_{name}", a.shape, mybir.dt.from_np(a.dtype), kind="ExternalInput").ap())
    args.append(nc.dram_tensor("out_x", (B, T, D), F32, kind="ExternalOutput").ap())
    build(nc, *args)
    r = _run(nc, [arrays], core_ids=[0])
    return r.results[0]["out_x"]
```

```python
import concourse.bass as bass
from concourse import mybir
from contextlib import ExitStack
import numpy as np


F32 = mybir.dt.float32
BF16 = mybir.dt.bfloat16
F32R = mybir.dt.float32r
I32 = mybir.dt.int32
ALU = mybir.AluOpType
ACT = mybir.ActivationFunctionType
AX = mybir.AxisListType

B, T, D = 4, 256, 256
P = 128
NC = T // P
NT = B * NC
KC = D // P
NKH, R = 16, 2
NVH = NKH * R
DK = 128
CW = 2 * DK + 2 * R * DK
TAPS = 4
BLK = 32
NBLK = P // BLK
SLOTS = NC * NBLK * B * R
HID = 704
HT = (HID + P - 1) // P
HREM = HID - (HT - 1) * P
NH1, HD = 16, 16
QT = NH1 // 4
RANK = 8
MODS = 6


def build(nc, x_d, wqkvz_d, wba_d, convw_d, dtb_d, alog_d, nw_d, wout_d, wg_d, sg_d, wu_d, su_d, wd_d, sd_d,
          c0_d, wmod0_d, wq1_d, wk1_d, wv1_d, wo1_d, fac_d, bias_d, c1_d, wmod1_d, out_d):
    outer = ExitStack()
    sems = {}

    def sem(name):
        if name not in sems:
            sems[name] = outer.enter_context(nc.semaphore(name))
        return sems[name]

    def wait(eng, name, value):
        if isinstance(value, int) and value <= 0:
            return
        eng.wait_ge(sem(name), value)

    class Chain:

        def __init__(self, eng, name):
            self.eng, self.name, self.n = eng, name, 0

        def after(self, ins):
            ins.then_inc(sem(self.name), 1)
            self.n += 1
            self.eng.wait_ge(sem(self.name), self.n)

    with outer:
        def sb(name, shape, dt=F32, ctx=outer):
            return ctx.enter_context(nc.sbuf_tensor(name, shape, dt))

        bank = [outer.enter_context(nc.psum_tensor(f"bank{i}", [P, 512], F32)) for i in range(8)]

        alpha_dr = nc.dram_tensor("alpha_scratch", [NVH, B * T], F32, kind="Internal").ap()
        gates_dr = nc.dram_tensor("gates_scratch", [2 * 2, B, D], F32, kind="Internal").ap()
        blkin_dr = nc.dram_tensor("blk_in_scratch", [NC, NBLK, B * R, BLK, BLK], F32, kind="Internal").ap()
        tinv_dr, ttin_dr = (nc.dram_tensor(name, [NBLK, B, NC, R, BLK, BLK], F32, kind="Internal").ap()
                            for name in ("tinv_scratch", "tinv_t_scratch"))

        x = sb("x", [P, NT, D])
        xn = sb("xn", [P, NT, D])
        hT = sb("hT", [P, KC, B * T])
        eye = sb("eye", [P, T])
        eyeb = sb("eyeb", [P, P], BF16)
        cmask = sb("cmask", [P, P], BF16)
        modT = sb("modT", [P, 2, MODS * KC, B])
        stats = sb("stats", [P, NT, 6])
        mv = sb("mv", [P, NT, 2])
        rstd = sb("rstd", [P, NT])
        vare = sb("vare", [P, NT])
        mhalf = sb("mhalf", [P, NT])
        ident = eye[:, 0:P]

        def ln_vector(dve, i, ready):
            for t in range(NT):
                ready(t)
                nc.vector.bn_stats(stats[:, t, :], x[:, t, :]).then_inc(sem("ln_stats"), 1)
            for t in range(NT):
                dve.wait_ge(sem("ln_stats"), i * NT + t + 1)
                nc.vector.bn_aggr(mv[:, t, :], stats[:, t, :]).then_inc(sem("ln_mv"), 1)
            for t in range(NT):
                if t == 0:
                    dve.wait_ge(sem("ln_rstd"), 2 * i + 2)
                nc.vector.tensor_scalar(xn[:, t, :], x[:, t, :], mv[:, t, 0:1], rstd[:, t:t + 1],
                                        ALU.subtract, ALU.mult).then_inc(sem("ln_norm"), 1)

        def ln_pool(pool, i):
            pool.wait_ge(sem("ln_mv"), (i + 1) * NT)
            nc.gpsimd.tensor_scalar(vare[:], mv[:, :, 1], 1e-5, None, ALU.add).then_inc(sem("ln_rstd"), 1)
            pool.wait_ge(sem("ln_rstd"), 2 * i + 1)
            nc.gpsimd.tensor_tensor(rstd[:], vare[:], mhalf[:], ALU.pow).then_inc(sem("ln_rstd"), 1)

        def ln_tensor(pe, i):
            for b in range(B):
                pe.wait_ge(sem("ln_norm"), i * NT + NC * (b + 1))
                if b >= 2:
                    wait(pe, "ln_hT", i * KC * B + KC * (b - 1))
                for k in range(KC):
                    for c in range(NC):
                        last = nc.tensor.transpose(bank[b % 2][:, k * T + c * P:k * T + (c + 1) * P],
                                                   xn[:, NC * b + c, k * P:(k + 1) * P], ident)
                last.then_inc(sem("ln_tr"), 1)

        def ln_scalar(act, i, layer, shift, scale):
            for b in range(B):
                act.wait_ge(sem("ln_tr"), i * B + b + 1)
                for k in range(KC):
                    nc.scalar.activation(hT[:, k, b * T:(b + 1) * T], bank[b % 2][:, k * T:(k + 1) * T],
                                         ACT.Identity, bias=modT[:, layer, shift * KC + k, b:b + 1],
                                         scale=modT[:, layer, scale * KC + k, b:b + 1]).then_inc(sem("ln_hT"), 1)

        beta = sb("beta", [P, NT, NVH])
        mid = outer.enter_context(ExitStack())
        hh = sb("hh", [P, KC, B * T], F32R, ctx=mid)
        hl = sb("hl", [P, KC, B * T], F32R, ctx=mid)

        def ba(which):
            return bank[2][:].rearrange("p (n x r) -> p n x r", x=2, r=R)[:, :, which, :]

        with ExitStack() as s0:
            wmod = [sb(f"wmod{l}", [P, KC, MODS * D], ctx=s0) for l in range(2)]
            cin = sb("cin", [P, 2, KC, B], ctx=s0)
            csil = sb("csil", [P, 2, KC, B], ctx=s0)
            mrow = sb("mrow", [B, 2, MODS * D], ctx=s0)
            gsign = sb("gsign", [B, 4, D], ctx=s0)
            gabs = sb("gabs", [B, 4, D], ctx=s0)
            wba = sb("wba", [P, KC, NVH * 2], ctx=s0)
            dtb = sb("dtb", [P, NVH], ctx=s0)
            alog = sb("alog", [P, NVH], ctx=s0)
            ea = sb("ea", [P, NVH], ctx=s0)
            gx, gn, gu, gw, gl, gd = (sb(f"gate_tmp{i}", [P, NT, NVH], ctx=s0) for i in range(6))
            alpT = sb("alpT", [NVH, B * T], ctx=s0)

            block = s0.enter_context(nc.Block())

            @block.sync
            def _(sp):
                for b in range(B):
                    sp.dma_start(x[:, NC * b:NC * (b + 1), :], x_d[b].rearrange("(c p) d -> p c d", p=P)).then_inc(sem("x_in"), 16)
                for l, (c_d, w_d) in enumerate(((c0_d, wmod0_d), (c1_d, wmod1_d))):
                    for k in range(KC):
                        sp.dma_start(cin[:, l, k, :], c_d[:, k * P:(k + 1) * P].rearrange("b p -> p b"), allow_slow_non_contiguous=True).then_inc(sem("c_in"), 16)
                    sp.dma_start(wmod[l][:], w_d.rearrange("(k p) n -> p k n", p=P)).then_inc(sem(f"wmod_in{l}"), 16)
                    if l == 0:
                        sp.dma_start(wba[:], wba_d.rearrange("(k p) n -> p k n", p=P)).then_inc(sem("wba_in"), 16)
                        sp.dma_start(dtb[:], dtb_d.rearrange("(o h) -> o h", o=1).broadcast_to([P, NVH])).then_inc(sem("wba_in"), 16)
                        sp.dma_start(alog[:], alog_d.rearrange("(o h) -> o h", o=1).broadcast_to([P, NVH])).then_inc(sem("wba_in"), 16)
                sp.wait_ge(sem("gates"), 1)
                sp.dma_start(gates_dr.rearrange("g b d -> b g d"), gsign[:]).then_inc(sem("alpha_out"), 16)
                sp.wait_ge(sem("alpha_t"), 2)
                sp.dma_start(alpha_dr, alpT[:]).then_inc(sem("alpha_out"), 16)
                sp.wait_ge(sem("alpha_out"), 32)

            @block.gpsimd
            def _(pool):
                nc.gpsimd.memset(eye[:], 0.0).then_inc(sem("const"), 1)
                nc.gpsimd.memset(eyeb[:], 0.0).then_inc(sem("const"), 1)
                nc.gpsimd.memset(cmask[:], 0.0).then_inc(sem("const"), 1)
                nc.gpsimd.memset(mhalf[:], -0.5).then_inc(sem("const"), 1)
                pool.wait_ge(sem("const"), 4)
                nc.gpsimd.affine_select(out=eye[:, 0:P], in_=eye[:, 0:P], compare_op=ALU.not_equal, fill=1.0, base=0,
                                        pattern=[[-1, P]], channel_multiplier=1).then_inc(sem("const"), 1)
                nc.gpsimd.affine_select(out=eyeb[:], in_=eyeb[:], compare_op=ALU.not_equal, fill=1.0, base=0,
                                        pattern=[[-1, P]], channel_multiplier=1).then_inc(sem("const"), 1)
                nc.gpsimd.affine_select(out=cmask[:], in_=cmask[:], compare_op=ALU.is_ge, fill=-1e30, base=0,
                                        pattern=[[-1, P]], channel_multiplier=1).then_inc(sem("const"), 1)
                ln_pool(pool, 0)

            @block.scalar
            def _(act):
                act.wait_ge(sem("c_in"), 16 * 2 * KC)
                nc.scalar.activation(csil[:], cin[:], ACT.Silu).then_inc(sem("csil"), 1)
                act.wait_ge(sem("modT"), 4)
                ln_scalar(act, 0, 0, 0, 1)
                act.wait_ge(sem("g_neg"), 1)
                nc.scalar.activation(gu[:], gn[:], ACT.Exp).then_inc(sem("g_act"), 1)
                act.wait_ge(sem("wba_in"), 48)
                nc.scalar.activation(ea[:], alog[:], ACT.Exp).then_inc(sem("g_act"), 1)
                act.wait_ge(sem("gw"), 1)
                nc.scalar.activation(gl[:], gw[:], ACT.Ln).then_inc(sem("g_act"), 1)
                act.wait_ge(sem("g_log"), 1)
                nc.scalar.activation(gx[:], gu[:], ACT.Exp).then_inc(sem("alpha"), 1)
                nc.scalar.activation(beta[:].rearrange("p t (h r) -> p (t h) r", r=R), ba(0), ACT.Sigmoid).then_inc(sem("beta"), 1)
                nc.scalar.activation(hh[:], hT[:], ACT.Copy).then_inc(sem("hh"), 1)

            @block.vector
            def _(dve):
                for l in range(2):
                    for j in range(3):
                        dve.wait_ge(sem("mod_mm"), 3 * l + j + 1)
                        nc.vector.tensor_copy(mrow[:, l, j * 512:(j + 1) * 512], bank[2 + 3 * l + j][0:B, :]).then_inc(sem("mrow"), 1)
                for l in range(2):
                    dve.wait_ge(sem("mod_tr"), l + 1)
                    half = MODS * KC * B // 2
                    nc.vector.tensor_copy(modT[:, l].rearrange("p (g m) b -> p g (m b)", g=2)[:, :, 0:2 * KC * B],
                                          bank[2 + 3 * l][:, 0:2 * half].rearrange("p (g n) -> p g n", g=2)[:, :, 0:2 * KC * B]).then_inc(sem("modT"), 1)
                dve.wait_ge(sem("modT"), 2)
                for m in (1, 4):
                    v = modT[:, :, m * KC:(m + 1) * KC, :].rearrange("p l k b -> p l (k b)")
                    nc.vector.tensor_scalar(v, v, 1.0, None, ALU.add).then_inc(sem("modT"), 1)
                ln_vector(dve, 0, lambda t: dve.wait_ge(sem("x_in"), 16 * B))
                gc = Chain(dve, "g_chain")
                dve.wait_ge(sem("wba_in"), 48)
                dve.wait_ge(sem("ba_proj"), 1)
                gc.after(nc.vector.tensor_tensor(gx[:].rearrange("p t (h r) -> p t h r", r=R), ba(1).rearrange("p (t h) r -> p t h r", t=NT),
                                                 dtb[:].rearrange("p (h r) -> p h r", r=R).unsqueeze(1).broadcast_to([P, NT, NKH, R]), ALU.add))
                nc.vector.scalar_tensor_tensor(gn[:], gx[:], -1.0, gx[:], ALU.mult, ALU.min).then_inc(sem("g_neg"), 1)
                dve.wait_ge(sem("g_act"), 1)
                nc.vector.tensor_scalar(gw[:], gu[:], 1.0, None, ALU.add).then_inc(sem("gw"), 1)
                dve.wait_ge(sem("gw"), 1)
                gc.after(nc.vector.tensor_scalar(gd[:], gw[:], -1.0, 1e-30, ALU.add, ALU.add))
                gc.after(nc.vector.reciprocal(gd[:], gd[:]))
                dve.wait_ge(sem("g_act"), 3)
                gc.after(nc.vector.scalar_tensor_tensor(gl[:], gl[:], 1e-30, gd[:], ALU.add, ALU.mult))
                gc.after(nc.vector.tensor_tensor(gl[:], gl[:], gu[:], ALU.mult))
                gc.after(nc.vector.scalar_tensor_tensor(gl[:], gx[:], 0.0, gl[:], ALU.max, ALU.add))
                nc.vector.scalar_tensor_tensor(gu[:], gl[:], -1.0, ea[:].unsqueeze(1).broadcast_to([P, NT, NVH]), ALU.mult, ALU.mult)\
                    .then_inc(sem("g_log"), 1)
                ch = Chain(dve, "gate_chain")
                src = mrow[:].rearrange("b l (g n) -> b (l g) n", g=2)[:, :, 2 * D:3 * D]
                dve.wait_ge(sem("mrow"), 6)
                ch.after(nc.vector.scalar_tensor_tensor(gabs[:], src, -1.0, src, ALU.mult, ALU.max))
                ch.after(nc.vector.tensor_scalar(gabs[:], gabs[:], 0.25, None, ALU.max))
                ch.after(nc.vector.tensor_scalar(gsign[:], src, 0.0, 2.0, ALU.is_ge, ALU.mult))
                nc.vector.scalar_tensor_tensor(gsign[:], gsign[:], -1.0, gabs[:], ALU.add, ALU.mult).then_inc(sem("gates"), 1)
                dve.wait_ge(sem("hh"), 1)
                nc.vector.tensor_tensor(hl[:], hT[:], hh[:].bitcast(F32), ALU.subtract).then_inc(sem("hl"), 1)
                for h in range(2):
                    dve.wait_ge(sem("alpha_tr"), h + 1)
                    nc.vector.tensor_copy(alpT[:, h * 512:(h + 1) * 512], bank[6 + h][0:NVH, :]).then_inc(sem("alpha_t"), 1)

            @block.tensor
            def _(pe):
                pe.wait_ge(sem("const"), 7)
                for l in range(2):
                    pe.wait_ge(sem(f"wmod_in{l}"), 16)
                    pe.wait_ge(sem("csil"), 1)
                    for j in range(3):
                        for k in range(KC):
                            last = nc.tensor.matmul(bank[2 + 3 * l + j][0:B, :], csil[:, l, k, :], wmod[l][:, k, j * 512:(j + 1) * 512],
                                                    start=(k == 0), stop=(k == KC - 1))
                        last.then_inc(sem("mod_mm"), 1)
                for l in range(2):
                    pe.wait_ge(sem("mrow"), 3 * (l + 1))
                    for m in (0, 1, 3, 4):
                        for k in range(KC):
                            n = m * KC + k
                            last = nc.tensor.transpose(bank[2 + 3 * l][:, n * B:(n + 1) * B], mrow[:, l, n * P:(n + 1) * P], ident[0:B, 0:B])
                    last.then_inc(sem("mod_tr"), 1)
                ln_tensor(pe, 0)
                pe.wait_ge(sem("ln_hT"), 1 * KC * B)
                pe.wait_ge(sem("wba_in"), 48)
                pe.wait_ge(sem("modT"), 2)
                for t in range(NT):
                    for k in range(KC):
                        last = nc.tensor.matmul(bank[2][:, t * 2 * NVH:(t + 1) * 2 * NVH], hT[:, k, t * P:(t + 1) * P], wba[:, k, :],
                                                start=(k == 0), stop=(k == KC - 1))
                last.then_inc(sem("ba_proj"), 1)
                pe.wait_ge(sem("alpha"), 1)
                for t in range(NT):
                    last = nc.tensor.transpose(bank[6 + t // 4][0:NVH, t % 4 * P:(t % 4 + 1) * P], gx[:, t, :], ident)
                    if t % 4 == 3:
                        last.then_inc(sem("alpha_tr"), 1)

        acc = xn
        with ExitStack() as s1:
            rqk = sb("rqk", [P, KC, 2 * DK], ctx=s1)
            rvz = sb("rvz", [P, KC, 2 * R * DK], ctx=s1)
            wqk = [[sb(f"wqk_{part}{p}", [P, KC, 2 * DK], F32R, ctx=s1) for part in ("hi", "lo")] for p in range(2)]
            wvz = [[sb(f"wvz_{part}{p}", [P, KC, 2 * R * DK], F32R, ctx=s1) for part in ("hi", "lo")] for p in range(2)]
            wo = [sb(f"wo{p}", [P, R, D], ctx=s1) for p in range(2)]
            alb = [sb("alb0", [P, R, B * T], ctx=s1)[:], x[:].rearrange("p t d -> p (t d)").rearrange("p (r n) -> p r n", r=R)]
            cw = [sb(f"cw{p}", [P, 4, TAPS], ctx=s1) for p in range(2)]
            bet = [sb(f"bet{p}", [P, NT, R], ctx=s1) for p in range(2)]
            nw = sb("nw", [P, 1], ctx=s1)
            negoff = sb("negoff", [P, P], ctx=s1)
            ones = sb("ones", [P, 1], ctx=s1)
            npow = sb("npow", [P, 4], ctx=s1)
            nscale = sb("nscale", [P, 4], ctx=s1)
            cqk = sb("cqk", [P, 2, T], ctx=s1)
            sqk = [sb(f"sqk{i}", [P, 2, T], ctx=s1) for i in range(2)]
            sqq = [sb(f"sqq{i}", [P, 2, T], ctx=s1) for i in range(2)]
            cv = sb("cv", [P, R, T], ctx=s1)
            sv = [sb(f"sv{i}", [P, R, T], ctx=s1) for i in range(2)]
            nrm = [sb(f"nrm{i}", [P, 4], ctx=s1) for i in range(2)]
            rcn = [sb(f"rcn{i}", [P, 2], ctx=s1) for i in range(2)]
            cj = [sb(f"cj{i}", [P, NC, R], ctx=s1) for i in range(2)]
            vsc = [sb(f"vsc{p}", [P, B, 4], ctx=s1) for p in range(2)]
            E1 = sb("E1", [P, R, T], ctx=s1)
            E2 = sb("E2", [P, R, P], ctx=s1)
            BP = [sb(f"BP{p}", [P, B, R, 2, T + P], ctx=s1) for p in range(2)]
            Dm = sb("Dm", [SLOTS, BLK, BLK], ctx=s1)
            Tn = sb("Tn", [SLOTS, BLK, BLK], ctx=s1)
            Tt = sb("Tt", [SLOTS, BLK, BLK], ctx=s1)
            tmp = sb("tmp", [SLOTS, 256], ctx=s1)
            T32 = sb("T32", [P, B, NC * R, P], ctx=s1)
            W32 = sb("W32", [P, B, NC * R, P], ctx=s1)
            zs = hT[:].rearrange("p k n -> p (k n)").rearrange("p (b c n) -> p b c n", b=B, c=NC)
            Vs = sb("Vs", [P, B, NC, R, DK], ctx=s1)
            MTs = sb("MTs", [P, NC, R, P], ctx=s1)
            xs = sb("xs", [P, 3, R, DK], ctx=s1)
            R2 = sb("R2", [P, R, DK], ctx=s1)
            Y = sb("Y", [P, NC, R, DK], ctx=s1)
            og = [sb(f"og{i}", [P, NC, R, DK], ctx=s1) for i in range(2)]
            ogn = sb("ogn", [P, NC, R, DK], ctx=s1)
            junk = sb("junk", [P, DK], ctx=s1)
            ss = sb("ss", [P, 4], ctx=s1)
            sse = sb("sse", [P, 4], ctx=s1)
            ro = sb("ro", [P, 4], ctx=s1)
            OTs = sb("OTs", [P, R, NC, P], ctx=s1)

            bQK, bG2, bV, bZ, bVT, bMT, bX, bO = bank
            bG1, bOT, bF = bQK, bVT, bMT
            NTS = 2 + 2 * (BLK - 1)

            def at(kh, b, per, k=0):
                return kh * (B * per) + (b * per + k)

            LEAD_QK, LEAD_GRAM, LEAD_VZ = 2 * B, 2 * B - 1, 3
            NG = NKH * B

            def shift(kh, b, n):
                dk, bb = divmod(b + n, B)
                return kh + dk, bb

            def exists(kh, b, n):
                return not isinstance(kh, int) or 0 <= B * kh + b + n < NG

            PARTS = ((0, hh), (1, hh), (0, hl))

            def pe_qk(kh, p, b, t, lead=False):
                if t == 0:
                    if b == 0:
                        wait(nc.tensor, "wqk_split", kh + 1)
                    if lead:
                        wait(nc.tensor, "conv_qk", at(kh, b, 6))
                    else:
                        wait(nc.tensor, "bp", at(kh, b, 4))
                for k in range(KC):
                    for n, (w, h) in enumerate(PARTS):
                        last = nc.tensor.matmul(bQK[:, t * T:(t + 1) * T], wqk[p][w][:, k, t * DK:(t + 1) * DK],
                                                h[:, k, b * T:(b + 1) * T], start=(k + n == 0), stop=(k == KC - 1 and n == 2))
                if t == 1:
                    last.then_inc(sem("qk_mm"), 1)

            def pe_gram0(kh, p, b, g1=bG1):
                i = b % 2
                wait(nc.tensor, "silu_qk", at(kh, b, 1, 1))
                wait(nc.tensor, "square_qk", at(kh, b, 1, 1))
                wait(nc.tensor, "bp", at(kh, b, 4))
                nc.tensor.matmul(g1[:], sqk[i][:, 1, 0:P], sqk[i][:].rearrange("p x t -> p (x t)"), start=True, stop=True)

            def pe_gram1(kh, p, b):
                i = b % 2
                nc.tensor.matmul(bG2[:, 0:2 * P].rearrange("p (x t) -> p x t", x=2), sqk[i][:, 1, P:T], sqk[i][:, :, P:T],
                                 start=True, stop=True)
                for q in range(2):
                    for c in range(NC):
                        last = nc.tensor.matmul(bG2[:, 256 + 2 * q + c:257 + 2 * q + c], sqq[i][:, q, c * P:(c + 1) * P],
                                                ones[:, 0:1], start=True, stop=True)
                last.then_inc(sem("gram"), 1)

            def pe_v(kh, p, b, t):
                if t == 0:
                    if b == 0:
                        wait(nc.tensor, "wvz_split", kh + 1)
                    wait(nc.tensor, "conv_v", at(kh, b, 6))
                for k in range(KC):
                    for n, (w, h) in enumerate(PARTS):
                        last = nc.tensor.matmul(bV[:, t * T:(t + 1) * T], wvz[p][w][:, k, t * DK:(t + 1) * DK],
                                                h[:, k, b * T:(b + 1) * T], start=(k + n == 0), stop=(k == KC - 1 and n == 2))
                if t == 1:
                    last.then_inc(sem("v_mm"), 1)

            def pe_z(kh, p, b, c):
                if c == 0:
                    wait(nc.tensor, "silu_z", at(kh, b, 1))
                for k in range(KC):
                    for n, (w, h) in enumerate(PARTS):
                        last = nc.tensor.matmul(bZ[:, c * 256:(c + 1) * 256], h[:, k, b * T + c * P:b * T + (c + 1) * P],
                                                wvz[p][w][:, k, R * DK:2 * R * DK], start=(k + n == 0), stop=(k == KC - 1 and n == 2))
                if c == 1:
                    last.then_inc(sem("z_mm"), 1)

            def pe_vt(kh, p, b):
                wait(nc.tensor, "silu_v", at(kh, b, 1, 1))
                wait(nc.tensor, "vs", at(kh, b, 2))
                wait(nc.tensor, "ots", at(kh, b, 1, -3))
                for c in range(NC):
                    for h in range(R):
                        n = c * R + h
                        last = nc.tensor.transpose(bVT[:, n * P:(n + 1) * P], sv[b % 2][:, h, c * P:(c + 1) * P], ident)
                last.then_inc(sem("vt"), 1)

            def block_of(p, b, h, x, c, i):
                o = i * P if c == 0 else T
                return BP[p][:, b, h, x, o:o + P]

            def pe_mt(kh, p, b):
                wait(nc.tensor, f"t_in0{b}", (kh + 1) * 64)
                wait(nc.tensor, "acc", at(kh, b, 1, -1))
                for c in range(NC):
                    for h in range(R):
                        last = nc.tensor.matmul(bMT[:, (c * R + h) * P:(c * R + h + 1) * P], T32[:, b, c * R + h, :],
                                                block_of(p, b, h, 1, c, c), start=True, stop=True)
                last.then_inc(sem("mt"), 1)

            def pe_half(kh, b, n):
                if n == 0:
                    wait(nc.tensor, "y", at(kh, b, 2))
                return bX[:, (n + b) % 2 * 256:(n + b) % 2 * 256 + 256]

            def reader(kh, b, n):
                if n in (3, 8):
                    return "y", at(kh, b, 2, 1 if n == 3 else 2)
                return "x_add", at(kh, b, 7, n + 1 if n < 3 else n)

            def pe_product(kh, p, b, n):
                half = pe_half(kh, b, n)
                c = 0 if n < 4 else 1
                if n == 3:
                    wait(nc.tensor, f"t_in1{b}", (kh + 1) * 64)
                if n == 0:
                    wait(nc.tensor, "mt_evac", at(kh, b, 1, 1))
                    wait(nc.tensor, "vs", at(kh, b, 2, 2))
                else:
                    wait(nc.tensor, *reader(kh, b, n - 1))
                for h in range(R):
                    if n in (3, 8):
                        lhs, rhs = W32[:, b, c * R + h, :], xs[:, 2, h, :]
                    elif n == 4:
                        lhs, rhs = block_of(p, b, h, 1, 0, 1), Y[:, 0, h, :]
                    else:
                        r = n if c == 0 else n - 5
                        lhs = MTs[:, c, h, :]
                        rhs = xs[:, r - 1, h, :] if r else (Vs[:, b, 0, h, :] if c == 0 else R2[:, h, :])
                    last = nc.tensor.matmul(half[:, h * P:(h + 1) * P], lhs, rhs, start=True, stop=True)
                last.then_inc(sem("x_mm"), 1)

            def pe_o(kh, p, b, c):
                if c == 0:
                    wait(nc.tensor, "y", at(kh, b, 2, 1))
                    wait(nc.tensor, "og", at(kh, b, 2))
                else:
                    wait(nc.tensor, "y", at(kh, b, 2, 2))
                for h in range(R):
                    o = bO[:, (c * R + h) * P:(c * R + h + 1) * P]
                    last = nc.tensor.matmul(o, block_of(p, b, h, 0, 0, c), Y[:, 0, h, :], start=True, stop=(c == 0))
                    if c == 1:
                        last = nc.tensor.matmul(o, block_of(p, b, h, 0, 1, 1), Y[:, 1, h, :], start=False, stop=True)
                last.then_inc(sem("o"), 1)

            def pe_ot(kh, p, b):
                wait(nc.tensor, "ogn", at(kh, b, 4, 4))
                v = at(kh, b, 2, 8)
                wait(nc.tensor, "vs", min(v, 2 * NG) if isinstance(v, int) else v)
                for h in range(R):
                    for c in range(NC):
                        n = h * NC + c
                        last = nc.tensor.transpose(bOT[:, n * P:(n + 1) * P], ogn[:, c, h, :], ident)
                last.then_inc(sem("ot"), 1)

            def pe_f(kh, p, b, c):
                if c == 0:
                    wait(nc.tensor, "ots", at(kh, b, 1, 1))
                    v = at(kh, b, 1, 2)
                    wait(nc.tensor, "mt_evac", min(v, NG) if isinstance(v, int) else v)
                    if b == 0:
                        wait(nc.tensor, "wo_scaled", kh + 1)
                for h in range(R):
                    last = nc.tensor.matmul(bF[:, c * D:(c + 1) * D], OTs[:, h, c, :], wo[p][:, h, :],
                                            start=(h == 0), stop=(h == R - 1))
                if c == 1:
                    last.then_inc(sem("f"), 1)

            def beside(kh, p, b, n):
                k2, b2 = shift(kh, b, n)
                return (k2, (p + (b + n) // B) % 2, b2) if exists(kh, b, n) else None

            def pe_step(kh, p, b):
                qk, gram, vz, vt, last = (beside(kh, p, b, n) for n in (LEAD_QK, LEAD_GRAM, LEAD_VZ, LEAD_VZ - 1, -1))
                pe_mt(kh, p, b)
                if gram:
                    pe_gram0(*gram)
                    pe_gram1(*gram)
                pe_product(kh, p, b, 0)
                if vt:
                    pe_vt(*vt)
                pe_product(kh, p, b, 1)
                if vz:
                    pe_v(*vz, 0)
                pe_product(kh, p, b, 2)
                if vz:
                    pe_v(*vz, 1)
                pe_product(kh, p, b, 3)
                if qk:
                    pe_qk(*qk, 0)
                pe_product(kh, p, b, 4)
                if qk:
                    pe_qk(*qk, 1)
                pe_o(kh, p, b, 0)
                if last:
                    pe_ot(*last)
                pe_product(kh, p, b, 5)
                if last:
                    pe_f(*last, 0)
                pe_product(kh, p, b, 6)
                if last:
                    pe_f(*last, 1)
                pe_product(kh, p, b, 7)
                if vz:
                    pe_z(*vz, 0)
                pe_product(kh, p, b, 8)
                if vz:
                    pe_z(*vz, 1)
                pe_o(kh, p, b, 1)

            def act_tap0(kh, p, b, name, bk, dst, first):
                wait(nc.scalar, name + "_mm", at(kh, b, 1, 1))
                wait(nc.scalar, "silu_" + name, at(kh, b, 1))
                for t in range(2):
                    nc.scalar.activation(dst[:, t, :], bk[:, t * T:(t + 1) * T], ACT.Copy,
                                         scale=cw[p][:, first + t, TAPS - 1:TAPS]).then_inc(sem("tap0_" + name), 1)

            def act_silu_qk(kh, p, b):
                wait(nc.scalar, "conv_qk", at(kh, b, 6, 6))
                wait(nc.scalar, "gram", at(kh, b, 1, -1))
                wait(nc.scalar, "square_qk", at(kh, b, 1))
                nc.scalar.activation(sqk[b % 2][:], cqk[:], ACT.Silu).then_inc(sem("silu_qk"), 1)
                wait(nc.scalar, "silu_qk", at(kh, b, 1, 1))
                nc.scalar.activation(sqq[b % 2][:], sqk[b % 2][:], ACT.Square).then_inc(sem("square_qk"), 1)

            def act_silu_z(kh, p, b):
                wait(nc.scalar, "z_mm", at(kh, b, 1, 1))
                nc.scalar.activation(zs[:, b].rearrange("p c n -> p (c n)"), bZ[:], ACT.Silu).then_inc(sem("silu_z"), 1)

            def act_silu_v(kh, p, b):
                wait(nc.scalar, "conv_v", at(kh, b, 6, 6))
                wait(nc.scalar, "vt", at(kh, b, 1, -1))
                nc.scalar.activation(sv[b % 2][:], cv[:], ACT.Silu).then_inc(sem("silu_v"), 1)

            def act_vs(kh, p, b):
                wait(nc.scalar, "vt", at(kh, b, 1, 1))
                wait(nc.scalar, "vsc", at(kh, b, 1, 1))
                for c in range(NC):
                    nc.scalar.activation(Vs[:, b, c], bVT[:, c * 256:(c + 1) * 256].rearrange("p (h d) -> p h d", h=R), ACT.Copy,
                                         scale=vsc[p][:, b, 2 + c:3 + c]).then_inc(sem("vs"), 1)

            def act_y(kh, p, b, c):
                n = 3 if c == 0 else 8
                wait(nc.scalar, "x_mm", at(kh, b, 9, n + 1))
                if c == 0:
                    wait(nc.scalar, "o", at(kh, b, 2))
                nc.scalar.activation(Y[:, c], bX[:, (n + b) % 2 * 256:(n + b) % 2 * 256 + 256].rearrange("p (h d) -> p h d", h=R),
                                     ACT.Copy).then_inc(sem("y"), 1)

            def act_ss(kh, p, b):
                wait(nc.scalar, "ro", at(kh, b, 2, -1))
                for c in range(NC):
                    wait(nc.scalar, "og", at(kh, b, 2, c + 1))
                    for h in range(R):
                        n = c * R + h
                        wait(nc.scalar, "ss", at(kh, b, 4, n))
                        nc.scalar.activation(junk[:], og[b % 2][:, c, h, :], ACT.Square, accum_out=ss[:, n:n + 1]).then_inc(sem("ss"), 1)

            def act_ogn(kh, p, b):
                wait(nc.scalar, "ro", at(kh, b, 2, 2))
                wait(nc.scalar, "ot", at(kh, b, 1))
                for c in range(NC):
                    for h in range(R):
                        n = c * R + h
                        nc.scalar.activation(ogn[:, c, h, :], og[b % 2][:, c, h, :], ACT.Copy, scale=ro[:, n:n + 1]).then_inc(sem("ogn"), 1)

            def act_split_qk(kh, p):
                wait(nc.scalar, f"qk_in{p}", (kh - p) * 24 + 48)
                wait(nc.scalar, "qk_mm", at(kh - 1, 0, 1))
                nc.scalar.activation(wqk[p][0][:], rqk[:], ACT.Copy).then_inc(sem("wqk_high"), 1)

            def act_split_vz(kh, p):
                wait(nc.scalar, f"vz_in{p}", (kh - p) * 16 + 32)
                wait(nc.scalar, "z_mm", at(kh - 1, 0, 1))
                nc.scalar.activation(wvz[p][0][:], rvz[:], ACT.Copy).then_inc(sem("wvz_high"), 1)

            def act_turn(kh):
                wait(nc.scalar, "t_step", (kh + 1) * NTS)
                wait(nc.scalar, "t_out1", kh * 32)
                nc.scalar.activation(Tt[:], Tn[:].rearrange("s j i -> s i j"), ACT.Copy).then_inc(sem("t_turned"), 1)

            def act_ots(kh, p, b):
                wait(nc.scalar, "ot", at(kh, b, 1, 1))
                wait(nc.scalar, "f", at(kh, b, 1))
                nc.scalar.activation(OTs[:].rearrange("p h c t -> p (h c t)"), bOT[:], ACT.Copy).then_inc(sem("ots"), 1)

            def act_step(kh, p, b):
                qk, vz, vt, last = (beside(kh, p, b, n) for n in (LEAD_QK, LEAD_VZ, LEAD_VZ - 1, -1))
                if last:
                    act_ss(*last)
                if vt:
                    act_silu_z(*vt)
                    act_vs(*vt)
                if vz:
                    act_tap0(*vz, "v", bV, cv, 2)
                act_y(kh, p, b, 0)
                if last:
                    act_ogn(*last)
                if qk:
                    act_tap0(*qk, "qk", bQK, cqk, 0)
                if last:
                    act_ots(*last)
                if b == B - 1 and exists(kh, b, 1):
                    act_turn(kh + 1)
                if vz:
                    act_silu_v(*vz)
                splits(kh, p, b, act_split_qk, act_split_vz)
                act_y(kh, p, b, 1)
                if qk:
                    act_silu_qk(*qk)

            def dve_tap(kh, p, b, name, bk, dst, first, s):
                for t in range(2):
                    if s == 1:
                        wait(nc.vector, "tap0_" + name, at(kh, b, 2, 2))
                    else:
                        wait(nc.vector, "conv_" + name, at(kh, b, 6, 2 * (s - 2) + t + 1))
                    nc.vector.scalar_tensor_tensor(dst[:, t, s:T], bk[:, t * T:(t + 1) * T - s],
                                                   cw[p][:, first + t, TAPS - 1 - s:TAPS - s], dst[:, t, s:T],
                                                   ALU.mult, ALU.add).then_inc(sem("conv_" + name), 1)

            def dve_scan(kh, p, b, n):
                if b == 0 and n == 0:
                    wait(nc.vector, f"qk_in{p}", (kh - p) * 24 + 48)
                h = n % R
                wait(nc.vector, "bp", at(kh, b, 4))
                if n < R:
                    nc.vector.tensor_tensor_scan(E1[:, h, :], alb[p][:, h, b * T:(b + 1) * T], eye[:], 0.0,
                                                 ALU.mult, ALU.add).then_inc(sem("scan"), 1)
                else:
                    nc.vector.tensor_tensor_scan(E2[:, h, :], alb[p][:, h, b * T + P:(b + 1) * T], ident, 0.0,
                                                 ALU.mult, ALU.add).then_inc(sem("scan"), 1)

            def dve_split_qk(kh, p):
                wait(nc.vector, "wqk_high", kh + 1)
                nc.vector.tensor_tensor(wqk[p][1][:], rqk[:], wqk[p][0][:].bitcast(F32), ALU.subtract).then_inc(sem("wqk_split"), 1)

            def dve_split_vz(kh, p):
                wait(nc.vector, "wvz_high", kh + 1)
                nc.vector.tensor_tensor(wvz[p][1][:], rvz[:], wvz[p][0][:].bitcast(F32), ALU.subtract).then_inc(sem("wvz_split"), 1)

            def splits(kh, p, b, split_qk, split_vz):
                if b == 2 and exists(kh + 3, 0, 0):
                    split_qk(kh + 3, 1 - p)
                if b == 3 and exists(kh + 2, 0, 0):
                    split_vz(kh + 2, p)

            def dve_bet(kh, p):
                src = beta[:, :, kh * R:kh * R + R] if isinstance(kh, int) else beta[:, :, bass.ds(kh * R, R)]
                nc.vector.tensor_copy(bet[p][:], src).then_inc(sem("bet"), 1)

            def dve_wo(kh, p):
                wait(nc.vector, "wo_in", (kh + 1) * 16)
                nc.vector.tensor_scalar(wo[p][:], wo[p][:], nw[:, 0:1], None, ALU.mult).then_inc(sem("wo_scaled"), 1)

            def dve_scales(kh, p, b):
                i = b % 2
                wait(nc.vector, "gram", at(kh, b, 1, 1))
                wait(nc.vector, "vsc", at(kh, b, 1, -1))
                nc.vector.scalar_tensor_tensor(nrm[i][:], bG2[:, 256:260], 1e-6, nscale[:], ALU.add, ALU.mult).then_inc(sem("nrm"), 1)
                wait(nc.vector, "nrm", at(kh, b, 1, 1))
                nc.vector.reciprocal(rcn[i][:], nrm[i][:, 2:4]).then_inc(sem("rcn"), 1)
                wait(nc.vector, "rcn", at(kh, b, 1, 1))
                wait(nc.vector, "bet", kh + 1)
                nc.vector.tensor_tensor(cj[i][:], bet[p][:, NC * b:NC * (b + 1), :], rcn[i][:].unsqueeze(2).broadcast_to([P, NC, R]),
                                        ALU.mult).then_inc(sem("cj"), 1)

            def dve_bp(kh, p, b, h, g1=bG1):
                i = b % 2
                if h == 0:
                    wait(nc.vector, "cj", at(kh, b, 1, 1))
                    wait(nc.vector, "scan", at(kh, b, 4, 4))
                nc.vector.scalar_tensor_tensor(BP[p][:, b, h, :, 0:T], g1[:].rearrange("p (x t) -> p x t", x=2), cj[i][:, 0, h:h + 1],
                                               E1[:, h, :].unsqueeze(1).broadcast_to([P, 2, T]), ALU.mult, ALU.mult).then_inc(sem("bp"), 1)
                nc.vector.scalar_tensor_tensor(BP[p][:, b, h, :, T:T + P], bG2[:, 0:2 * P].rearrange("p (x t) -> p x t", x=2), cj[i][:, 1, h:h + 1],
                                               E2[:, h, :].unsqueeze(1).broadcast_to([P, 2, P]), ALU.mult, ALU.mult).then_inc(sem("bp"), 1)

            def dve_mt(kh, p, b):
                wait(nc.vector, "mt", at(kh, b, 1, 1))
                nc.vector.tensor_tensor(MTs[:].rearrange("p c h t -> p (c h) t"), bMT[:].rearrange("p (n t) -> p n t", t=P),
                                        negoff[:].unsqueeze(1).broadcast_to([P, NC * R, P]), ALU.mult).then_inc(sem("mt_evac"), 1)

            def dve_x(kh, p, b, n):
                wait(nc.vector, "x_mm", at(kh, b, 9, n + 1))
                half = bX[:, (n + b) % 2 * 256:(n + b) % 2 * 256 + 256].rearrange("p (h d) -> p h d", h=R)
                if n == 4:
                    wait(nc.vector, "x_add", at(kh, b, 7, 3))
                    nc.vector.tensor_tensor(R2[:], Vs[:, b, 1], half, ALU.subtract).then_inc(sem("x_add"), 1)
                else:
                    rhs = Vs[:, b, 0] if n < 4 else R2[:]
                    if n == 5:
                        wait(nc.vector, "x_add", at(kh, b, 7, 4))
                    nc.vector.tensor_tensor(xs[:, n if n < 4 else n - 5], rhs, half, ALU.add).then_inc(sem("x_add"), 1)

            def dve_og(kh, p, b):
                for c in range(NC):
                    wait(nc.vector, "o", at(kh, b, 2, 2))
                    wait(nc.vector, "silu_z", at(kh, b, 1, 1))
                    if c == 0:
                        wait(nc.vector, "ogn", at(kh, b, 4, -4))
                    nc.vector.scalar_tensor_tensor(og[b % 2][:, c].rearrange("p h d -> p (h d)"), bO[:, c * 256:(c + 1) * 256],
                                                   vsc[p][:, b, c:c + 1], zs[:, b, c, :], ALU.mult, ALU.mult).then_inc(sem("og"), 1)

            def dve_acc(kh, p, b):
                wait(nc.vector, "f", at(kh, b, 1, 1))
                a = acc[:, NC * b:NC * (b + 1), :].rearrange("p c d -> p (c d)")
                wait(nc.vector, "acc", at(kh, b, 1, 1 - B))
                nc.vector.tensor_tensor(a, a, bF[:], ALU.add).then_inc(sem("acc"), 1)

            def dve_step(kh, p, b):
                qk, gram, vz, last = (beside(kh, p, b, n) for n in (LEAD_QK, LEAD_GRAM, LEAD_VZ, -1))

                def taps_qk(n):
                    if qk:
                        dve_tap(*qk, "qk", bQK, cqk, 0, n)

                def taps_v(n):
                    if vz:
                        dve_tap(*vz, "v", bV, cv, 2, n)

                if last:
                    dve_og(*last)
                dve_mt(kh, p, b)
                if b == 0:
                    dve_wo(kh, p)
                if gram and gram[2] == 0:
                    dve_bet(gram[0], gram[1])
                dve_x(kh, p, b, 0)
                if gram:
                    dve_scales(*gram)
                dve_x(kh, p, b, 1)
                if gram:
                    dve_bp(*gram, 0)
                dve_x(kh, p, b, 2)
                if gram:
                    dve_bp(*gram, 1)
                taps_v(1)
                dve_x(kh, p, b, 4)
                taps_v(2)
                taps_qk(1)
                dve_x(kh, p, b, 5)
                taps_v(3)
                dve_x(kh, p, b, 6)
                taps_qk(2)
                dve_x(kh, p, b, 7)
                taps_qk(3)
                if last:
                    dve_acc(*last)
                if qk:
                    for n in range(2 * R):
                        dve_scan(*qk, n)
                splits(kh, p, b, dve_split_qk, dve_split_vz)

            def pool_vsc(kh, p, b):
                wait(nc.gpsimd, "nrm", at(kh, b, 1, 1))
                wait(nc.gpsimd, "og", at(kh - 2, b, 2, 2))
                nc.gpsimd.tensor_tensor(vsc[p][:, b, :], nrm[b % 2][:], npow[:], ALU.pow).then_inc(sem("vsc"), 1)

            def pool_ro(kh, p, b):
                wait(nc.gpsimd, "ss", at(kh, b, 4, 4))
                wait(nc.gpsimd, "ro", at(kh, b, 2))
                nc.gpsimd.tensor_scalar(sse[:], ss[:], 1.0 / DK, 1e-6, ALU.mult, ALU.add).then_inc(sem("ro"), 1)
                wait(nc.gpsimd, "ro", at(kh, b, 2, 1))
                wait(nc.gpsimd, "ogn", at(kh, b, 4))
                nc.gpsimd.tensor_tensor(ro[:], sse[:], mhalf[:, 0:4], ALU.pow).then_inc(sem("ro"), 1)

            SPLIT = {0: (0, 3), 1: (3, 16), 2: (16, 25), 3: (25, BLK - 1)}

            def pool_step_done(ins, value):
                ins.then_inc(sem("t_step"), 1)
                wait(nc.gpsimd, "t_step", value)

            def pool_inverse_start(kh):
                wait(nc.gpsimd, "t_out0", kh * 32)
                wait(nc.gpsimd, "t_turned", kh)
                pool_step_done(nc.gpsimd.memset(Tn[:], 0.0), kh * NTS + 1)
                pool_step_done(nc.gpsimd.affine_select(out=Tn[:], in_=Tn[:], compare_op=ALU.not_equal, fill=1.0, base=0,
                                                       pattern=[[1, BLK], [-1, BLK]], channel_multiplier=0), kh * NTS + 2)

            def pool_inverse(kh, lo, hi):
                if lo == 0:
                    wait(nc.gpsimd, "blk_in", (kh + 1) * 16)
                for j in range(lo, hi):
                    r, c = BLK - 1 - j, j + 1
                    t = tmp[:, 0:r * c].rearrange("p (i c) -> p i c", c=c)
                    pool_step_done(nc.gpsimd.tensor_tensor(t, Dm[:, j, j + 1:BLK].unsqueeze(2).broadcast_to([SLOTS, r, c]),
                                                           Tn[:, j, 0:c].unsqueeze(1).broadcast_to([SLOTS, r, c]), ALU.mult),
                                   kh * NTS + 2 * j + 3)
                    pool_step_done(nc.gpsimd.tensor_tensor(Tn[:, j + 1:BLK, 0:c], Tn[:, j + 1:BLK, 0:c], t, ALU.subtract),
                                   kh * NTS + 2 * j + 4)
                    if kh == 0 and j % 8 == 7:
                        pool_vsc(1, 1, j // 8)

            def pool_step(kh, p, b):
                last, gram = beside(kh, p, b, -1), beside(kh, p, b, LEAD_GRAM)
                if last:
                    pool_ro(*last)
                if gram:
                    pool_vsc(*gram)
                if kh + 1 < NKH:
                    if b == 0:
                        pool_inverse_start(kh + 1)
                    pool_inverse(kh + 1, *SPLIT[b])

            def sp_load_qk(kh):
                p = kh % 2
                wait(nc.sync, "wqk_split", kh)
                wait(nc.sync, "conv_qk", at(kh - 1, 0, 6))
                wait(nc.sync, "scan", at(kh - 1, 0, 4))
                nc.sync.dma_start(rqk[:], wqkvz_d[:, kh * CW:kh * CW + 2 * DK].rearrange("(k p) n -> p k n", p=P)).then_inc(sem(f"qk_in{p}"), 16)
                nc.sync.dma_start(cw[p][:, 0:2, :], convw_d[0:2 * NKH * P].rearrange("(x g p) s -> p x g s", x=2, p=P)[:, :, kh, :])\
                    .then_inc(sem(f"qk_in{p}"), 16)
                nc.sync.dma_start(alb[p].rearrange("p r t -> p (r t)"),
                                  alpha_dr[kh * R:(kh + 1) * R, :].rearrange("(o r) t -> o (r t)", o=1).broadcast_to([P, R * B * T]))\
                    .then_inc(sem(f"qk_in{p}"), 16)

            def sp_load_vz(kh):
                p = kh % 2
                wait(nc.sync, "wvz_split", kh)
                wait(nc.sync, "conv_v", at(kh - 1, 0, 6))
                nc.sync.dma_start(rvz[:], wqkvz_d[:, kh * CW + 2 * DK:(kh + 1) * CW].rearrange("(k p) n -> p k n", p=P)).then_inc(sem(f"vz_in{p}"), 16)
                nc.sync.dma_start(cw[p][:, 2:4, :], convw_d.rearrange("(g p) s -> p g s", p=P)[:, 2 * NKH + kh * R:2 * NKH + (kh + 1) * R, :])\
                    .then_inc(sem(f"vz_in{p}"), 16)

            def sp_load_wo(kh):
                wait(nc.sync, "f", at(kh - 1, 0, 1))
                nc.sync.dma_start(wo[kh % 2][:], wout_d[kh * R * DK:(kh + 1) * R * DK, :].rearrange("(h p) n -> p h n", p=DK)).then_inc(sem("wo_in"), 16)

            def sp_blocks_in(kh):
                wait(nc.sync, "bp", at(kh, B - 1, 4, 4))
                for n in range(NBLK):
                    r = slice(n * BLK, (n + 1) * BLK)
                    for c in range(NC):
                        i = (T if c else 0) + n * BLK
                        nc.sync.dma_start(blkin_dr[c, n].rearrange("u j i -> j u i"),
                                          BP[kh % 2][r, :, :, 1, i:i + BLK].rearrange("j b h i -> j (b h) i")).then_inc(sem("blk_dr"), 16)
                wait(nc.sync, "blk_dr", (kh + 1) * 16 * NC * NBLK)
                nc.sync.dma_start(Dm[:].rearrange("s j i -> s (j i)"), blkin_dr.rearrange("c n u j i -> (c n u) (j i)")).then_inc(sem("blk_in"), 16)

            def sp_blocks_out(kh):
                wait(nc.sync, "t_step", (kh + 1) * NTS)
                for i, (dr, src) in enumerate(((tinv_dr, Tn), (ttin_dr, Tt))):
                    if i == 1:
                        wait(nc.sync, "t_turned", kh + 1)
                    for b in range(B):
                        wait(nc.sync, f"t_in{i}{b}", kh * 64)
                    for c in range(NC):
                        half = slice(c * SLOTS // NC, (c + 1) * SLOTS // NC)
                        nc.sync.dma_start(dr[:, :, c].rearrange("n b h j i -> (n b) h (j i)"), src[half].rearrange("s j i -> s (j i)"))\
                            .then_inc(sem(f"t_out{i}"), 16)
                for b in range(B):
                    wait(nc.sync, "y", at(kh - 1, b, 2, 2))
                    for i, (dst, dr) in enumerate(((T32, tinv_dr), (W32, ttin_dr))):
                        wait(nc.sync, f"t_out{i}", (kh + 1) * 32)
                        for n in range(NBLK):
                            r = slice(n * BLK, (n + 1) * BLK)
                            nc.sync.dma_start(dst[r, b, :, r], dr[n, b].rearrange("c h j i -> j (c h) i")).then_inc(sem(f"t_in{i}{b}"), 16)

            block = s1.enter_context(nc.Block())

            @block.sync
            def _(sp):
                sp.dma_start(nw[:], nw_d.rearrange("(p o) -> p o", o=1)).then_inc(sem("nw_in"), 16)
                sp_load_qk(0)
                sp_load_vz(0)
                sp_load_qk(1)
                sp_load_vz(1)
                sp_load_wo(0)
                sp.wait_ge(sem("zero"), 2)
                for kh in range(-1, NKH - 1):
                    sp_blocks_in(kh + 1)
                    if kh + 3 < NKH:
                        sp_load_qk(kh + 3)
                    if 0 <= kh and kh + 2 < NKH:
                        sp_load_vz(kh + 2)
                    if 0 <= kh:
                        sp_load_wo(kh + 1)
                    sp_blocks_out(kh + 1)
                sp.wait_ge(sem("scan"), 4 * NG)
                for b in range(B):
                    sp.dma_start(x[:, NC * b:NC * (b + 1), :], x_d[b].rearrange("(c p) d -> p c d", p=P)).then_inc(sem("x_in"), 16)

            LOOP = (1, NKH - 4)

            def steps(one, kh, p):
                for b in range(B):
                    one(kh, p, b)

            @block.tensor
            def _(pe):
                pe.wait_ge(sem("const1"), 1)
                for g in range(LEAD_QK):
                    kh, b = divmod(g, B)
                    for t in range(2):
                        pe_qk(kh, kh, b, t, lead=True)
                    if g:
                        gk, gb = divmod(g - 1, B)
                        pe_gram0(gk, gk, gb, bX)
                        pe_gram1(gk, gk, gb)
                    if 0 <= g - B < LEAD_VZ:
                        for t in range(2):
                            pe_v(0, 0, b, t)
                        for c in range(NC):
                            pe_z(0, 0, b, c)
                        if b:
                            pe_vt(0, 0, b - 1)
                steps(pe_step, 0, 0)
                with pe.Fori(*LOOP, 2) as kh:
                    steps(pe_step, kh, 1)
                    steps(pe_step, kh + 1, 0)
                for kh in range(NKH - 3, NKH):
                    steps(pe_step, kh, kh % 2)
                pe_ot(NKH - 1, 1, B - 1)
                for c in range(NC):
                    pe_f(NKH - 1, 1, B - 1, c)

            @block.scalar
            def _(act):
                act_split_qk(0, 0)
                act_split_vz(0, 0)
                for g in range(LEAD_QK):
                    kh, b = divmod(g, B)
                    if g == 2:
                        act_split_qk(1, 1)
                        act_split_vz(1, 1)
                    act_tap0(kh, kh, b, "qk", bQK, cqk, 0)
                    act_silu_qk(kh, kh, b)
                    if 0 <= g - B < LEAD_VZ:
                        act_tap0(0, 0, b, "v", bV, cv, 2)
                        if b:
                            act_silu_z(0, 0, b - 1)
                            act_vs(0, 0, b - 1)
                        act_silu_v(0, 0, b)
                act_split_qk(2, 0)
                act_turn(0)
                steps(act_step, 0, 0)
                with act.Fori(*LOOP, 2) as kh:
                    steps(act_step, kh, 1)
                    steps(act_step, kh + 1, 0)
                for kh in range(NKH - 3, NKH):
                    steps(act_step, kh, kh % 2)
                act_ss(NKH - 1, 1, B - 1)
                act_ogn(NKH - 1, 1, B - 1)
                act_ots(NKH - 1, 1, B - 1)

            @block.vector
            def _(dve):
                dve.wait_ge(sem("const1"), 1)
                dve.wait_ge(sem("nw_in"), 16)
                dve_split_qk(0, 0)
                dve_split_vz(0, 0)
                for g in range(LEAD_QK):
                    kh, b = divmod(g, B)
                    if g == 2:
                        dve_split_qk(1, 1)
                        dve_split_vz(1, 1)
                    if b == 0:
                        dve_bet(kh, kh)
                    for n in range(1, TAPS):
                        dve_tap(kh, kh, b, "qk", bQK, cqk, 0, n)
                    if g:
                        gk, gb = divmod(g - 1, B)
                        dve_scales(gk, gk, gb)
                        for h in range(R):
                            dve_bp(gk, gk, gb, h, bX)
                    for n in range(2 * R):
                        dve_scan(kh, kh, b, n)
                    if 0 <= g - B < LEAD_VZ:
                        for n in range(1, TAPS):
                            dve_tap(0, 0, b, "v", bV, cv, 2, n)
                dve_split_qk(2, 0)
                dve.wait_ge(sem("acc0"), 1)
                steps(dve_step, 0, 0)
                with dve.Fori(*LOOP, 2) as kh:
                    steps(dve_step, kh, 1)
                    steps(dve_step, kh + 1, 0)
                for kh in range(NKH - 3, NKH):
                    steps(dve_step, kh, kh % 2)
                dve_og(NKH - 1, 1, B - 1)
                dve_acc(NKH - 1, 1, B - 1)

            @block.gpsimd
            def _(pool):
                n = 0
                for t, v in ((negoff[:], -1.0), (ones[:], 1.0), (npow[:, 0:2], -0.5), (npow[:, 2:4], 0.5),
                             (nscale[:, 0:2], float(DK)), (nscale[:, 2:4], 1.0)):
                    nc.gpsimd.memset(t, v).then_inc(sem("const1a"), 1)
                    n += 1
                pool.wait_ge(sem("const1a"), n)
                for m in range(NBLK):
                    r = slice(m * BLK, (m + 1) * BLK)
                    nc.gpsimd.memset(negoff[r, r], 0.0).then_inc(sem("const1a"), 1)
                    n += 1
                pool.wait_ge(sem("const1a"), n)
                nc.gpsimd.memset(tmp[:], 0.0).then_inc(sem("const1"), 1)
                pool.wait_ge(sem("const1"), 1)
                for t in (T32, W32):
                    nc.gpsimd.memset(t[:].rearrange("p b u t -> p (b u t)"), 0.0).then_inc(sem("zero"), 1)
                nc.gpsimd.memset(acc[:].rearrange("p t d -> p (t d)"), 0.0).then_inc(sem("acc0"), 1)
                for b in range(B):
                    pool_vsc(0, 0, b)
                pool_inverse_start(0)
                pool_inverse(0, 0, BLK - 1)
                for kh in range(NKH):
                    for b in range(B):
                        pool_step(kh, kh % 2, b)
                pool_ro(NKH - 1, 1, B - 1)

        mid.close()
        gates = sb("gates", [P, 2, 2, B, D])

        def residual(ch, t_out, b, branch, layer, m, mark):
            g = gates[:, layer, m, b, :].unsqueeze(1).broadcast_to([P, NC, D])
            if b == 0:
                nc.vector.wait_ge(sem("gate_in0"), 16)
                if (layer, m) != (0, 0):
                    nc.vector.wait_ge(sem("gate_in1"), 48)
            wait(nc.vector, mark, b)
            ch.after(nc.vector.tensor_tensor(t_out, branch, g, ALU.mult))
            xv = x[:, NC * b:NC * (b + 1), :]
            nc.vector.tensor_tensor(xv, xv, t_out, ALU.add).then_inc(sem(mark), 1)

        with ExitStack() as s2:
            wraw = [sb(f"wraw{i}", [P, HT, D], I32, ctx=s2) for i in range(2)]
            draw = sb("draw", [P, KC, HID], I32, ctx=s2)
            wsc = sb("wsc", [P, 3, HT], ctx=s2)
            wnat = [sb(f"wnat{i}", [P, HT, D], ctx=s2) for i in range(2)]
            dnat = sb("dnat", [P, KC, HID], ctx=s2)
            wT = [sb(f"wT{i}", [P, KC, HT * P], ctx=s2) for i in range(2)]
            dT = sb("dT", [P, HT, D], ctx=s2)
            gsil = sb("gsil", [P, 2, 512], ctx=s2)
            hact = sb("hact", [P, HT, B * T], ctx=s2)
            rt = sb("rt2", [P, NC, D], ctx=s2)
            block = s2.enter_context(nc.Block())

            def rows(m):
                return P if m < HT - 1 else HREM

            @block.sync
            def _(sp):
                for n in range(4):
                    sp.dma_start(gates[:, n // 2, n % 2].rearrange("p b d -> p (b d)"),
                                 gates_dr[n:n + 1].rearrange("g b d -> g (b d)").broadcast_to([P, B * D])).then_inc(sem(f"gate_in{min(n, 1)}"), 16)
                for i, (w_d, s_d) in enumerate(((wg_d, sg_d), (wu_d, su_d))):
                    sp.dma_start(wraw[i][:, 0:HT - 1, :], w_d[0:(HT - 1) * P, :].rearrange("(m p) d -> p m d", p=P)).then_inc(sem("ffn_w_in"), 16)
                    sp.dma_start(wraw[i][0:HREM, HT - 1, :], w_d[(HT - 1) * P:HID, :]).then_inc(sem("ffn_w_in"), 16)
                    sp.dma_start(wsc[:, i, 0:HT - 1], s_d[0:(HT - 1) * P].rearrange("(m p) -> p m", p=P), allow_slow_non_contiguous=True).then_inc(sem("ffn_w_in"), 16)
                    sp.dma_start(wsc[0:HREM, i, HT - 1:HT], s_d[(HT - 1) * P:HID].rearrange("(p o) -> p o", o=1)).then_inc(sem("ffn_w_in"), 16)
                sp.dma_start(draw[:], wd_d.rearrange("(m p) d -> p m d", p=P)).then_inc(sem("ffn_w_in"), 16)
                sp.dma_start(wsc[:, 2, 0:KC], sd_d.rearrange("(m p) -> p m", p=P), allow_slow_non_contiguous=True).then_inc(sem("ffn_w_in"), 16)

            @block.gpsimd
            def _(pool):
                ln_pool(pool, 1)

            @block.vector
            def _(dve):
                ch = Chain(dve, "ffn_chain")
                dve.wait_ge(sem("x_in"), 2 * 16 * B)
                for b in range(B):
                    residual(ch, rt[:], b, acc[:, NC * b:NC * (b + 1), :], 0, 0, "res0a")
                ln_vector(dve, 1, lambda t: dve.wait_ge(sem("res0a"), t // NC + 1))
                dve.wait_ge(sem("ffn_w_in"), 160)
                for i in range(2):
                    for m in range(HT):
                        r = rows(m)
                        nc.vector.tensor_scalar(wnat[i][0:r, m, :], wraw[i][0:r, m, :], -128.0, wsc[0:r, i, m:m + 1],
                                                ALU.add, ALU.mult).then_inc(sem("deq"), 1)
                for m in range(KC):
                    nc.vector.tensor_scalar(dnat[:, m, :], draw[:, m, :], -128.0, wsc[:, 2, m:m + 1],
                                            ALU.add, ALU.mult).then_inc(sem("deq"), 1)
                for n in range(2 * HT):
                    th, m = divmod(n, HT)
                    r = rows(m)
                    dve.wait_ge(sem("up_mm"), n + 1)
                    dve.wait_ge(sem("gsil"), n + 1)
                    nc.vector.tensor_tensor(hact[0:r, m, th * 512:(th + 1) * 512], gsil[0:r, n % 2, :], bank[4 + n % 2][0:r, :],
                                            ALU.mult).then_inc(sem("hact"), 1)
                for b in range(B):
                    dve.wait_ge(sem("down_mm"), b + 1)
                    residual(ch, rt[:], b, bank[6 + b % 2][:].rearrange("p (c d) -> p c d", c=NC), 0, 1, "res0b")

            @block.scalar
            def _(act):
                ln_scalar(act, 1, 0, 3, 4)
                for n in range(3 * HT):
                    i, m = divmod(n, HT)
                    r = rows(m)
                    act.wait_ge(sem("wtr"), n + 1)
                    bk = bank[2 + n % 2]
                    if i < 2:
                        nc.scalar.activation(wT[i][:, :, m * P:m * P + r], bk[:, 0:2 * P].rearrange("p (k r) -> p k r", k=2)[:, :, 0:r],
                                             ACT.Copy).then_inc(sem("wT"), 1)
                    else:
                        nc.scalar.activation(dT[0:r, m, :], bk[0:r, 0:D], ACT.Copy).then_inc(sem("wT"), 1)
                for n in range(2 * HT):
                    th, m = divmod(n, HT)
                    r = rows(m)
                    act.wait_ge(sem("gate_mm2"), n + 1)
                    wait(act, "hact", n - 1)
                    nc.scalar.activation(gsil[0:r, n % 2, :], bank[2 + n % 2][0:r, :], ACT.Silu).then_inc(sem("gsil"), 1)

            @block.tensor
            def _(pe):
                ln_tensor(pe, 1)
                for n in range(3 * HT):
                    i, m = divmod(n, HT)
                    r = rows(m)
                    pe.wait_ge(sem("deq"), 2 * HT + KC if i == 2 else n + 1)
                    wait(pe, "wT", n - 1)
                    bk = bank[2 + n % 2]
                    for k in range(KC):
                        if i < 2:
                            last = nc.tensor.transpose(bk[:, k * P:k * P + r], wnat[i][0:r, m, k * P:(k + 1) * P], ident[0:r, 0:r])
                        else:
                            last = nc.tensor.transpose(bk[0:r, k * P:(k + 1) * P], dnat[:, k, m * P:m * P + r], ident)
                    last.then_inc(sem("wtr"), 1)
                pe.wait_ge(sem("ln_hT"), 2 * KC * B)
                pe.wait_ge(sem("wT"), 3 * HT)
                for n in range(2 * HT):
                    th, m = divmod(n, HT)
                    r = rows(m)
                    wait(pe, "gsil", n - 1)
                    for k in range(KC):
                        last = nc.tensor.matmul(bank[2 + n % 2][0:r, :], wT[0][:, k, m * P:m * P + r], hT[:, k, th * 512:(th + 1) * 512],
                                                start=(k == 0), stop=(k == KC - 1))
                    last.then_inc(sem("gate_mm2"), 1)
                    wait(pe, "hact", n - 1)
                    for k in range(KC):
                        last = nc.tensor.matmul(bank[4 + n % 2][0:r, :], wT[1][:, k, m * P:m * P + r], hT[:, k, th * 512:(th + 1) * 512],
                                                start=(k == 0), stop=(k == KC - 1))
                    last.then_inc(sem("up_mm"), 1)
                for b in range(B):
                    pe.wait_ge(sem("hact"), HT * (b // 2 + 1))
                    wait(pe, "res0b", b - 1)
                    for c in range(NC):
                        t = NC * b + c
                        for m in range(HT):
                            r = rows(m)
                            last = nc.tensor.matmul(bank[6 + b % 2][:, c * D:(c + 1) * D], hact[0:r, m, t * P:(t + 1) * P], dT[0:r, m, :],
                                                    start=(m == 0), stop=(m == HT - 1))
                    last.then_inc(sem("down_mm"), 1)

        with ExitStack() as s3:
            wn1 = sb("wn1", [P, 4, KC, D], ctx=s3)
            wrep = sb("wrep", [P, 2, KC, NH1, 2, HD], ctx=s3)
            wv = sb("wv", [P, KC, D], ctx=s3)
            won = sb("won", [P, KC, NH1, 32], ctx=s3)
            wpo = sb("wpo", [P, QT, D], ctx=s3)
            split = sb("split", [P, 2, 4], ctx=s3)
            low = sb("low", [P, 2], ctx=s3)
            qkr = [sb(f"qkr{i}", [P, 512], F32R, ctx=s3) for i in range(2)]
            qhl = sb("qhl", [P, QT, B * T], F32R, ctx=s3)
            khl = sb("khl", [P, QT, B * T], F32R, ctx=s3)
            klh = sb("klh", [P, QT, B * T], F32R, ctx=s3)
            v1 = sb("v1", [P, NT, NH1, 32], ctx=s3)
            NBUF = 4
            prob = sb("prob", [P, NBUF, 384], ctx=s3)
            probT = sb("probT", [P, NBUF, 384], ctx=s3)
            mx = sb("mx", [P, B, NH1, NC], ctx=s3)
            nmx = sb("nmx", [P, B, NH1, NC], ctx=s3)
            sums = sb("sums", [P, B, NH1, NC], ctx=s3)
            rsum = sb("rsum", [P, B, NH1, NC], ctx=s3)
            atT = sb("atT", [P, QT, T], ctx=s3)
            rt = sb("rt3", [P, NC, D], ctx=s3)
            block = s3.enter_context(nc.Block())
            NBH = B * NH1
            HS = float(HD) ** -0.5
            NQK = 2 * QT * 2
            LAG_T, LAG_PV, LAG_EVAC, LAG_O, LAG_RES = 3, 4, 5, 6, 7

            @block.sync
            def _(sp):
                for i, w_d in enumerate((wq1_d, wk1_d, wv1_d, wo1_d)):
                    sp.dma_start(wn1[:, i], w_d.rearrange("(m p) d -> p m d", p=P)).then_inc(sem("w1_in"), 16)

            @block.gpsimd
            def _(pool):
                nc.gpsimd.memset(split[:], -1.0).then_inc(sem("split"), 1)
                nc.gpsimd.memset(won[:].rearrange("p k h e -> p (k h e)"), 0.0).then_inc(sem("won0"), 1)
                ln_pool(pool, 2)
                pool.wait_ge(sem("split"), 1)
                n = 1
                for i, first in enumerate((HD, 0)):
                    for sign, base in ((1, -first), (-1, first + HD - 1)):
                        nc.gpsimd.affine_select(out=split[:, i], in_=split[:, i], compare_op=ALU.is_ge, fill=0.0, base=base,
                                                pattern=[[-32 * sign, 4]], channel_multiplier=sign).then_inc(sem("split"), 1)
                        n += 1
                        pool.wait_ge(sem("split"), n)
                nc.gpsimd.memset(v1[:].rearrange("p t h e -> p (t h e)"), 0.0).then_inc(sem("v10"), 1)
                pool.wait_ge(sem("w1_in"), 64)
                pool.wait_ge(sem("won0"), 1)
                for m in range(KC):
                    nc.gpsimd.tensor_copy(won[:, m, :, 0:HD], wn1[:, 3, m, :].rearrange("p (h e) -> p h e", e=HD)).then_inc(sem("won"), 1)
                for n in range(NBH):
                    b, h = divmod(n, NH1)
                    pool.wait_ge(sem("rsum"), n + 1)
                    pr = prob[:, n % NBUF, P:3 * P]
                    nc.gpsimd.tensor_scalar(pr, pr, rsum[:, b, h, 1:2], None, ALU.mult).then_inc(sem("prob1"), 1)

            @block.vector
            def _(dve):
                ln_vector(dve, 2, lambda t: None)
                dve.wait_ge(sem("split"), 5)
                nc.vector.tensor_reduce(low[:], split[:], AX.X, ALU.add).then_inc(sem("low"), 1)
                dve.wait_ge(sem("low"), 1)
                for n in range(NQK):
                    i, rest = divmod(n, QT * 2)
                    q, th = divmod(rest, 2)
                    dve.wait_ge(sem("qkr"), n + 1)
                    for j, dst in enumerate((qhl,) if i == 0 else (khl, klh)):
                        last = nc.vector.scalar_tensor_tensor(dst[:, q, th * 512:(th + 1) * 512], qkr[n % 2][:].bitcast(F32),
                                                              low[:, j:j + 1], bank[2 + n % 2][:], ALU.mult, ALU.add)
                    last.then_inc(sem("qk1"), 1)
                ch = Chain(dve, "att_chain")
                for n in range(NBH + LAG_RES - 1):
                    if n < NBH:
                        b, h = divmod(n, NH1)
                        dve.wait_ge(sem("s_mm"), n + 1)
                        s = bank[n % 3]
                        nc.vector.reduce_max(mx[:, b, h, 0:1], s[:, 0:P], AX.X).then_inc(sem("mx"), 1)
                        nc.vector.reduce_max(mx[:, b, h, 1:2], s[:, P:3 * P], AX.X).then_inc(sem("mx"), 1)
                        dve.wait_ge(sem("mx"), 2 * (n + 1))
                        nc.vector.tensor_scalar(nmx[:, b, h, :], mx[:, b, h, :], -HS, None, ALU.mult).then_inc(sem("nmx"), 1)
                    if 1 <= n <= NBH:
                        b, h = divmod(n - 1, NH1)
                        dve.wait_ge(sem("expo"), 2 * n)
                        nc.vector.reciprocal(rsum[:, b, h], sums[:, b, h]).then_inc(sem("rsum"), 1)
                    m = n - LAG_T
                    if 0 <= m < NBH:
                        dve.wait_ge(sem("pt_mm"), m + 1)
                        wait(dve, "pv", m - NBUF + 1)
                        nc.vector.tensor_copy(probT[:, m % NBUF, :], bank[3 + m % 2][:, 0:384]).then_inc(sem("pt"), 1)
                    if n >= LAG_RES and (n - LAG_RES) % NH1 == NH1 - 1:
                        b = (n - LAG_RES) // NH1
                        dve.wait_ge(sem("o1_mm"), b + 1)
                        residual(ch, rt[:], b, bank[7][:].rearrange("p (c d) -> p c d", c=NC), 1, 0, "res1a")
                b = B - 1
                dve.wait_ge(sem("o1_mm"), B)
                residual(ch, rt[:], b, bank[7][:].rearrange("p (c d) -> p c d", c=NC), 1, 0, "res1a")

            @block.scalar
            def _(act):
                ln_scalar(act, 2, 1, 0, 1)
                for n in range(2 * KC + KC + QT):
                    act.wait_ge(sem("w1tr"), n + 1)
                    src = bank[2 + n % 2][:, 0:D]
                    if n < 2 * KC:
                        for half in range(2):
                            last = nc.scalar.activation(wrep[:, n // KC, n % KC, :, half, :], src.rearrange("p (h e) -> p h e", e=HD), ACT.Copy)
                    elif n < 3 * KC:
                        last = nc.scalar.activation(wv[:, n % KC, :], src, ACT.Copy)
                    else:
                        last = nc.scalar.activation(wpo[:, n - 3 * KC, :], src, ACT.Copy)
                    last.then_inc(sem("w1T"), 1)
                for n in range(NQK):
                    act.wait_ge(sem("qk1_mm"), n + 1)
                    wait(act, "qk1", n - 1)
                    nc.scalar.activation(qkr[n % 2][:], bank[2 + n % 2][:], ACT.Copy).then_inc(sem("qkr"), 1)
                act.wait_ge(sem("v10"), 1)
                for b in range(B):
                    act.wait_ge(sem("v1_mm"), b + 1)
                    for c in range(NC):
                        last = nc.scalar.activation(v1[:, NC * b + c, :, 0:HD],
                                                    bank[4 + b % 2][:, c * D:(c + 1) * D].rearrange("p (h e) -> p h e", e=HD), ACT.Copy)
                    last.then_inc(sem("v1"), 1)
                for n in range(NBH + LAG_EVAC - 1):
                    if n < NBH:
                        b, h = divmod(n, NH1)
                        act.wait_ge(sem("nmx"), n + 1)
                        wait(act, "pt_mm", n - NBUF + 1)
                        s = bank[n % 3]
                        for c in range(NC):
                            lo, hi = (0, P) if c == 0 else (P, 3 * P)
                            nc.scalar.activation(prob[:, n % NBUF, lo:hi], s[:, lo:hi], ACT.Exp, bias=nmx[:, b, h, c:c + 1],
                                                 scale=HS, accum_out=sums[:, b, h, c:c + 1]).then_inc(sem("expo"), 1)
                    if 1 <= n <= NBH:
                        b, h = divmod(n - 1, NH1)
                        act.wait_ge(sem("rsum"), n)
                        pr = prob[:, (n - 1) % NBUF, 0:P]
                        nc.scalar.activation(pr, pr, ACT.Copy, scale=rsum[:, b, h, 0:1]).then_inc(sem("prob0"), 1)
                    m = n - LAG_EVAC
                    if m >= 0 and m % 8 == 7:
                        b, half = divmod(m // 8, 2)
                        act.wait_ge(sem("pv"), m + 1)
                        if half == 0:
                            wait(act, "o1_mm", b)
                        nc.scalar.activation(atT[:, 2 * half:2 * half + 2, :].rearrange("p q t -> p (q t)"), bank[5 + half][:], ACT.Copy)\
                            .then_inc(sem("atT"), 1)
                act.wait_ge(sem("pv"), NBH)
                nc.scalar.activation(atT[:, 2:4, :].rearrange("p q t -> p (q t)"), bank[6][:], ACT.Copy).then_inc(sem("atT"), 1)

            @block.tensor
            def _(pe):
                ln_tensor(pe, 2)
                pe.wait_ge(sem("w1_in"), 64)
                for n in range(2 * KC + KC + QT):
                    wait(pe, "w1T", n - 1)
                    if n == 3 * KC:
                        pe.wait_ge(sem("won"), KC)
                    for m in range(KC):
                        src = wn1[:, n // KC, m, (n % KC) * P:(n % KC + 1) * P] if n < 3 * KC else \
                            won[:, m, 4 * (n - 3 * KC):4 * (n - 3 * KC + 1), :].rearrange("p h e -> p (h e)")
                        last = nc.tensor.transpose(bank[2 + n % 2][:, m * P:(m + 1) * P], src, ident)
                    last.then_inc(sem("w1tr"), 1)
                pe.wait_ge(sem("w1T"), 3 * KC + QT)
                pe.wait_ge(sem("ln_hT"), 3 * KC * B)
                for n in range(NQK):
                    i, rest = divmod(n, QT * 2)
                    q, th = divmod(rest, 2)
                    wait(pe, "qk1", n - 1)
                    for k in range(KC):
                        last = nc.tensor.matmul(bank[2 + n % 2][:], wrep[:, i, k, 4 * q:4 * q + 4].rearrange("p h x e -> p (h x e)"),
                                                hT[:, k, th * 512:(th + 1) * 512], start=(k == 0), stop=(k == KC - 1))
                    last.then_inc(sem("qk1_mm"), 1)
                for b in range(B):
                    wait(pe, "v1", b - 1)
                    for c in range(NC):
                        t = NC * b + c
                        for k in range(KC):
                            last = nc.tensor.matmul(bank[4 + b % 2][:, c * D:(c + 1) * D], hT[:, k, t * P:(t + 1) * P], wv[:, k, :],
                                                    start=(k == 0), stop=(k == KC - 1))
                    last.then_inc(sem("v1_mm"), 1)
                pe.wait_ge(sem("qk1"), NQK)
                pe.wait_ge(sem("v1"), B)

                def project(b):
                    pe.wait_ge(sem("atT"), 2 * (b + 1))
                    wait(pe, "res1a", b)
                    for c in range(NC):
                        for q in range(QT):
                            last = nc.tensor.matmul(bank[7][:, c * D:(c + 1) * D], atT[:, q, c * P:(c + 1) * P], wpo[:, q, :],
                                                    start=(q == 0), stop=(q == QT - 1))
                    last.then_inc(sem("o1_mm"), 1)

                for n in range(NBH + LAG_O - 1):
                    if n < NBH:
                        b, h = divmod(n, NH1)
                        wait(pe, "expo", 2 * (n - 2))
                        s = bank[n % 3]
                        pr = slice(32 * (h % 4), 32 * (h % 4) + 32)
                        for c in range(NC):
                            lo, w = (0, P) if c == 0 else (P, 2 * P)
                            for j, ks in enumerate((khl, klh)):
                                nc.tensor.matmul(s[:, lo:lo + w], qhl[pr, h // 4, b * T + c * P:b * T + (c + 1) * P],
                                                 ks[pr, h // 4, b * T:b * T + w], start=(j == 0), stop=False)
                            last = nc.tensor.matmul(s[:, lo + w - P:lo + w], eyeb[:], cmask[:], start=False, stop=True)
                        last.then_inc(sem("s_mm"), 1)
                    m = n - LAG_T
                    if 0 <= m < NBH:
                        pe.wait_ge(sem("prob0"), m + 1)
                        pe.wait_ge(sem("prob1"), m + 1)
                        wait(pe, "pt", m - 1)
                        for j in range(3):
                            last = nc.tensor.transpose(bank[3 + m % 2][:, j * P:(j + 1) * P], prob[:, m % NBUF, j * P:(j + 1) * P], ident)
                        last.then_inc(sem("pt_mm"), 1)
                    m = n - LAG_PV
                    if 0 <= m < NBH:
                        b, h = divmod(m, NH1)
                        pe.wait_ge(sem("pt"), m + 1)
                        if h % 8 == 0:
                            wait(pe, "atT", 2 * b + h // 8 - 1)
                        pr = slice(32 * (h % 4), 32 * (h % 4) + 32)
                        o = bank[5 + h // 8][pr, (h // 4 % 2) * T:(h // 4 % 2 + 1) * T]
                        nc.tensor.matmul(o, v1[:, NC * b, h, :], probT[:, m % NBUF, 0:T], start=True, stop=False)
                        nc.tensor.matmul(o[:, P:T], v1[:, NC * b + 1, h, :], probT[:, m % NBUF, T:T + P], start=False, stop=True)\
                            .then_inc(sem("pv"), 1)
                    if n >= LAG_O and (n - LAG_O) % NH1 == NH1 - 1:
                        project((n - LAG_O) // NH1)
                project(B - 1)

        with ExitStack() as s4:
            fac = sb("fac", [P, RANK, KC, D], ctx=s4)
            fsum = sb("fsum", [P, KC, D], ctx=s4)
            biasb = sb("biasb", [P, D], ctx=s4)
            rt = sb("rt4", [P, NC, D], ctx=s4)
            block = s4.enter_context(nc.Block())

            @block.sync
            def _(sp):
                sp.dma_start(fac[:], fac_d.rearrange("r (k p) e -> p r k e", p=P)).then_inc(sem("fac_in"), 16)
                sp.dma_start(biasb[:], bias_d.rearrange("(o e) -> o e", o=1).broadcast_to([P, D])).then_inc(sem("fac_in"), 16)
                for b in range(B):
                    sp.wait_ge(sem("res1b"), b + 1)
                    sp.dma_start(out_d[b].rearrange("(c p) d -> p c d", p=P), x[:, NC * b:NC * (b + 1), :]).then_inc(sem("out"), 16)
                sp.wait_ge(sem("out"), 16 * B)

            @block.gpsimd
            def _(pool):
                ln_pool(pool, 3)

            @block.scalar
            def _(act):
                ln_scalar(act, 3, 1, 3, 4)

            @block.vector
            def _(dve):
                ln_vector(dve, 3, lambda t: None)
                ch = Chain(dve, "fac_chain")
                dve.wait_ge(sem("fac_in"), 32)
                ch.after(nc.vector.tensor_tensor(fsum[:], fac[:, 0], fac[:, 1], ALU.add))
                for r in range(2, RANK):
                    i = nc.vector.tensor_tensor(fsum[:], fsum[:], fac[:, r], ALU.add)
                    if r < RANK - 1:
                        ch.after(i)
                i.then_inc(sem("fsum"), 1)
                for b in range(B):
                    dve.wait_ge(sem("fac_mm"), b + 1)
                    wait(dve, "res1b", b)
                    ch.after(nc.vector.scalar_tensor_tensor(rt[:], bank[2 + b % 2][:].rearrange("p (c d) -> p c d", c=NC), float(RANK) ** -0.5,
                                                            biasb[:].unsqueeze(1).broadcast_to([P, NC, D]), ALU.mult, ALU.add))
                    residual(ch, rt[:], b, rt[:], 1, 1, "res1b")

            @block.tensor
            def _(pe):
                ln_tensor(pe, 3)
                pe.wait_ge(sem("ln_hT"), 4 * KC * B)
                pe.wait_ge(sem("fsum"), 1)
                for b in range(B):
                    wait(pe, "res1b", b - 1)
                    for c in range(NC):
                        t = NC * b + c
                        for k in range(KC):
                            last = nc.tensor.matmul(bank[2 + b % 2][:, c * D:(c + 1) * D], hT[:, k, t * P:(t + 1) * P], fsum[:, k, :],
                                                    start=(k == 0), stop=(k == KC - 1))
                    last.then_inc(sem("fac_mm"), 1)


_INS = ['L0_attn_hidden_states', 'L0_attn_W_qkvz', 'L0_attn_W_ba', 'L0_attn_conv_w', 'L0_attn_dt_bias', 'L0_attn_A_log',
        'L0_attn_norm_weight', 'L0_attn_W_out', 'L0_ffn_wq_gate', 'L0_ffn_s_gate', 'L0_ffn_wq_up', 'L0_ffn_s_up',
        'L0_ffn_wq_down', 'L0_ffn_s_down', 'L0_c', 'L0_wmod', 'L1_attn_wq', 'L1_attn_wk', 'L1_attn_wv', 'L1_attn_wo',
        'L1_ffn_factors', 'L1_ffn_bias', 'L1_c', 'L1_wmod']


def kernel(**inputs):
    import concourse.bacc as _bacc
    from concourse.bass_utils import run_bass_kernel_spmd as _run

    nc = _bacc.Bacc("TRN2", target_bir_lowering=False, num_devices=1)
    arrays, args = {}, []
    for name in _INS:
        a = np.ascontiguousarray(inputs[name])
        arrays[f"in_{name}"] = a
        args.append(nc.dram_tensor(f"in_{name}", a.shape, mybir.dt.from_np(a.dtype), kind="ExternalInput").ap())
    args.append(nc.dram_tensor("out_x", (B, T, D), F32, kind="ExternalOutput").ap())
    build(nc, *args)
    r = _run(nc, [arrays], core_ids=[0])
    return r.results[0]["out_x"]
```
